# Optimizing a Trainium2 kernel written in Bass

```python
import numpy as np
import jax
import jax.numpy as jnp

def _softmax(x, axis=-1):
    return jax.nn.softmax(x, axis=axis)

def _gelu(x):
    return jax.nn.gelu(x, approximate=True)

def _silu(x):
    return jax.nn.silu(x)

def _sigmoid(x):
    return jax.nn.sigmoid(x)

def _layernorm(x, axis=-1, eps=1e-05):
    m = jnp.mean(x, axis=axis, keepdims=True)
    v = jnp.var(x, axis=axis, keepdims=True)
    return (x - m) / jnp.sqrt(v + eps)

def _scatter_add(tgt, idx, src, axis=0):
    return tgt.at[idx].add(src)

def _segment_sum(src, seg, n):
    return jax.ops.segment_sum(src, seg, n)
kernel_name = 'mk_metaformer_d2_conv_nhwc128_r2_41f5a6'

def setup_inputs(seed: int=0):
    np.random.seed(seed)
    _w = jnp.asarray

    def _rec_inputs():
        import jax
        import jax.numpy as jnp
        _gk = jax.random.key(seed)
        x = -0.000125 + 0.9999 * jax.random.normal(jax.random.fold_in(_gk, 1), (1, 256, 256, 64), jnp.float32)
        return x
    x = _rec_inputs()

    def _L0_conv_setup():
        import jax, jax.numpy as jnp
        import numpy as np
        EPS = 1e-05

        def _layer_norm(x, w, b):
            mu = jnp.mean(x, axis=-1, keepdims=True)
            var = jnp.var(x, axis=-1, keepdims=True)
            return (x - mu) * jax.lax.rsqrt(var + EPS) * w + b
        key = jax.random.key(seed)
        ks = jax.random.split(key, 8)
        B, N, CZ, CH = (1, 256, 64, 64)
        s = 0.02
        return {'z': jax.random.normal(ks[0], (B, N, N, CZ), dtype=jnp.float32), 'mask': jnp.ones((B, N, N), dtype=jnp.float32), 'ln_in_w': jnp.ones((CZ,), jnp.float32), 'ln_in_b': jnp.zeros((CZ,), jnp.float32), 'w_ap': jax.random.normal(ks[1], (CZ, CH), jnp.float32) * s, 'b_ap': jnp.zeros((CH,), jnp.float32), 'w_ag': jax.random.normal(ks[2], (CZ, CH), jnp.float32) * s, 'b_ag': jnp.ones((CH,), jnp.float32), 'w_bp': jax.random.normal(ks[3], (CZ, CH), jnp.float32) * s, 'b_bp': jnp.zeros((CH,), jnp.float32), 'w_bg': jax.random.normal(ks[4], (CZ, CH), jnp.float32) * s, 'b_bg': jnp.ones((CH,), jnp.float32), 'ln_out_w': jnp.ones((CH,), jnp.float32), 'ln_out_b': jnp.zeros((CH,), jnp.float32), 'w_z': jax.random.normal(ks[5], (CH, CZ), jnp.float32) * s, 'b_z': jnp.zeros((CZ,), jnp.float32), 'w_g': jax.random.normal(ks[6], (CZ, CZ), jnp.float32) * s, 'b_g': jnp.ones((CZ,), jnp.float32)}
    _L0_conv_all = _L0_conv_setup()
    _L0_conv_in = {k: v for k, v in _L0_conv_all.items() if k in ('mask', 'ln_in_w', 'ln_in_b', 'w_ap', 'b_ap', 'w_ag', 'b_ag', 'w_bp', 'b_bp', 'w_bg', 'b_bg', 'ln_out_w', 'ln_out_b', 'w_z', 'b_z', 'w_g', 'b_g')}
    del _L0_conv_all

    def _L0_ffn_setup():
        import jax, jax.numpy as jnp
        import numpy as np
        BN_EPS = 1e-05
        key = jax.random.key(seed)
        k1, k2, k3 = jax.random.split(key, 3)
        B, T, I, H = (32, 1024, 64, 64)
        x = jax.random.normal(k1, (B, T, I), dtype=jnp.float32)
        W = jax.random.normal(k2, (H, I), dtype=jnp.float32) * (1.0 / np.sqrt(I))
        V = jnp.linalg.qr(jax.random.normal(k3, (H, H), dtype=jnp.float32))[0]
        gamma = jnp.ones((H,), dtype=jnp.float32)
        beta = jnp.zeros((H,), dtype=jnp.float32)
        return {'x': x, 'W': W, 'V': V, 'gamma': gamma, 'beta': beta}
    _L0_ffn_all = _L0_ffn_setup()
    _L0_ffn_in = {k: v for k, v in _L0_ffn_all.items() if k in ('W', 'V', 'gamma', 'beta')}
    del _L0_ffn_all

    def _L1_conv_setup():
        import jax, jax.numpy as jnp
        import numpy as np
        C_Z = 64
        C_HIDDEN = 64
        EPS = 1e-05

        def _layer_norm(x, w, b):
            mu = jnp.mean(x, axis=-1, keepdims=True)
            var = jnp.var(x, axis=-1, keepdims=True)
            return (x - mu) * jax.lax.rsqrt(var + EPS) * w + b
        key = jax.random.key(seed)
        ks = jax.random.split(key, 8)
        B, N = (1, 256)
        z = jax.random.normal(ks[0], (B, N, N, C_Z), dtype=jnp.float32)
        mask = jnp.ones((B, N, N), dtype=jnp.float32)
        s = 0.02
        params = {'w_ap': jax.random.normal(ks[1], (C_Z, C_HIDDEN), jnp.float32) * s, 'b_ap': jnp.zeros((C_HIDDEN,), jnp.float32), 'w_ag': jax.random.normal(ks[2], (C_Z, C_HIDDEN), jnp.float32) * s, 'b_ag': jnp.ones((C_HIDDEN,), jnp.float32), 'w_bp': jax.random.normal(ks[3], (C_Z, C_HIDDEN), jnp.float32) * s, 'b_bp': jnp.zeros((C_HIDDEN,), jnp.float32), 'w_bg': jax.random.normal(ks[4], (C_Z, C_HIDDEN), jnp.float32) * s, 'b_bg': jnp.ones((C_HIDDEN,), jnp.float32), 'w_g': jax.random.normal(ks[5], (C_Z, C_Z), jnp.float32) * s, 'b_g': jnp.ones((C_Z,), jnp.float32), 'w_z': jax.random.normal(ks[6], (C_HIDDEN, C_Z), jnp.float32) * s, 'b_z': jnp.zeros((C_Z,), jnp.float32), 'ln_in_w': jnp.ones((C_Z,), jnp.float32), 'ln_in_b': jnp.zeros((C_Z,), jnp.float32), 'ln_out_w': jnp.ones((C_HIDDEN,), jnp.float32), 'ln_out_b': jnp.zeros((C_HIDDEN,), jnp.float32)}
        return {'z': z, 'mask': mask, **params}
    _L1_conv_all = _L1_conv_setup()
    _L1_conv_in = {k: v for k, v in _L1_conv_all.items() if k in ('mask', 'w_ap', 'b_ap', 'w_ag', 'b_ag', 'w_bp', 'b_bp', 'w_bg', 'b_bg', 'w_g', 'b_g', 'w_z', 'b_z', 'ln_in_w', 'ln_in_b', 'ln_out_w', 'ln_out_b')}
    del _L1_conv_all

    def _L1_ffn_setup():
        import jax, jax.numpy as jnp
        import numpy as np
        B, N, D, C, E, K = (8, 4096, 64, 64, 8, 2)
        key = jax.random.key(seed)
        k0, k1, k2 = jax.random.split(key, 3)
        x = jax.random.normal(k0, (B, N, D), dtype=jnp.float32)
        router_w = jax.random.normal(k1, (D, E), dtype=jnp.float32) * 0.05
        router_b = jnp.zeros((E,), dtype=jnp.float32)
        expert_w = jax.random.normal(k2, (E, D, C), dtype=jnp.float32) * (1.0 / np.sqrt(D))
        expert_b = jnp.zeros((E, C), dtype=jnp.float32)
        return {'x': x, 'router_w': router_w, 'router_b': router_b, 'expert_w': expert_w, 'expert_b': expert_b}
    _L1_ffn_all = _L1_ffn_setup()
    _L1_ffn_in = {k: v for k, v in _L1_ffn_all.items() if k in ('router_w', 'router_b', 'expert_w', 'expert_b')}
    del _L1_ffn_all
    return {'x': x, 'L0_conv_mask': _L0_conv_in['mask'], 'L0_conv_ln_in_w': _L0_conv_in['ln_in_w'], 'L0_conv_ln_in_b': _L0_conv_in['ln_in_b'], 'L0_conv_w_ap': _L0_conv_in['w_ap'], 'L0_conv_b_ap': _L0_conv_in['b_ap'], 'L0_conv_w_ag': _L0_conv_in['w_ag'], 'L0_conv_b_ag': _L0_conv_in['b_ag'], 'L0_conv_w_bp': _L0_conv_in['w_bp'], 'L0_conv_b_bp': _L0_conv_in['b_bp'], 'L0_conv_w_bg': _L0_conv_in['w_bg'], 'L0_conv_b_bg': _L0_conv_in['b_bg'], 'L0_conv_ln_out_w': _L0_conv_in['ln_out_w'], 'L0_conv_ln_out_b': _L0_conv_in['ln_out_b'], 'L0_conv_w_z': _L0_conv_in['w_z'], 'L0_conv_b_z': _L0_conv_in['b_z'], 'L0_conv_w_g': _L0_conv_in['w_g'], 'L0_conv_b_g': _L0_conv_in['b_g'], 'L0_ffn_W': _L0_ffn_in['W'], 'L0_ffn_V': _L0_ffn_in['V'], 'L0_ffn_gamma': _L0_ffn_in['gamma'], 'L0_ffn_beta': _L0_ffn_in['beta'], 'L1_conv_mask': _L1_conv_in['mask'], 'L1_conv_w_ap': _L1_conv_in['w_ap'], 'L1_conv_b_ap': _L1_conv_in['b_ap'], 'L1_conv_w_ag': _L1_conv_in['w_ag'], 'L1_conv_b_ag': _L1_conv_in['b_ag'], 'L1_conv_w_bp': _L1_conv_in['w_bp'], 'L1_conv_b_bp': _L1_conv_in['b_bp'], 'L1_conv_w_bg': _L1_conv_in['w_bg'], 'L1_conv_b_bg': _L1_conv_in['b_bg'], 'L1_conv_w_g': _L1_conv_in['w_g'], 'L1_conv_b_g': _L1_conv_in['b_g'], 'L1_conv_w_z': _L1_conv_in['w_z'], 'L1_conv_b_z': _L1_conv_in['b_z'], 'L1_conv_ln_in_w': _L1_conv_in['ln_in_w'], 'L1_conv_ln_in_b': _L1_conv_in['ln_in_b'], 'L1_conv_ln_out_w': _L1_conv_in['ln_out_w'], 'L1_conv_ln_out_b': _L1_conv_in['ln_out_b'], 'L1_ffn_router_w': _L1_ffn_in['router_w'], 'L1_ffn_router_b': _L1_ffn_in['router_b'], 'L1_ffn_expert_w': _L1_ffn_in['expert_w'], 'L1_ffn_expert_b': _L1_ffn_in['expert_b']}

def reference(x, L0_conv_mask, L0_conv_ln_in_w, L0_conv_ln_in_b, L0_conv_w_ap, L0_conv_b_ap, L0_conv_w_ag, L0_conv_b_ag, L0_conv_w_bp, L0_conv_b_bp, L0_conv_w_bg, L0_conv_b_bg, L0_conv_ln_out_w, L0_conv_ln_out_b, L0_conv_w_z, L0_conv_b_z, L0_conv_w_g, L0_conv_b_g, L0_ffn_W, L0_ffn_V, L0_ffn_gamma, L0_ffn_beta, L1_conv_mask, L1_conv_w_ap, L1_conv_b_ap, L1_conv_w_ag, L1_conv_b_ag, L1_conv_w_bp, L1_conv_b_bp, L1_conv_w_bg, L1_conv_b_bg, L1_conv_w_g, L1_conv_b_g, L1_conv_w_z, L1_conv_b_z, L1_conv_ln_in_w, L1_conv_ln_in_b, L1_conv_ln_out_w, L1_conv_ln_out_b, L1_ffn_router_w, L1_ffn_router_b, L1_ffn_expert_w, L1_ffn_expert_b):
    import jax
    import jax.numpy as jnp

    def _L0_conv_ref(z, mask, ln_in_w, ln_in_b, w_ap, b_ap, w_ag, b_ag, w_bp, b_bp, w_bg, b_bg, ln_out_w, ln_out_b, w_z, b_z, w_g, b_g):
        import jax, jax.numpy as jnp
        import numpy as np
        EPS = 1e-05

        def _layer_norm(x, w, b):
            mu = jnp.mean(x, axis=-1, keepdims=True)
            var = jnp.var(x, axis=-1, keepdims=True)
            return (x - mu) * jax.lax.rsqrt(var + EPS) * w + b
        m = mask[..., None]
        zn = _layer_norm(z, ln_in_w, ln_in_b)
        a = m * jax.nn.sigmoid(zn @ w_ag + b_ag) * (zn @ w_ap + b_ap)
        b = m * jax.nn.sigmoid(zn @ w_bg + b_bg) * (zn @ w_bp + b_bp)
        p = jnp.einsum('bikc,bjkc->bijc', a, b)
        x = _layer_norm(p, ln_out_w, ln_out_b) @ w_z + b_z
        g = jax.nn.sigmoid(zn @ w_g + b_g)
        return x * g

    def _L0_ffn_ref(x, W, V, gamma, beta):
        import jax, jax.numpy as jnp
        import numpy as np
        BN_EPS = 1e-05
        B, T, H = (x.shape[0], x.shape[1], W.shape[0])
        Wx = jnp.einsum('bti,hi->bth', x, W)
        flat = Wx.reshape(B * T, H)
        mean = jnp.mean(flat, axis=0)
        var = jnp.var(flat, axis=0)
        Wx = ((flat - mean) * jax.lax.rsqrt(var + BN_EPS) * gamma + beta).reshape(B, T, H)
        Vt = V.T

        def step(yt, wx_t):
            yt = jax.nn.sigmoid(wx_t + yt @ Vt)
            return (yt, yt)
        y0 = jnp.zeros((B, H), dtype=Wx.dtype)
        _, ys = jax.lax.scan(step, y0, jnp.swapaxes(Wx, 0, 1))
        return jnp.swapaxes(ys, 0, 1)

    def _L1_conv_ref(z, mask, w_ap, b_ap, w_ag, b_ag, w_bp, b_bp, w_bg, b_bg, w_g, b_g, w_z, b_z, ln_in_w, ln_in_b, ln_out_w, ln_out_b):
        import jax, jax.numpy as jnp
        import numpy as np
        C_Z = 64
        C_HIDDEN = 64
        EPS = 1e-05

        def _layer_norm(x, w, b):
            mu = jnp.mean(x, axis=-1, keepdims=True)
            var = jnp.var(x, axis=-1, keepdims=True)
            return (x - mu) * jax.lax.rsqrt(var + EPS) * w + b
        m = mask[..., None]
        zn = _layer_norm(z, ln_in_w, ln_in_b)
        a = (zn @ w_ap + b_ap) * jax.nn.sigmoid(zn @ w_ag + b_ag) * m
        b = (zn @ w_bp + b_bp) * jax.nn.sigmoid(zn @ w_bg + b_bg) * m
        x = jnp.einsum('bikc,bjkc->bijc', a, b)
        x = _layer_norm(x, ln_out_w, ln_out_b) @ w_z + b_z
        g = jax.nn.sigmoid(zn @ w_g + b_g)
        return x * g

    def _L1_ffn_ref(x, router_w, router_b, expert_w, expert_b):
        import jax, jax.numpy as jnp
        import numpy as np
        B, N, D, C, E, K = (8, 4096, 64, 64, 8, 2)
        router_probs = jax.nn.softmax(x @ router_w + router_b, axis=-1)
        top_p, top_i = jax.lax.top_k(router_probs, K)
        top_p = top_p / jnp.sum(top_p, axis=-1, keepdims=True)
        expert_out = jnp.einsum('bnd,edc->bnec', x, expert_w) + expert_b
        gathered = jnp.take_along_axis(expert_out, top_i[..., None], axis=2)
        return jnp.einsum('bnk,bnkc->bnc', top_p, gathered)

    def _gn(v, G=32, eps=1e-05):
        B_, H_, W_, C_ = v.shape
        g = v.reshape(B_, H_, W_, G, C_ // G)
        m = jnp.mean(g, axis=(1, 2, 4), keepdims=True)
        s = jnp.var(g, axis=(1, 2, 4), keepdims=True)
        return ((g - m) / jnp.sqrt(s + eps)).reshape(v.shape)

    def _ln_c(v, eps=1e-06):
        m = jnp.mean(v, axis=-1, keepdims=True)
        s = jnp.var(v, axis=-1, keepdims=True)
        return (v - m) / jnp.sqrt(s + eps)

    def _ln_t(v, eps=1e-05):
        m = jnp.mean(v, axis=-1, keepdims=True)
        s = jnp.var(v, axis=-1, keepdims=True)
        return (v - m) / jnp.sqrt(s + eps)

    def _to_tokens(v):
        B_, H_, W_, C_ = v.shape
        return v.reshape(B_, H_ * W_, C_)

    def _from_tokens(t, like):
        return t.reshape(like.shape)
    x = x + _L0_conv_ref(_ln_c(x), L0_conv_mask, L0_conv_ln_in_w, L0_conv_ln_in_b, L0_conv_w_ap, L0_conv_b_ap, L0_conv_w_ag, L0_conv_b_ag, L0_conv_w_bp, L0_conv_b_bp, L0_conv_w_bg, L0_conv_b_bg, L0_conv_ln_out_w, L0_conv_ln_out_b, L0_conv_w_z, L0_conv_b_z, L0_conv_w_g, L0_conv_b_g)
    t = _to_tokens(x)
    t = t + _L0_ffn_ref(_ln_t(t), L0_ffn_W, L0_ffn_V, L0_ffn_gamma, L0_ffn_beta)
    x = _from_tokens(t, x)
    x = x + _L1_conv_ref(_ln_c(x), L1_conv_mask, L1_conv_w_ap, L1_conv_b_ap, L1_conv_w_ag, L1_conv_b_ag, L1_conv_w_bp, L1_conv_b_bp, L1_conv_w_bg, L1_conv_b_bg, L1_conv_w_g, L1_conv_b_g, L1_conv_w_z, L1_conv_b_z, L1_conv_ln_in_w, L1_conv_ln_in_b, L1_conv_ln_out_w, L1_conv_ln_out_b)
    t = _to_tokens(x)
    t = t + _L1_ffn_ref(_ln_t(t), L1_ffn_router_w, L1_ffn_router_b, L1_ffn_expert_w, L1_ffn_expert_b)
    x = _from_tokens(t, x)
    return x

_drawn_inputs = setup_inputs


def setup_inputs(seed=0):
    import zlib

    import numpy as np

    out = dict(_drawn_inputs(seed))
    spreads = {'L0_conv_ln_in_w': (1.0, 0.2),
     'L0_conv_ln_in_b': (0.0, 0.1),
     'L0_conv_b_ap': (0.0, 0.1),
     'L0_conv_b_ag': (1.0, 0.552),
     'L0_conv_b_bp': (0.0, 0.1),
     'L0_conv_b_bg': (1.0, 0.2),
     'L0_conv_ln_out_w': (1.0, 0.2),
     'L0_conv_ln_out_b': (0.0, 0.1),
     'L0_conv_b_z': (0.0, 0.1),
     'L0_conv_b_g': (1.0, 0.2),
     'L0_ffn_gamma': (1.0, 0.2),
     'L0_ffn_beta': (0.0, 0.1),
     'L1_conv_b_ap': (0.0, 0.1),
     'L1_conv_b_ag': (1.0, 0.2),
     'L1_conv_b_bp': (0.0, 0.1),
     'L1_conv_b_bg': (1.0, 0.2),
     'L1_conv_b_g': (1.0, 0.2),
     'L1_conv_b_z': (0.0, 0.1),
     'L1_conv_ln_in_w': (1.0, 0.2),
     'L1_conv_ln_in_b': (0.0, 0.1),
     'L1_conv_ln_out_w': (1.0, 0.2),
     'L1_conv_ln_out_b': (0.0, 0.1),
     'L1_ffn_router_b': (0.0, 0.1),
     'L1_ffn_expert_b': (0.0, 0.1)}
    factors = {'L0_conv_w_ag': 3.58, 'L0_conv_w_bg': 3.909, 'L1_conv_w_ag': 2.987, 'L1_conv_w_bg': 3.285}
    for name, (base, spread) in spreads.items():
        noise = np.random.default_rng([zlib.crc32(name.encode()), seed]).standard_normal(out[name].shape)
        drawn = base * np.exp(spread * noise) if base else spread * noise
        out[name] = jnp.asarray(drawn.astype(out[name].dtype))
    for name, factor in factors.items():
        out[name] = (out[name] * factor).astype(out[name].dtype)
    return out
```

```python
from contextlib import ExitStack

import numpy as np
import concourse.bass as bass
from concourse import mybir

F32 = mybir.dt.float32
BF16 = mybir.dt.bfloat16
I32 = mybir.dt.int32
ALU = mybir.AluOpType
ACT = mybir.ActivationFunctionType
AX = mybir.AxisListType

P = 128
N = 256
C = 64
H = 2
R = 4
G = N // R
BLK = 32
NB = N // BLK
RB = NB // H
CH = 2
E = 8


class Scope(ExitStack):

    def __init__(self, nc, tag):
        super().__init__()
        self.nc, self.tag, self.sems = nc, tag, []

    def sb(self, name, shape, dt=F32):
        return self.enter_context(self.nc.sbuf_tensor(f"{self.tag}_{name}", shape, dt))

    def ps(self, name, shape=(P, 512), dt=F32):
        return self.enter_context(self.nc.psum_tensor(f"{self.tag}_{name}", list(shape), dt))

    def sem(self, name):
        self.sems.append(self.nc.alloc_semaphore(f"{self.tag}_{name}"))
        return self.sems[-1]

    def __exit__(self, *raised):
        if self.sems and raised[0] is None:
            self.nc.clear_and_free_semaphores(self.sems)
            self.nc.all_engine_barrier()
        return super().__exit__(*raised)


def over(ap, n):
    return ap.unsqueeze(len(ap.shape)).to_broadcast(list(ap.shape) + [n])


def constants(nc, ident, ones3, numbers):
    with Scope(nc, "cst") as m:
        made, rows_made = m.sem("made"), m.sem("rows_made")
        with nc.Block() as block:

            @block.vector
            def _(dve):
                dve.memset(ones3[:], 0.0).then_inc(rows_made, 1)
                dve.wait_ge(rows_made, 1)
                for q in range(3):
                    dve.memset(ones3[32 * q:32 * q + 1, :], 1.0).then_inc(rows_made, 1)

            @block.gpsimd
            def _(pool):
                pool.memset(ident[:], 0.0).then_inc(made, 1)
                for q, number in enumerate(NUMBERS):
                    pool.memset(numbers[:, q:q + 1], number).then_inc(made, 1)
                pool.wait_ge(made, 1 + len(NUMBERS))
                pool.affine_select(out=ident[:], in_=ident[:], compare_op=ALU.not_equal, fill=1.0, base=0,
                                   pattern=[[-1, P]], channel_multiplier=1).then_inc(made, 1)
                pool.wait_ge(made, 2 + len(NUMBERS))



def prepare_weights(nc, tag, weight, bias3, blocks, gain, offset):
    width = len(blocks) * H * C
    with Scope(nc, tag) as m:
        gain_col = m.sb("gain_col", [P, 1])
        offset_col = m.sb("offset_col", [P, 1])
        offset_rows = m.sb("offset_rows", [P, P])
        bias_rows = m.sb("bias_rows", [P, width])
        part = [m.sb(f"part{q}", [P, width], BF16) for q in range(3)]
        folded = [m.ps(f"folded{q}") for q in range(2)]
        zeroed, loaded, rows, summed, step = (m.sem(n) for n in ("zeroed", "loaded", "rows", "summed", "step"))
        n_loads = len(blocks) * H * 4 + 2 * H
        cuts = [(at, min(at + 512, width)) for at in range(0, width, 512)]
        with nc.Block() as block:

            @block.sync
            def _(sp):
                sp.wait_ge(zeroed, 3)
                for k, (matrix, bias) in enumerate(blocks):
                    for h in range(H):
                        at = (k * H + h) * C
                        sp.dma_start(weight[h * C:(h + 1) * C, at:at + C], matrix).then_inc(loaded, 16)
                        for q in range(3):
                            sp.dma_start(bias_rows[32 * q:32 * q + 1, at:at + C],
                                         bias.unsqueeze(0)).then_inc(loaded, 16)
                for h in range(H):
                    sp.dma_start(gain_col[h * C:(h + 1) * C, :], gain.unsqueeze(1)).then_inc(loaded, 16)
                    sp.dma_start(offset_col[h * C:(h + 1) * C, :], offset.unsqueeze(1)).then_inc(loaded, 16)

            @block.tensor
            def _(pe):
                pe.wait_ge(rows, 1)
                for q, (a, b) in enumerate(cuts):
                    pe.matmul(folded[q][:, 0:b - a], offset_rows[:], weight[:, a:b],
                              start=True, stop=True).then_inc(summed, 1)

            @block.vector
            def _(dve):
                dve.memset(weight[:], 0.0).then_inc(zeroed, 1)
                dve.memset(bias_rows[:], 0.0).then_inc(zeroed, 1)
                dve.memset(offset_rows[:], 0.0).then_inc(zeroed, 1)
                dve.memset(bias3[:], 0.0).then_inc(step, 1)
                dve.wait_ge(loaded, 16 * n_loads)
                dve.wait_ge(zeroed, 3)
                for q in range(3):
                    ins = dve.tensor_copy(offset_rows[:, 32 * q:32 * q + 1], offset_col[:])
                ins.then_inc(rows, 1)
                dve.wait_ge(summed, len(cuts))
                for q, (a, b) in enumerate(cuts):
                    ins = dve.tensor_tensor(bias_rows[:, a:b], bias_rows[:, a:b], folded[q][:, 0:b - a], ALU.add)
                ins.then_inc(step, 1)
                dve.tensor_scalar(weight[:], weight[:], gain_col[:], None, ALU.mult).then_inc(step, 1)
                at = 3
                dve.wait_ge(step, at)
                for q in range(3):
                    dve.tensor_copy(part[q][:], bias_rows[:]).then_inc(step, 1)
                    at += 1
                    dve.wait_ge(step, at)
                    if q < 2:
                        dve.tensor_tensor(bias_rows[:], bias_rows[:], part[q][:], ALU.subtract).then_inc(step, 1)
                        at += 1
                        dve.wait_ge(step, at)
                cols = bias3.shape[1]
                for q in range(3):
                    ins = dve.tensor_copy(bias3[32 * q:32 * q + 32, :], part[q][32 * q:32 * q + 32, 0:cols])
                ins.then_inc(step, 1)


STAT_STEPS = 9
NUMBERS = [-0.5, 0.5, 4.0, 1.0 / C, 1e-5, (1.0 + 1e-5) / C, 1e-11]
POWER, HALF, FOUR, PLAIN, DOUBLE = 0, 1, 2, 3, 5


def statistics(pool, chain, base, stats, mean, rstd, tmp, numbers, kind, done):
    k = mean.shape[1]
    even_mean, even_m2 = stats[:, :, 1], stats[:, :, 2]
    odd_mean, odd_m2 = stats[:, :, 4], stats[:, :, 5]
    d, q, s = tmp[:, 0, 0:k], tmp[:, 1, 0:k], tmp[:, 2, 0:k]

    def number(column):
        return numbers[:, column:column + 1].to_broadcast([P, k])

    pool.tensor_tensor(d, even_mean, odd_mean, ALU.subtract).then_inc(chain, 1)
    pool.tensor_tensor(q, even_m2, odd_m2, ALU.add).then_inc(chain, 1)
    pool.tensor_tensor(s, even_mean, odd_mean, ALU.add).then_inc(chain, 1)
    pool.wait_ge(chain, base + 3)
    pool.tensor_tensor(d, d, number(FOUR), ALU.mult).then_inc(chain, 1)
    pool.tensor_tensor(mean, s, number(HALF), ALU.mult)
    pool.wait_ge(chain, base + 4)
    pool.tensor_tensor(d, d, d, ALU.mult).then_inc(chain, 1)
    pool.wait_ge(chain, base + 5)
    pool.tensor_tensor(q, q, d, ALU.add).then_inc(chain, 1)
    pool.wait_ge(chain, base + 6)
    pool.tensor_tensor(q, q, number(kind), ALU.mult).then_inc(chain, 1)
    pool.wait_ge(chain, base + 7)
    pool.tensor_tensor(q, q, number(kind + 1), ALU.add).then_inc(chain, 1)
    pool.wait_ge(chain, base + 8)
    pool.tensor_tensor(rstd, q, number(POWER), ALU.pow).then_inc(chain, 1)
    pool.wait_ge(chain, base + 9)
    pool.sem_inc(done, 1)


def conv_project(nc, tag, x, mask, w, a_res, b_dram, gate_dram, ident, ones3, numbers):
    W_COLS = 10 * C
    with Scope(nc, tag) as m:
        weight = m.sb("weight", [P, W_COLS])
        bias3 = m.sb("bias3", [P, W_COLS], BF16)
        prepare_weights(nc, tag + "p", weight, bias3,
                        [(w["w_ag"], w["b_ag"]), (w["w_bg"], w["b_bg"]), (w["w_ap"], w["b_ap"]),
                         (w["w_bp"], w["b_bp"]), (w["w_g"], w["b_g"])], w["ln_in_w"], w["ln_in_b"])

        mask_sb = m.sb("mask", [P, H, N])
        b_stage = m.sb("b_stage", [P, 2, H, C // CH, BLK, CH])
        xs = [m.sb(f"x{q}", [P, H, R, C]) for q in range(2)]
        xn = [m.sb(f"xn{q}", [P, R, H, C]) for q in range(2)]
        zt = [m.sb(f"zt{q}", [P, R * P]) for q in range(2)]
        sig = m.sb("sig", [P, R, 4 * C])
        prod = m.sb("prod", [P, R, 2, H, C])
        gs = [m.sb(f"gs{q}", [P, H, R, C]) for q in range(2)]
        stats = [m.sb(f"stats{q}", [P, H * R, 6]) for q in range(2)]
        mean = [m.sb(f"mean{q}", [P, H * R]) for q in range(2)]
        rstd = [m.sb(f"rstd{q}", [P, H * R]) for q in range(2)]
        tmp = m.sb("tmp", [P, 3, H * R])
        tp = [m.ps(f"tp{q}") for q in range(2)]
        pg = [m.ps(f"pg{q}") for q in range(2)]
        pv = [m.ps(f"pv{i}") for i in range(R)]

        mask_in = m.sem("mask_in")
        x_in = [m.sem(f"x_in{q}") for q in range(2)]
        stats_made, norm_known, chain, xn_made, xt_made, zt_made = (
            m.sem(n) for n in ("stats_made", "norm_known", "chain", "xn_made", "xt_made", "zt_made"))
        v_made, sig_made, prod_made, g_made, gs_made = (
            m.sem(n) for n in ("v_made", "sig_made", "prod_made", "g_made", "gs_made"))
        gs_stored = [m.sem(f"gs_stored{q}") for q in range(2)]
        b_made = m.sem("b_made")
        b_stored = [m.sem(f"b_stored{q}") for q in range(2)]

        def units(eng, unit):
            with eng.Fori(0, G // 2 - 1) as t:
                for q in range(2):
                    unit(t * 2 + q, t, q, True)
            for q in range(2):
                unit(G - 2 + q, G // 2 - 1, q, q == 0)

        with nc.Block() as block:

            @block.sync
            def _(sp):
                sp.dma_start(mask_sb[:], mask).then_inc(mask_in, 16)
                sp.sem_inc(xn_made, 2)
                with sp.Fori(0, G // 2) as t:
                    for q in range(2):
                        n = t * 2 + q
                        sp.wait_ge(xn_made, n + 1)
                        sp.dma_start(xs[q][:], x[:, :, bass.ds(n * R, R), :]).then_inc(x_in[q], 16)

            @block.vector
            def _(dve):
                dve.sem_inc(prod_made, R)
                dve.sem_inc(b_made, 1)

                def measure(half_t, q):
                    dve.wait_ge(x_in[q], 16 * (half_t + 1))
                    for h in range(H):
                        for i in range(R):
                            ins = dve.bn_stats(stats[q][:, h * R + i, :], xs[q][:, h, i, :])
                    ins.then_inc(stats_made, 1)

                def normalise(n, q):
                    dve.wait_ge(norm_known, n + 1)
                    for h in range(H):
                        for i in range(R):
                            k = h * R + i
                            ins = dve.tensor_scalar(xn[q][:, i, h, :], xs[q][:, h, i, :], mean[q][:, k:k + 1],
                                                    rstd[q][:, k:k + 1], ALU.subtract, ALU.mult)
                    ins.then_inc(xn_made, 1)

                def product(u, i):
                    dve.wait_ge(sig_made, u * R + i + 1)
                    dve.tensor_tensor(prod[:, i].rearrange("p a h c -> p (a h c)"), pv[i][:, 4 * C:8 * C],
                                      sig[:, i, :], ALU.mult).then_inc(prod_made, 1)

                measure(0, 0)
                normalise(0, 0)

                def unit(u, t, q, more):
                    if more:
                        measure(t + q, 1 - q)
                    dve.wait_ge(b_made, u + 1)
                    product(u, 0)
                    product(u, 1)
                    if more:
                        normalise(u + 1, 1 - q)
                    product(u, 2)
                    product(u, 3)

                units(dve, unit)

            @block.gpsimd
            def _(pool):
                def know(n, q):
                    pool.wait_ge(stats_made, n + 1)
                    statistics(pool, chain, n * STAT_STEPS, stats[q], mean[q][:], rstd[q][:], tmp, numbers, DOUBLE,
                               norm_known)

                know(0, 0)
                pool.wait_ge(mask_in, 16)

                def unit(u, q, more, buf, row):
                    if more:
                        know(u + 1, 1 - q)
                    pool.wait_ge(prod_made, u * R + 2 * R)
                    by = over(mask_sb[:, :, bass.ds(u * R, R)].rearrange("p h i -> p i h"), C)
                    pool.tensor_tensor(a_res[:, :, :, bass.ds(u * R, R)].rearrange("p h c i -> p i h c"),
                                       prod[:, :, 0], by, ALU.mult)
                    for h in range(H):
                        ins = pool.tensor_tensor(
                            b_stage[:, buf, h, :, bass.ds(row, R), :].rearrange("p n i c -> p i n c"),
                            prod[:, :, 1, h, :].rearrange("p i (n c) -> p i n c", c=CH),
                            over(over(mask_sb[:, h, bass.ds(u * R, R)], C // CH), CH), ALU.mult)
                    ins.then_inc(b_made, 1)
                    pool.wait_ge(b_made, u + 2)

                per = BLK // R // 2

                def one_block(row_half, b2, buf, last):
                    blk = row_half * RB + b2 * 2 + buf
                    if blk >= 2:
                        pool.wait_ge(b_stored[buf], blk // 2 * 16 * H)
                    with pool.Fori(0, per - 1 if last else per) as t:
                        for q in range(2):
                            unit(blk * (BLK // R) + t * 2 + q, q, True, buf, (t * 2 + q) * R)
                    if last:
                        for q in range(2):
                            unit(G - 2 + q, q, q == 0, buf, BLK - 2 * R + q * R)
                    for k in range(H):
                        pool.dma_start(b_dram[row_half, :, :, k, b2 * 2 + buf].rearrange("n p i c -> p n (i c)"),
                                       b_stage[:, buf, k].rearrange("p n i c -> p n (i c)")).then_inc(b_stored[buf], 16)

                for row_half in range(H):
                    for b2 in range(RB // 2):
                        for buf in range(2):
                            one_block(row_half, b2, buf, row_half * RB + b2 * 2 + buf == NB - 1)
                for buf in range(2):
                    pool.wait_ge(b_stored[buf], 16 * H * (NB // 2))

            @block.tensor
            def _(pe):
                def flip(n, q):
                    pe.wait_ge(xn_made, n + 3)
                    for i in range(R):
                        ins = pe.transpose(tp[q][:, i * P:(i + 1) * P],
                                           xn[q][:, i].rearrange("p h c -> p (h c)"), ident[:])
                    ins.then_inc(xt_made, 1)

                def project(u, q, i):
                    tokens = zt[q][:, i * P:(i + 1) * P]
                    if i == 0:
                        pe.wait_ge(zt_made, u + 1)
                        pe.wait_ge(gs_made, u + 1)
                        pe.matmul(pg[q][:], ones3[:], bias3[:, 8 * C:].unsqueeze(1).to_broadcast([P, R, 2 * C]),
                                  start=True, stop=True)
                    pe.wait_ge(prod_made, u * R + i + 1)
                    pe.matmul(pv[i][:], ones3[:], bias3[:, 0:8 * C], start=True, stop=False)
                    pe.matmul(pv[i][:], tokens, weight[:, 0:8 * C], start=False, stop=True).then_inc(v_made, 1)
                    ins = pe.matmul(pg[q][:, i * 2 * C:(i + 1) * 2 * C], tokens, weight[:, 8 * C:],
                                    start=False, stop=True, skip_group_check=True)
                    if i == R - 1:
                        ins.then_inc(g_made, 1)

                flip(0, 0)

                def unit(u, t, q, more):
                    for i in range(R):
                        if i == R - 1 and more:
                            flip(u + 1, 1 - q)
                        project(u, q, i)

                units(pe, unit)

            @block.scalar
            def _(act):
                act.sem_inc(gs_made, 2)
                act.sem_inc(gs_stored[0], 16)
                act.sem_inc(gs_stored[1], 16)

                def take(n, q):
                    act.wait_ge(xt_made, n + 1)
                    act.activation(zt[q][:], tp[q][:], ACT.Copy).then_inc(zt_made, 1)

                take(0, 0)

                def unit(u, t, q, more):
                    for i in range(R):
                        if i == R - 1 and more:
                            take(u + 1, 1 - q)
                        act.wait_ge(v_made, u * R + i + 1)
                        act.activation(sig[:, i, :], pv[i][:, 0:4 * C], ACT.Sigmoid).then_inc(sig_made, 1)
                    act.wait_ge(g_made, u + 1)
                    act.wait_ge(gs_stored[q], (t + 1) * 16)
                    act.activation(gs[q][:].rearrange("p h i c -> p i h c"),
                                   pg[q][:].rearrange("p (i h c) -> p i h c", i=R, h=H),
                                   ACT.Sigmoid).then_inc(gs_made, 1)
                    act.wait_ge(gs_made, u + 3)
                    act.dma_start(gate_dram[:, :, bass.ds(u * R, R), :], gs[q][:]).then_inc(gs_stored[q], 16)

                units(act, unit)
                for q in range(2):
                    act.wait_ge(gs_stored[q], 16 * (G // 2 + 1))


def conv_combine(nc, tag, x, w, a_res, b_dram, gate_dram, out, ident, ones3, numbers):
    TI = P
    TILES = [(h, ih) for h in range(H) for ih in range(N // TI)]
    STEPS = 16
    SR = TI // STEPS
    SC = C // STEPS
    SUBS = SC // CH
    PAIRS = SR // 2
    ROUNDS = len(TILES) + 1
    last_step = len(TILES) * STEPS - 1
    rows = [t.rearrange("p h i c -> p (h i) c") for t in (x, gate_dram, out)]
    with Scope(nc, tag) as m:
        weight = m.sb("weight", [P, H * C])
        bias3 = m.sb("bias3", [P, C], BF16)
        prepare_weights(nc, tag + "p", weight, bias3, [(w["w_z"], w["b_z"])], w["ln_out_w"], w["ln_out_b"])
        ptile = [m.sb(f"p{q}", [P, TI, C]) for q in range(2)]
        bch = [m.sb(f"bch{q}", [P, H, P, CH]) for q in range(SUBS)]
        gs = [m.sb(f"g{q}", [P, SR, C]) for q in range(2)]
        pn = m.sb("pn", [P, SR, C])
        pt = m.sb("pt", [P, PAIRS * P])
        stats = m.sb("stats", [P, SR, 6])
        mean = m.sb("mean", [P, SR])
        rstd = m.sb("rstd", [P, SR])
        tmp = m.sb("tmp", [P, 3, SR])
        psum = [m.ps(f"sum{q}") for q in range(2)]
        tp = [m.ps(f"tp{q}") for q in range(2)]
        po = [m.ps(f"po{q}") for q in range(2)]

        b_in = [m.sem(f"b_in{j}") for j in range(SUBS)]
        chunk_used, p_made = m.sem("chunk_used"), m.sem("p_made")
        x_in = [m.sem(f"x_in{q}") for q in range(2)]
        g_in = [m.sem(f"g_in{q}") for q in range(2)]
        stats_made, chain, norm_known, pn_made, pt_made, pt_copied, o_made, gated, added, stored = (
            m.sem(n) for n in ("stats_made", "chain", "norm_known", "pn_made", "pt_made", "pt_copied", "o_made",
                               "gated", "added", "stored"))

        def rounds(eng, body):
            for r in range(ROUNDS):
                for q in range(2):
                    body(r, 0, q, q == 0)
                with eng.Fori(1, STEPS // 2 - 1) as t:
                    for q in range(2):
                        body(r, t, q, False)
                for q in range(2):
                    body(r, STEPS // 2 - 1, q, False)

        def now(part, r, t, q):
            if r > 0:
                half = t + (r - 1) * (STEPS // 2)
                part(half * 2 + q, half, q, r - 1)

        def behind(part, r, t, q, first):
            if r > 0 and not (r == 1 and first):
                half = t + (r - 1) * (STEPS // 2) - (1 - q)
                part(half * 2 + 1 - q, half, 1 - q, r - 2 if first else r - 1)

        def at_end(part):
            part(last_step, last_step // 2, 1, len(TILES) - 1)

        def slot(n, tile, i=None):
            at = (n - tile * STEPS) * SR
            return bass.ds(at, SR) if i is None else bass.ds(at + i, 1)

        with nc.Block() as block:

            @block.sync
            def _(sp):
                sp.sem_inc(chunk_used, SUBS)

                def body(r, t, q, first):
                    if r < len(TILES):
                        for j in range(SUBS):
                            s = t * 2 + q
                            sp.wait_ge(chunk_used, (s + r * STEPS) * SUBS + j + 1)
                            sp.dma_start(bch[j][:].rearrange("p k j c -> p (k j c)"),
                                         b_dram[TILES[r][0], bass.ds(s * SUBS + j, 1)]
                                         .rearrange("n p k b j c -> p (n k b j c)")).then_inc(b_in[j], 16)

                rounds(sp, body)

            @block.tensor
            def _(pe):
                pe.sem_inc(pt_made, 1)

                def add_up(r, s, q):
                    _, ih = TILES[r]
                    n = s + r * STEPS
                    pe.wait_ge(p_made, n + 1)
                    for j in range(SUBS):
                        pe.wait_ge(b_in[j], (n + 1) * 16)
                        for c in range(CH):
                            at = (j * CH + c) * TI
                            for k in range(H):
                                ins = pe.matmul(psum[q][:, at:at + TI], bch[j][:, k, :, c],
                                                a_res[:, k, bass.ds(s * SC + j * CH + c, 1), ih * TI:(ih + 1) * TI],
                                                start=k == 0, stop=k == H - 1)
                        ins.then_inc(chunk_used, 1)

                def flip(n, half, q, tile):
                    pe.wait_ge(pn_made, n + 1)
                    for j in range(PAIRS):
                        ins = pe.transpose(tp[q][:, j * P:(j + 1) * P],
                                           pn[:, 2 * j:2 * j + 2, :].rearrange("p i c -> p (i c)"), ident[:])
                    ins.then_inc(pt_made, 1)

                def project(n, half, q, tile):
                    pe.wait_ge(pt_copied, n + 1)
                    pe.wait_ge(gated, n + 1)
                    pe.matmul(po[q][:], ones3[:], bias3[:].unsqueeze(1).to_broadcast([P, SR, C]),
                              start=True, stop=True)
                    for j in range(PAIRS):
                        ins = pe.matmul(po[q][:, j * 2 * C:(j + 1) * 2 * C], pt[:, j * P:(j + 1) * P], weight[:],
                                        start=False, stop=True, skip_group_check=True)
                    ins.then_inc(o_made, 1)

                def body(r, t, q, first):
                    if r < len(TILES):
                        add_up(r, t * 2 + q, q)
                    behind(project, r, t, q, first)
                    now(flip, r, t, q)

                rounds(pe, body)
                at_end(project)

            @block.vector
            def _(dve):
                dve.sem_inc(gated, 2)

                def measure(n, half, q, tile):
                    dve.wait_ge(p_made, (tile + 1) * STEPS + 2)
                    for i in range(SR):
                        ins = dve.bn_stats(stats[:, i, :], ptile[tile % 2][:, slot(n, tile, i), :])
                    ins.then_inc(stats_made, 1)

                def normalise(n, half, q, tile):
                    dve.wait_ge(norm_known, n + 1)
                    dve.wait_ge(pt_made, n + 1)
                    for i in range(SR):
                        ins = dve.tensor_scalar(pn[:, i:i + 1, :], ptile[tile % 2][:, slot(n, tile, i), :],
                                                mean[:, i:i + 1], rstd[:, i:i + 1], ALU.subtract, ALU.mult)
                    ins.then_inc(pn_made, 1)

                def gate(n, half, q, tile):
                    dve.wait_ge(o_made, n + 1)
                    dve.wait_ge(g_in[q], (half + 1) * 16)
                    flat = gs[q][:].rearrange("p i c -> p (i c)")
                    dve.tensor_tensor(flat, po[q][:], flat, ALU.mult).then_inc(gated, 1)

                def body(r, t, q, first):
                    now(measure, r, t, q)
                    behind(gate, r, t, q, first)
                    now(normalise, r, t, q)

                rounds(dve, body)
                at_end(gate)

            @block.gpsimd
            def _(pool):
                def know(n, half, q, tile):
                    pool.wait_ge(stats_made, n + 1)
                    statistics(pool, chain, n * STAT_STEPS, stats, mean[:], rstd[:], tmp, numbers, PLAIN,
                               norm_known)

                def add(n, half, q, tile):
                    pool.wait_ge(gated, n + 3)
                    pool.wait_ge(x_in[q], (half + 1) * 16)
                    at = ptile[tile % 2][:, slot(n, tile), :]
                    pool.tensor_tensor(at, at, gs[q][:], ALU.add).then_inc(added, 1)

                def body(r, t, q, first):
                    now(know, r, t, q)
                    behind(add, r, t, q, first)

                rounds(pool, body)
                at_end(add)

            @block.scalar
            def _(act):
                act.sem_inc(p_made, 2)

                def fetch_gate(n, q):
                    act.dma_start(gs[q][:], rows[1][:, bass.ds(n * SR, SR), :]).then_inc(g_in[q], 16)

                fetch_gate(0, 0)
                fetch_gate(1, 1)

                def take_sums(r, s, q):
                    n = s + r * STEPS
                    act.wait_ge(chunk_used, (n + 2) * SUBS)
                    act.activation(ptile[r % 2][:, :, bass.ds(s * SC, SC)].rearrange("p i c -> p c i"),
                                   psum[q][:].rearrange("p (c i) -> p c i", c=SC), ACT.Copy).then_inc(p_made, 1)

                def take_flipped(n, half, q, tile):
                    act.wait_ge(pt_made, n + 2)
                    act.activation(pt[:], tp[q][:], ACT.Copy).then_inc(pt_copied, 1)
                    act.dma_start(ptile[tile % 2][:, slot(n, tile), :],
                                  rows[0][:, bass.ds(n * SR, SR), :]).then_inc(x_in[q], 16)

                def store(n, half, q, tile):
                    act.wait_ge(added, n + 1)
                    act.dma_start(rows[2][:, bass.ds(n * SR, SR), :],
                                  ptile[tile % 2][:, slot(n, tile), :]).then_inc(stored, 16)
                    if not isinstance(n, int) or n + 2 <= last_step:
                        fetch_gate(n + 2, q)

                def body(r, t, q, first):
                    if first:
                        behind(store, r, t, q, first)
                        if 2 <= r < len(TILES):
                            act.wait_ge(stored, 16 * STEPS * (r - 1))
                    if r < len(TILES):
                        take_sums(r, t * 2 + q, q)
                    now(take_flipped, r, t, q)
                    if not first:
                        behind(store, r, t, q, first)

                rounds(act, body)
                at_end(store)
                act.wait_ge(stored, 16 * (last_step + 1))


def scan_input(nc, tag, x, w_t, gamma, beta, wx, scale, shift, ident, numbers):
    with Scope(nc, tag) as m:
        weight = m.sb("weight", [P, P])
        average = m.sb("average", [P, P])
        gamma_col, beta_col = m.sb("gamma", [P, 1]), m.sb("beta", [P, 1])
        xs = [m.sb(f"x{q}", [P, H, R, C]) for q in range(2)]
        xn = [m.sb(f"xn{q}", [P, R, H, C]) for q in range(2)]
        zt = [m.sb(f"zt{q}", [P, R * P]) for q in range(2)]
        stats = [m.sb(f"stats{q}", [P, H * R, 6]) for q in range(2)]
        mean = [m.sb(f"mean{q}", [P, H * R]) for q in range(2)]
        rstd = [m.sb(f"rstd{q}", [P, H * R]) for q in range(2)]
        tmp = m.sb("tmp", [P, 3, H * R])
        batch = m.sb("batch", [P, G, 6])
        moments = m.sb("moments", [P, 2])
        means, diff, var = m.sb("means", [P, 1]), m.sb("diff", [P, 1]), m.sb("var", [P, 1])
        inv = m.sb("inv", [P, 1])
        tp = [m.ps(f"tp{q}") for q in range(2)]
        po = [m.ps(f"po{q}") for q in range(2)]
        pm = m.ps("pm")
        pm2 = m.ps("pm2")
        x_in = [m.sem(f"x_in{q}") for q in range(2)]
        w_in, zeroed, w_made = m.sem("w_in"), m.sem("zeroed"), m.sem("w_made")
        stats_made, norm_known, chain, xn_made, xt_made, zt_made, o_made, wx_made, counted = (
            m.sem(n) for n in ("stats_made", "norm_known", "chain", "xn_made", "xt_made", "zt_made", "o_made",
                               "wx_made", "counted"))
        end = m.sem("end")
        inv_made = m.sem("inv_made")
        averaged = m.sem("averaged")

        def units(eng, unit):
            with eng.Fori(0, G // 2 - 1) as t:
                for q in range(2):
                    unit(t * 2 + q, t, q, True)
            for q in range(2):
                unit(G - 2 + q, G // 2 - 1, q, q == 0)

        with nc.Block() as block:

            @block.sync
            def _(sp):
                sp.wait_ge(zeroed, 1)
                for h in range(H):
                    sp.dma_start(weight[h * C:(h + 1) * C, h * C:(h + 1) * C], w_t).then_inc(w_in, 16)
                    sp.dma_start(gamma_col[h * C:(h + 1) * C, :], gamma.unsqueeze(1)).then_inc(w_in, 16)
                    sp.dma_start(beta_col[h * C:(h + 1) * C, :], beta.unsqueeze(1)).then_inc(w_in, 16)
                sp.sem_inc(xn_made, 2)
                with sp.Fori(0, G // 2) as t:
                    for q in range(2):
                        n = t * 2 + q
                        sp.wait_ge(xn_made, n + 1)
                        sp.dma_start(xs[q][:], x[:, :, bass.ds(n * R, R), :]).then_inc(x_in[q], 16)

            @block.vector
            def _(dve):
                dve.memset(weight[:], 0.0).then_inc(zeroed, 1)
                at = 0
                for a in range(H):
                    for b in range(H):
                        cols = average[:, a * C:(a + 1) * C]
                        if b == 0:
                            dve.tensor_scalar(cols, ident[:, 0:C], 0.5, None, ALU.mult).then_inc(end, 1)
                        else:
                            dve.wait_ge(end, at)
                            dve.scalar_tensor_tensor(cols, ident[:, C:2 * C], 0.5, cols, ALU.mult, ALU.add
                                                     ).then_inc(end, 1)
                        at += 1

                def measure(half_t, q):
                    dve.wait_ge(x_in[q], 16 * (half_t + 1))
                    for h in range(H):
                        for i in range(R):
                            ins = dve.bn_stats(stats[q][:, h * R + i, :], xs[q][:, h, i, :])
                    ins.then_inc(stats_made, 1)

                def normalise(n, q):
                    dve.wait_ge(norm_known, n + 1)
                    for h in range(H):
                        for i in range(R):
                            k = h * R + i
                            ins = dve.tensor_scalar(xn[q][:, i, h, :], xs[q][:, h, i, :], mean[q][:, k:k + 1],
                                                    rstd[q][:, k:k + 1], ALU.subtract, ALU.mult)
                    ins.then_inc(xn_made, 1)

                measure(0, 0)
                normalise(0, 0)

                def unit(u, t, q, more):
                    if more:
                        measure(t + q, 1 - q)
                        normalise(u + 1, 1 - q)
                    dve.wait_ge(wx_made, u + 3)
                    dve.bn_stats(batch[:, bass.ds(u, 1), :], wx[:, :, bass.ds(u * R, R)]).then_inc(counted, 1)

                units(dve, unit)
                dve.wait_ge(counted, G)
                dve.bn_aggr(moments[:], batch[:].rearrange("p g f -> p (g f)")).then_inc(end, 1)
                dve.wait_ge(averaged, 1)
                dve.tensor_copy(means[:], pm[:, 0:1]).then_inc(end, 1)
                dve.wait_ge(end, at + 2)
                dve.tensor_tensor(diff[:], moments[:, 0:1], means[:], ALU.subtract).then_inc(end, 1)
                dve.wait_ge(end, at + 3)
                dve.tensor_tensor(diff[:], diff[:], diff[:], ALU.mult).then_inc(end, 1)
                dve.wait_ge(end, at + 4)
                dve.tensor_tensor(var[:], diff[:], moments[:, 1:2], ALU.add).then_inc(end, 1)
                dve.wait_ge(averaged, 2)
                dve.tensor_scalar(inv[:], pm2[:, 0:1], 1e-5, None, ALU.add).then_inc(end, 1)
                dve.wait_ge(inv_made, 1)
                dve.wait_ge(w_in, 16 * 3 * H)
                dve.tensor_tensor(scale[:], inv[:], gamma_col[:], ALU.mult).then_inc(end, 1)
                dve.wait_ge(end, at + 7)
                dve.tensor_tensor(diff[:], means[:], scale[:], ALU.mult).then_inc(end, 1)
                dve.wait_ge(end, at + 8)
                dve.tensor_tensor(shift[:], beta_col[:], diff[:], ALU.subtract).then_inc(end, 1)

            @block.gpsimd
            def _(pool):
                def know(n, q):
                    pool.wait_ge(stats_made, n + 1)
                    statistics(pool, chain, n * STAT_STEPS, stats[q], mean[q][:], rstd[q][:], tmp, numbers, PLAIN,
                               norm_known)

                know(0, 0)
                with pool.Fori(0, G // 2 - 1) as t:
                    for q in range(2):
                        know(t * 2 + q + 1, 1 - q)
                know(G - 1, 1)
                pool.wait_ge(end, 2 * H + 6)
                pool.tensor_tensor(inv[:], inv[:], numbers[:, POWER:POWER + 1], ALU.pow).then_inc(inv_made, 1)

            @block.tensor
            def _(pe):
                def flip(n, q):
                    pe.wait_ge(xn_made, n + 3)
                    for i in range(R):
                        ins = pe.transpose(tp[q][:, i * P:(i + 1) * P], xn[q][:, i].rearrange("p h c -> p (h c)"),
                                           ident[:])
                    ins.then_inc(xt_made, 1)

                flip(0, 0)
                pe.wait_ge(w_in, 16 * 3 * H)

                def unit(u, t, q, more):
                    if more:
                        flip(u + 1, 1 - q)
                    pe.wait_ge(zt_made, u + 1)
                    pe.wait_ge(wx_made, u + 1)
                    pe.matmul(po[q][:], weight[:], zt[q][:], start=True, stop=True).then_inc(o_made, 1)

                units(pe, unit)
                pe.wait_ge(end, 2 * H + 1)
                pe.matmul(pm[:, 0:2], average[:], moments[:], start=True, stop=True).then_inc(averaged, 1)
                pe.wait_ge(end, 2 * H + 5)
                pe.matmul(pm2[:, 0:1], average[:], var[:], start=True, stop=True).then_inc(averaged, 1)

            @block.scalar
            def _(act):
                act.sem_inc(wx_made, 2)

                def take(n, q):
                    act.wait_ge(xt_made, n + 1)
                    act.activation(zt[q][:], tp[q][:], ACT.Copy).then_inc(zt_made, 1)

                take(0, 0)

                def unit(u, t, q, more):
                    if more:
                        take(u + 1, 1 - q)
                    act.wait_ge(o_made, u + 1)
                    act.activation(wx[:, :, bass.ds(u * R, R)].rearrange("p s i -> p i s"),
                                   po[q][:].rearrange("p (i s) -> p i s", i=R), ACT.Copy).then_inc(wx_made, 1)

                units(act, unit)


def scan(nc, tag, v_t, wx, scale, shift, y_dram):
    STEPS = 64
    SH = P // STEPS
    CHUNKS = N * H * SH
    WARM = 16
    NY = 8
    LANES = SH * 2
    CLOSE = 2.0 ** -18
    with Scope(nc, tag) as m:
        vt = m.sb("vt", [P, P])
        ys = m.sb("ys", [P, 2, SH, NB, NY, BLK])
        start = m.sb("start", [P, SH, N])
        found = m.sb("found", [P, SH, N])
        ends = m.sb("ends", [P, SH, N])
        pre = m.sb("pre", [P, LANES, P])
        worst = m.sb("worst", [P, 1])
        ones_col = m.sb("ones_col", [P, 1])
        again = m.sb("again", [P, 1], I32)
        pl = [m.ps(f"lane{q}") for q in range(LANES)]
        pc = m.ps("count")
        v_in, zeroed, started, product, summed, y_made, ends_made, check, counted, again_made = (
            m.sem(n) for n in ("v_in", "zeroed", "started", "product", "summed", "y_made", "ends_made", "check",
                               "counted", "again_made"))
        seen = m.sem("seen")
        CHECKS = 5
        stored = [m.sem(f"stored{q}") for q in range(2)]
        SWEEP_STORES = STEPS // NY // 2

        def lane(q):
            return q // 2, q % 2

        def steps(eng, sweep, batch):
            if sweep is None:
                for buf in range(WARM // NY):
                    batch(buf * NY, STEPS - WARM + buf * NY, buf, None, buf)
            else:
                for b2 in range(STEPS // NY // 2):
                    for buf in range(2):
                        k0 = (b2 * 2 + buf) * NY
                        batch(sweep * STEPS + (WARM + k0), k0, buf, sweep * SWEEP_STORES + b2, b2 * 2 + buf)

        def sweeps(eng, run, sets_flag=False):
            run(0)
            eng.wait_ge(again_made, 1)
            flag = eng.value_load(again[0:1, 0:1], min_val=0, max_val=1)
            with eng.If(flag > 0):
                with eng.Fori(1, CHUNKS) as k:
                    eng.wait_ge(again_made, k)
                    eng.sem_inc(seen, 1)
                    more = eng.value_load(again[0:1, 0:1], min_val=0, max_val=1)
                    with eng.If(more > 0):
                        run(k)
                    if sets_flag:
                        with eng.If(more < 1):
                            eng.sem_inc(again_made, 1)

        with nc.Block() as block:

            @block.tensor
            def _(pe):
                pe.wait_ge(v_in, 16 * H)
                pe.wait_ge(zeroed, 4)

                def batch(base, k0, buf, stores, b):
                    for k in range(NY):
                        for q in range(LANES):
                            sh, ih = lane(q)
                            if k == 0 and b == 0:
                                state = start[:, sh, ih * P:(ih + 1) * P]
                            else:
                                from_buf, from_k = (buf, k - 1) if k else (1 - buf, NY - 1)
                                pe.wait_ge(y_made, (base + k - 1) * LANES + q + 1)
                                state = ys[:, from_buf, sh, ih * (NB // 2):(ih + 1) * (NB // 2), from_k, :]
                            pe.matmul(pl[q][:, 0:P], vt[:], state, start=True, stop=True).then_inc(product, 1)

                steps(pe, None, batch)

                def run(sweep):
                    pe.wait_ge(started, sweep + 1)
                    steps(pe, sweep, batch)
                    pe.wait_ge(check, (sweep + 1) * CHECKS)
                    pe.matmul(pc[0:1, 0:1], worst[:], ones_col[:], start=True, stop=True).then_inc(counted, 1)

                sweeps(pe, run)

            @block.vector
            def _(dve):
                dve.memset(vt[:], 0.0).then_inc(zeroed, 1)
                dve.memset(start[:], 0.0).then_inc(zeroed, 1)
                dve.memset(found[:], 0.0).then_inc(zeroed, 1)
                dve.memset(ones_col[:], 1.0).then_inc(zeroed, 1)

                def batch(base, k0, buf, stores, b):
                    for k in range(NY):
                        for q in range(LANES):
                            sh, ih = lane(q)
                            dve.wait_ge(product, (base + k) * LANES + q + 1)
                            dve.scalar_tensor_tensor(pre[:, q, :], wx[:, sh * STEPS + k0 + k, ih * P:(ih + 1) * P],
                                                     scale[:], pl[q][:, 0:P], ALU.mult, ALU.add).then_inc(summed, 1)

                def guesses(to, step):
                    dve.wait_ge(y_made, step * LANES)
                    for sh in range(SH):
                        dve.tensor_copy(ends[:, sh].rearrange("p (b i) -> p b i", i=BLK),
                                        ys[:, 1, sh, :, NY - 1, :]).then_inc(ends_made, 1)

                    return [lambda: dve.tensor_copy(to[:, 1, :], ends[:, 0, :]),
                            lambda: dve.tensor_copy(to[C:P, 0, :], ends[0:C, 1, :]),
                            lambda: dve.tensor_copy(to[0:C, 0, 1:N], ends[C:P, 1, 0:N - 1])]

                steps(dve, None, batch)
                dve.wait_ge(zeroed, 4)
                copies = guesses(start, WARM)
                dve.wait_ge(ends_made, SH)
                for copy in copies:
                    ins = copy()
                ins.then_inc(started, 1)

                def run(sweep):
                    steps(dve, sweep, batch)
                    copies = guesses(found, sweep * STEPS + (WARM + STEPS))
                    dve.wait_ge(ends_made, sweep * SH + 2 * SH)
                    for copy in copies:
                        ins = copy()
                    at = sweep * CHECKS
                    ins.then_inc(check, 1)
                    dve.wait_ge(check, at + 1)
                    dve.tensor_tensor(ends[:], found[:], start[:], ALU.subtract).then_inc(check, 1)
                    dve.wait_ge(check, at + 2)
                    dve.tensor_tensor(ends[:], ends[:], ends[:], ALU.mult).then_inc(check, 1)
                    dve.wait_ge(check, at + 3)
                    dve.tensor_reduce(worst[:], ends[:], AX.XY, ALU.max).then_inc(check, 1)
                    dve.wait_ge(check, at + 4)
                    dve.tensor_scalar(worst[:], worst[:], CLOSE * CLOSE, None, ALU.is_gt).then_inc(check, 1)
                    dve.tensor_copy(start[:], found[:]).then_inc(started, 1)
                    dve.wait_ge(counted, sweep + 1)
                    dve.tensor_scalar(again[0:1, :], pc[0:1, 0:1], 0.5, None, ALU.is_gt).then_inc(again_made, 1)

                sweeps(dve, run, sets_flag=True)

            @block.scalar
            def _(act):
                act.sem_inc(stored[0], 16 * SH)
                act.sem_inc(stored[1], 16 * SH)

                def batch(base, k0, buf, stores, b):
                    if stores is not None:
                        act.wait_ge(stored[buf], (stores + 1) * (16 * SH))
                    for k in range(NY):
                        for q in range(LANES):
                            sh, ih = lane(q)
                            act.wait_ge(summed, (base + k) * LANES + q + 1)
                            act.activation(ys[:, buf, sh, ih * (NB // 2):(ih + 1) * (NB // 2), k, :],
                                           pre[:, q, :].rearrange("p (b i) -> p b i", i=BLK), ACT.Sigmoid,
                                           bias=shift[:]).then_inc(y_made, 1)

                steps(act, None, batch)

                def run(sweep):
                    act.wait_ge(started, sweep + 1)
                    steps(act, sweep, batch)

                sweeps(act, run)

            @block.sync
            def _(sp):
                sp.wait_ge(zeroed, 1)
                for h in range(H):
                    sp.dma_start(vt[h * C:(h + 1) * C, h * C:(h + 1) * C], v_t).then_inc(v_in, 16)

                def batch(base, k0, buf, stores, b):
                    if stores is None:
                        return
                    sp.wait_ge(y_made, (base + NY) * LANES)
                    for sh in range(SH):
                        to = y_dram[:, :, sh * STEPS + k0:sh * STEPS + k0 + NY, :]
                        sp.dma_start(to.rearrange("p b s i -> p b (s i)"),
                                     ys[:, buf, sh].rearrange("p b s i -> p b (s i)")).then_inc(stored[buf], 16)

                def run(sweep):
                    steps(sp, sweep, batch)
                    for buf in range(2):
                        sp.wait_ge(stored[buf], (sweep + 1) * (SWEEP_STORES * 16 * SH) + 16 * SH)
                    sp.sem_inc(seen, 1)

                sweeps(sp, run)


def add_scan(nc, tag, x, y_dram, out, ident):
    GB = BLK // R
    with Scope(nc, tag) as m:
        yb = [m.sb(f"y{q}", [P, P, BLK]) for q in range(2)]
        xs = [m.sb(f"x{q}", [P, H, R, C]) for q in range(4)]
        tp = [m.ps(f"tp{q}") for q in range(2)]
        y_in = [m.sem(f"y_in{q}") for q in range(2)]
        x_in = [m.sem(f"x_in{q}") for q in range(4)]
        stored = [m.sem(f"stored{q}") for q in range(4)]
        flipped, added, y_used = m.sem("flipped"), m.sem("added"), m.sem("y_used")

        with nc.Block() as block:

            @block.sync
            def _(sp):
                with sp.Fori(0, G // 4) as t:
                    for j in range(4):
                        sp.wait_ge(stored[j], (t + 1) * 16)
                        sp.dma_start(xs[j][:], x[:, :, bass.ds((t * 4 + j) * R, R), :]).then_inc(x_in[j], 16)

            @block.gpsimd
            def _(pool):
                pool.sem_inc(y_used, 2)
                with pool.Fori(0, NB // 2) as b2:
                    for buf in range(2):
                        pool.wait_ge(y_used, b2 * 2 + buf + 1)
                        pool.dma_start(yb[buf][:], y_dram[:, bass.ds(b2 * 2 + buf, 1)]
                                      .rearrange("p b s i -> p (b s) i")).then_inc(y_in[buf], 16)

            @block.tensor
            def _(pe):
                with pe.Fori(0, NB // 2) as b2:
                    for buf in range(2):
                        pe.wait_ge(y_in[buf], (b2 + 1) * 16)
                        for g in range(GB):
                            n = (b2 * 2 + buf) * GB + g
                            pe.wait_ge(added, n + 1)
                            for i in range(R):
                                ins = pe.transpose(tp[g % 2][:, i * P:(i + 1) * P], yb[buf][:, :, g * R + i], ident[:])
                            ins.then_inc(flipped, 1)
                            if g == GB - 1:
                                pe.wait_ge(flipped, n + 1)
                                pe.sem_inc(y_used, 1)

            @block.vector
            def _(dve):
                dve.sem_inc(added, 2)
                with dve.Fori(0, G // 4) as t:
                    for j in range(4):
                        n = t * 4 + j
                        dve.wait_ge(x_in[j], (t + 1) * 16)
                        dve.wait_ge(flipped, n + 1)
                        at = xs[j][:].rearrange("p h i c -> p i h c")
                        dve.tensor_tensor(at, tp[j % 2][:].rearrange("p (i h c) -> p i h c", i=R, h=H), at,
                                          ALU.add).then_inc(added, 1)

            @block.scalar
            def _(act):
                for j in range(4):
                    act.sem_inc(stored[j], 16)
                with act.Fori(0, G // 4) as t:
                    for j in range(4):
                        n = t * 4 + j
                        act.wait_ge(added, n + 3)
                        act.dma_start(out[:, :, bass.ds(n * R, R), :], xs[j][:]).then_inc(stored[j], 16)
                for j in range(4):
                    act.wait_ge(stored[j], 16 * (G // 4 + 1))


def experts(nc, tag, x, router_w, router_b, expert_w, expert_b, out, ident, ones3, numbers):
    T = H * R
    TH = 4
    PAIRS = E // 2
    ROUNDS = (T // TH) * PAIRS
    FAR = 1e30
    F16 = mybir.dt.float16
    with Scope(nc, tag) as m:
        router = m.sb("router", [P, E])
        router3 = m.sb("router3", [P, E], BF16)
        router_rows = m.sb("router_rows", [P, E])
        part = m.sb("part", [P, 3, E], BF16)
        expert = m.sb("expert", [P, PAIRS, C])
        expert_bias = m.sb("expert_bias", [T * E, T, C])
        spread = m.sb("spread", [P, T, PAIRS, 2, C], F16)
        twice = m.sb("twice", [P, T * E])
        rank = m.sb("rank", [P, E])
        xs = [m.sb(f"x{q}", [P, H, R, C]) for q in range(3)]
        xn = m.sb("xn", [P, T, 2, C])
        xt = [m.sb(f"xt{q}", [P, T, P]) for q in range(2)]
        xe = [m.sb(f"xe{q}", [P, TH, P]) for q in range(2)]
        stats = [m.sb(f"stats{q}", [P, T, 6]) for q in range(2)]
        mean = [m.sb(f"mean{q}", [P, T]) for q in range(2)]
        rstd = [m.sb(f"rstd{q}", [P, T]) for q in range(2)]
        tmp = m.sb("tmp", [P, 3, T])
        logit = m.sb("logit", [P, T, E])
        first = m.sb("first", [P, T, E])
        second = m.sb("second", [P, T, E])
        work = m.sb("work", [P, T, E])
        top = m.sb("top", [P, 2, T])
        pick = m.sb("pick", [P, T])
        gap = m.sb("gap", [P, T])
        share = m.sb("share", [P, 2, T])
        shares = m.sb("shares", [P, 2, T * E])
        wt = [m.sb(f"wt{q}", [T * E, P]) for q in range(2)]
        wt16 = [m.sb(f"wt16{q}", [P, P], F16) for q in range(2)]
        whole16 = m.sb("whole16", [P, P], F16)
        outs = [m.sb(f"out{q}", [P, H, R, C]) for q in range(2)]
        tp = [m.ps(f"tp{q}") for q in range(2)]
        pl = m.ps("logits")
        pw = m.ps("turned")
        pb = [m.ps(f"spread{q}") for q in range(2)]
        po = [m.ps(f"po{q}") for q in range(2)]

        zeroed, loaded, made = (m.sem(n) for n in ("zeroed", "loaded", "made"))
        n_loads = 2 + 3 + E + T * E
        with nc.Block() as block:

            @block.sync
            def _(sp):
                sp.wait_ge(zeroed, 5)
                sp.dma_start(router[0:C, :], router_w).then_inc(loaded, 16)
                for q in range(3):
                    sp.dma_start(router_rows[32 * q:32 * q + 1, :], router_b.unsqueeze(0)).then_inc(loaded, 16)
                for e in range(E):
                    sp.dma_start(expert[(e % 2) * C:(e % 2 + 1) * C, e // 2, :], expert_w[e]).then_inc(loaded, 16)
                for t in range(T):
                    sp.dma_start(expert_bias[t * E:(t + 1) * E, t, :], expert_b).then_inc(loaded, 16)

            @block.vector
            def _(dve):
                for t in (router, router_rows, expert_bias, router3):
                    dve.memset(t[:], 0.0).then_inc(zeroed, 1)
                for e in range(E):
                    ins = dve.memset(rank[:, e:e + 1], float(E - e))
                ins.then_inc(zeroed, 1)
                dve.tensor_tensor(twice[:], ident[:, 0:C], ident[:, C:2 * C], ALU.add).then_inc(made, 1)
                dve.wait_ge(made, 1)
                dve.tensor_copy(spread[:].rearrange("p t a b c -> p (t a b) c"), over(twice[:], C)).then_inc(made, 1)
                dve.wait_ge(loaded, 16 * (1 + 3 + E + T))
                at = 2
                for q in range(3):
                    dve.tensor_copy(part[:, q, :], router_rows[:]).then_inc(made, 1)
                    at += 1
                    dve.wait_ge(made, at)
                    if q < 2:
                        dve.tensor_tensor(router_rows[:], router_rows[:], part[:, q, :], ALU.subtract).then_inc(made, 1)
                        at += 1
                        dve.wait_ge(made, at)
                for q in range(3):
                    ins = dve.tensor_copy(router3[32 * q:32 * q + 32, :], part[32 * q:32 * q + 32, q, :])
                ins.then_inc(made, 1)

        x_in = [m.sem(f"x_in{q}") for q in range(2)]
        x_free, stats_made, chain, norm_known, xn_made, xt_made, xt_copied, l_made = (
            m.sem(n) for n in ("x_free", "stats_made", "chain", "norm_known", "xn_made", "xt_made", "xt_copied",
                               "l_made"))
        gap_made, share_made, w_made, w_turned, w_copied, w_split, spread_made, xe_made, o_made, out_made, route = (
            m.sem(n) for n in ("gap_made", "share_made", "w_made", "w_turned", "w_copied", "w_split", "spread_made",
                               "xe_made", "o_made", "out_made", "route"))
        stored = [m.sem(f"stored{q}") for q in range(2)]
        xe_used, xt_half = m.sem("xe_used"), m.sem("xt_half")
        ROUTE_STEPS = 14

        def units(eng, unit):
            with eng.Fori(0, G // 2 - 1) as t:
                for q in range(2):
                    unit(t * 2 + q, t, q, True)
            for q in range(2):
                unit(G - 2 + q, G // 2 - 1, q, q == 0)

        with nc.Block() as block:

            @block.sync
            def _(sp):
                sp.sem_inc(out_made, 2)
                with sp.Fori(0, G // 2) as t:
                    for q in range(2):
                        n = t * 2 + q
                        sp.wait_ge(out_made, n + 1)
                        sp.dma_start(xs[q][:], x[:, :, bass.ds(n * R, R), :]).then_inc(x_in[q], 16)

            @block.vector
            def _(dve):
                def measure(half_t, q):
                    dve.wait_ge(x_in[q], 16 * (half_t + 1))
                    for h in range(H):
                        for i in range(R):
                            ins = dve.bn_stats(stats[q][:, h * R + i, :], xs[q][:, h, i, :])
                    ins.then_inc(stats_made, 1)

                def normalise(n, q):
                    dve.wait_ge(norm_known, n + 1)
                    dve.wait_ge(xt_made, n + 1)
                    for h in range(H):
                        for i in range(R):
                            k = h * R + i
                            ins = dve.tensor_scalar(xn[:, k], xs[q][:, h, i, :].unsqueeze(1).to_broadcast([P, 2, C]), mean[q][:, k:k + 1],
                                                    rstd[q][:, k:k + 1], ALU.subtract, ALU.mult)
                    ins.then_inc(xn_made, 1)

                def choose(n):
                    base = n * ROUTE_STEPS
                    at = [0]

                    def step(ins):
                        ins.then_inc(route, 1)
                        at[0] += 1
                        dve.wait_ge(route, base + at[0])

                    def one_hot(to, largest):
                        step(dve.tensor_tensor(work[:], logit[:], over(largest, E), ALU.is_ge))
                        step(dve.tensor_tensor(work[:], work[:], rank[:].unsqueeze(1).to_broadcast([P, T, E]),
                                               ALU.mult))
                        step(dve.tensor_reduce(pick[:], work[:], AX.X, ALU.max))
                        step(dve.tensor_tensor(to[:], work[:], over(pick[:], E), ALU.is_ge))

                    dve.wait_ge(l_made, n + 1)
                    step(dve.tensor_copy(logit[:].rearrange("p t e -> p (t e)"), pl[:, 0:T * E]))
                    step(dve.tensor_reduce(top[:, 0, :], logit[:], AX.X, ALU.max))
                    one_hot(first, top[:, 0, :])
                    step(dve.scalar_tensor_tensor(logit[:], first[:], -FAR, logit[:], ALU.mult, ALU.add))
                    step(dve.tensor_reduce(top[:, 1, :], logit[:], AX.X, ALU.max))
                    dve.tensor_tensor(gap[:], top[:, 1, :], top[:, 0, :], ALU.subtract).then_inc(gap_made, 1)
                    one_hot(second, top[:, 1, :])
                    dve.wait_ge(share_made, n + 1)
                    step(dve.tensor_tensor(first[:], first[:], over(share[:, 0, :], E), ALU.mult))
                    step(dve.tensor_tensor(second[:], second[:], over(share[:, 1, :], E), ALU.mult))
                    dve.tensor_tensor(shares[:], twofold(first), twofold(second), ALU.add).then_inc(w_made, 1)
                    assert at[0] == ROUTE_STEPS

                def twofold(t):
                    return t[:].rearrange("p t e -> p (t e)").unsqueeze(1).to_broadcast([P, 2, T * E])

                def split(n, q):
                    dve.wait_ge(w_turned, n + 1)
                    dve.tensor_copy(wt[q][:], pw[0:T * E, 0:P])
                    dve.tensor_copy(whole16[:], pw[:, 0:P]).then_inc(w_split, 1)
                    dve.wait_ge(w_split, n * 2 + 1)
                    dve.tensor_copy(wt16[q][0:C, :], whole16[0:C, :])
                    dve.tensor_tensor(wt16[q][C:P, :], pw[C:P, 0:P], whole16[C:P, :], ALU.subtract
                                      ).then_inc(w_split, 1)

                def scale_inputs(u, q, k):
                    dve.wait_ge(spread_made, u * ROUNDS + k + 1)
                    dve.wait_ge(xe_used, u * ROUNDS + k + 1)
                    dve.tensor_tensor(xe[k % 2][:].rearrange("p t s -> p (t s)"), pb[k % 2][:],
                                      xt[q][:, (k // PAIRS) * TH:(k // PAIRS + 1) * TH, :]
                                      .rearrange("p t s -> p (t s)"), ALU.mult).then_inc(xe_made, 1)

                dve.sem_inc(xe_made, 2)
                measure(0, 0)
                normalise(0, 0)
                choose(0)
                split(0, 0)

                def unit(u, t, q, more):
                    if more:
                        measure(t + q, 1 - q)
                    for k in range(ROUNDS):
                        scale_inputs(u, q, k)
                        if k == 1 and more:
                            normalise(u + 1, 1 - q)
                        if k == 4 and more:
                            choose(u + 1)
                    if more:
                        split(u + 1, 1 - q)
                    dve.wait_ge(o_made, u + 1)
                    dve.wait_ge(stored[q], (t + 1) * 16)
                    dve.tensor_tensor(outs[q][:].rearrange("p h i c -> p (h i c)"), po[q][:],
                                      xs[q][:].rearrange("p h i c -> p (h i c)"), ALU.add).then_inc(out_made, 1)

                units(dve, unit)

            @block.gpsimd
            def _(pool):
                def know(n, q):
                    pool.wait_ge(stats_made, n + 1)
                    statistics(pool, chain, n * STAT_STEPS, stats[q], mean[q][:], rstd[q][:], tmp, numbers, PLAIN,
                               norm_known)

                know(0, 0)

                def unit(u, t, q, more):
                    if more:
                        know(u + 1, 1 - q)

                units(pool, unit)

            @block.scalar
            def _(act):
                act.sem_inc(stored[0], 16)
                act.sem_inc(stored[1], 16)

                def take(n, q):
                    for b in range(T // TH):
                        act.wait_ge(xt_half, n * (T // TH) + b + 1)
                        act.activation(xt[q][:, b * TH:(b + 1) * TH, :].rearrange("p t s -> p (t s)"), tp[b][:],
                                       ACT.Copy).then_inc(xt_copied, 1)

                def weigh(n):
                    act.wait_ge(gap_made, n + 1)
                    act.activation(share[:, 0, :], gap[:], ACT.Sigmoid, scale=-1.0)
                    act.activation(share[:, 1, :], gap[:], ACT.Sigmoid).then_inc(share_made, 1)

                take(0, 0)
                weigh(0)

                def unit(u, t, q, more):
                    if more:
                        take(u + 1, 1 - q)
                        weigh(u + 1)
                    act.wait_ge(out_made, u + 3)
                    act.dma_start(out[:, :, bass.ds(u * R, R), :], outs[q][:]).then_inc(stored[q], 16)

                units(act, unit)
                for q in range(2):
                    act.wait_ge(stored[q], 16 * (G // 2 + 1))

            @block.tensor
            def _(pe):
                pe.sem_inc(xt_made, 1)
                pe.sem_inc(xe_used, 2)

                def flip(n, q):
                    pe.wait_ge(xn_made, n + 1)
                    for b in range(T // TH):
                        for j in range(TH):
                            ins = pe.transpose(tp[b][:, j * P:(j + 1) * P],
                                               xn[:, b * TH + j].rearrange("p b c -> p (b c)"), ident[:])
                        ins.then_inc(xt_half, 1)
                    pe.wait_ge(xt_half, (n + 1) * (T // TH))
                    pe.sem_inc(xt_made, 1)
                    pe.matmul(pl[:, 0:T * E], ones3[:], router3[:].unsqueeze(1).to_broadcast([P, T, E]),
                              start=True, stop=True)
                    for t in range(T):
                        if t % TH == 0:
                            pe.wait_ge(xt_copied, n * (T // TH) + t // TH + 1)
                        ins = pe.matmul(pl[:, t * E:(t + 1) * E], xt[q][:, t, :], router[:], start=False, stop=True,
                                        skip_group_check=True)
                    ins.then_inc(l_made, 1)

                def turn_shares(n):
                    pe.wait_ge(w_made, n + 1)
                    pe.transpose(pw[:, 0:P], shares[:].rearrange("p b t -> p (b t)"), ident[:]).then_inc(w_turned, 1)

                def spread_out(u, q, k):
                    if k == 0:
                        pe.wait_ge(w_split, u * 2 + 2)
                    pe.wait_ge(xe_made, u * ROUNDS + k + 1)
                    for j in range(TH):
                        ins = pe.matmul(pb[k % 2][:, j * P:(j + 1) * P],
                                        spread[:, (k // PAIRS) * TH + j, k % PAIRS].rearrange("p b c -> p (b c)"),
                                        wt16[q][:], start=True, stop=True)
                    ins.then_inc(spread_made, 1)

                def add_experts(u, q, k):
                    pe.wait_ge(xe_made, u * ROUNDS + k + 3)
                    for j in range(TH):
                        t = (k // PAIRS) * TH + j
                        ins = pe.matmul(po[q][:, t * C:(t + 1) * C], xe[k % 2][:, j, :], expert[:, k % PAIRS, :],
                                        start=False, stop=True, skip_group_check=True)
                    ins.then_inc(xe_used, 1)

                flip(0, 0)
                turn_shares(0)

                def unit(u, t, q, more):
                    spread_out(u, q, 0)
                    pe.wait_ge(out_made, u + 1)
                    pe.matmul(po[q][:], wt[q][:], expert_bias[:].rearrange("k t c -> k (t c)"), start=True, stop=True)
                    for k in range(ROUNDS):
                        if k + 1 < ROUNDS:
                            spread_out(u, q, k + 1)
                        if k == 2 and more:
                            flip(u + 1, 1 - q)
                        if k == 6 and more:
                            turn_shares(u + 1)
                        add_experts(u, q, k)
                    pe.wait_ge(xe_used, (u + 1) * ROUNDS + 2)
                    pe.sem_inc(o_made, 1)

                units(pe, unit)


CONV = ["ln_in_w", "ln_in_b", "w_ap", "b_ap", "w_ag", "b_ag", "w_bp", "b_bp", "w_bg", "b_bg", "ln_out_w",
        "ln_out_b", "w_z", "b_z", "w_g", "b_g"]


def build(nc, a, out):
    def scratch(name, shape):
        return nc.dram_tensor(name, shape, F32, kind="Internal").ap()

    b_dram = scratch("b_scratch", [H, C // CH, P, H, RB, BLK, CH])
    gate_dram = scratch("gate_scratch", [P, H, N, C])
    t0 = scratch("after_conv0", [P, H, N, C])
    y_dram = scratch("scan_scratch", [P, NB, P, BLK])
    t1 = scratch("after_scan", [P, H, N, C])
    t2 = scratch("after_conv1", [P, H, N, C])

    with ExitStack() as s:
        ident = s.enter_context(nc.sbuf_tensor("ident", [P, P], F32))
        ones3 = s.enter_context(nc.sbuf_tensor("ones3", [P, P], BF16))
        numbers = s.enter_context(nc.sbuf_tensor("numbers", [P, len(NUMBERS)], F32))
        constants(nc, ident, ones3, numbers)
        for layer, (x, y) in enumerate([(a["x"], t0), (t1, t2)]):
            w = {k: a[f"L{layer}_conv_{k}"] for k in CONV}
            with nc.sbuf_tensor(f"a_res{layer}", [P, H, C, N], F32) as a_res:
                conv_project(nc, f"cp{layer}", x, a[f"L{layer}_conv_mask"], w, a_res, b_dram, gate_dram, ident,
                             ones3, numbers)
                conv_combine(nc, f"cc{layer}", x, w, a_res, b_dram, gate_dram, y, ident, ones3, numbers)
            if layer == 0:
                with nc.sbuf_tensor("wx", [P, P, N], F32) as wx, nc.sbuf_tensor("bn_scale", [P, 1], F32) as scale, \
                        nc.sbuf_tensor("bn_shift", [P, 1], F32) as shift:
                    scan_input(nc, "si", t0, a["L0_ffn_W_t"], a["L0_ffn_gamma"], a["L0_ffn_beta"], wx, scale, shift,
                               ident, numbers)
                    scan(nc, "sc", a["L0_ffn_V_t"], wx, scale, shift, y_dram)
                add_scan(nc, "as", t0, y_dram, t1, ident)
        experts(nc, "ex", t2, a["L1_ffn_router_w"], a["L1_ffn_router_b"], a["L1_ffn_expert_w"],
                a["L1_ffn_expert_b"], out, ident, ones3, numbers)


def kernel(**inputs):
    import concourse.bacc as bacc
    from concourse.bass_utils import run_bass_kernel_spmd

    arrays = {}
    for name, value in inputs.items():
        v = np.asarray(value)
        if name == "x":
            v = v.reshape(N, H, P, C).transpose(2, 1, 0, 3)
        elif name.endswith("_mask"):
            v = v.reshape(N, H, P).transpose(2, 1, 0)
        elif name in ("L0_ffn_W", "L0_ffn_V"):
            name, v = name + "_t", v.T
        arrays[name] = np.ascontiguousarray(v)
    nc = bacc.Bacc("TRN2", target_bir_lowering=False, num_devices=1)
    aps = {k: nc.dram_tensor("in_" + k, v.shape, mybir.dt.from_np(v.dtype), kind="ExternalInput").ap()
           for k, v in arrays.items()}
    out = nc.dram_tensor("out_0", (P, H, N, C), F32, kind="ExternalOutput").ap()
    build(nc, aps, out)
    r = run_bass_kernel_spmd(nc, [{"in_" + k: v for k, v in arrays.items()}], core_ids=[0])
    return r.results[0]["out_0"].transpose(2, 1, 0, 3).reshape(1, N, N, C)
```

```python
from contextlib import ExitStack

import numpy as np
import concourse.bass as bass
from concourse import mybir

F32 = mybir.dt.float32
BF16 = mybir.dt.bfloat16
I32 = mybir.dt.int32
ALU = mybir.AluOpType
ACT = mybir.ActivationFunctionType
AX = mybir.AxisListType

P = 128
N = 256
C = 64
H = 2
R = 4
G = N // R
BLK = 32
NB = N // BLK
RB = NB // H
CH = 2
E = 8


class Scope(ExitStack):

    def __init__(self, nc, tag):
        super().__init__()
        self.nc, self.tag, self.sems = nc, tag, []

    def sb(self, name, shape, dt=F32):
        return self.enter_context(self.nc.sbuf_tensor(f"{self.tag}_{name}", shape, dt))

    def ps(self, name, shape=(P, 512), dt=F32):
        return self.enter_context(self.nc.psum_tensor(f"{self.tag}_{name}", list(shape), dt))

    def sem(self, name):
        self.sems.append(self.nc.alloc_semaphore(f"{self.tag}_{name}"))
        return self.sems[-1]

    def __exit__(self, *raised):
        if self.sems and raised[0] is None:
            self.nc.clear_and_free_semaphores(self.sems)
            self.nc.all_engine_barrier()
        return super().__exit__(*raised)


def over(ap, n):
    return ap.unsqueeze(len(ap.shape)).to_broadcast(list(ap.shape) + [n])


def constants(nc, ident, ones3, numbers):
    with Scope(nc, "cst") as m:
        made, rows_made = m.sem("made"), m.sem("rows_made")
        with nc.Block() as block:

            @block.vector
            def _(dve):
                dve.memset(ones3[:], 0.0).then_inc(rows_made, 1)
                dve.wait_ge(rows_made, 1)
                for q in range(3):
                    dve.memset(ones3[32 * q:32 * q + 1, :], 1.0).then_inc(rows_made, 1)

            @block.gpsimd
            def _(pool):
                pool.memset(ident[:], 0.0).then_inc(made, 1)
                pool.memset(numbers[:], -0.5).then_inc(made, 1)
                pool.wait_ge(made, 2)
                pool.affine_select(out=ident[:], in_=ident[:], compare_op=ALU.not_equal, fill=1.0, base=0,
                                   pattern=[[-1, P]], channel_multiplier=1).then_inc(made, 1)



def center_weights(nc, tag, weights, ident, banks):
    with Scope(nc, tag) as m:
        center = m.sb("center", [P, P])
        pc = banks
        step, centered = m.sem("step"), m.sem("centered")
        cuts = [(w, at, min(at + 512, w.shape[1])) for w in weights for at in range(0, w.shape[1], 512)]
        with nc.Block() as block:

            @block.vector
            def _(dve):
                dve.memset(center[:], 0.0).then_inc(step, 1)
                dve.wait_ge(step, 1)
                for h in range(H):
                    ins = dve.memset(center[h * C:(h + 1) * C, h * C:(h + 1) * C], -1.0 / C)
                ins.then_inc(step, 1)
                dve.wait_ge(step, 2)
                dve.tensor_tensor(center[:], center[:], ident[:], ALU.add).then_inc(step, 1)
                for n, (w, a, b) in enumerate(cuts):
                    dve.wait_ge(centered, n + 1)
                    dve.tensor_copy(w[:, a:b], pc[n % 2][:, 0:b - a]).then_inc(step, 1)

            @block.tensor
            def _(pe):
                for n, (w, a, b) in enumerate(cuts):
                    pe.wait_ge(step, 3 + max(n - 1, 0))
                    pe.matmul(pc[n % 2][:, 0:b - a], center[:], w[:, a:b], start=True, stop=True).then_inc(centered, 1)


def prepare_weights(nc, tag, weight, bias3, blocks, gain, offset, ident):
    width = len(blocks) * H * C
    with Scope(nc, tag) as m:
        gain_col = m.sb("gain_col", [P, 1])
        offset_col = m.sb("offset_col", [P, 1])
        offset_rows = m.sb("offset_rows", [P, P])
        bias_rows = m.sb("bias_rows", [P, width])
        part = [m.sb(f"part{q}", [P, width], BF16) for q in range(3)]
        folded = [m.ps(f"folded{q}") for q in range(2)]
        zeroed, loaded, rows, summed, step = (m.sem(n) for n in ("zeroed", "loaded", "rows", "summed", "step"))
        n_loads = len(blocks) * H * 4 + 2 * H
        cuts = [(at, min(at + 512, width)) for at in range(0, width, 512)]
        with nc.Block() as block:

            @block.sync
            def _(sp):
                sp.wait_ge(zeroed, 3)
                for k, (matrix, bias) in enumerate(blocks):
                    for h in range(H):
                        at = (k * H + h) * C
                        sp.dma_start(weight[h * C:(h + 1) * C, at:at + C], matrix).then_inc(loaded, 16)
                        for q in range(3):
                            sp.dma_start(bias_rows[32 * q:32 * q + 1, at:at + C],
                                         bias.unsqueeze(0)).then_inc(loaded, 16)
                for h in range(H):
                    sp.dma_start(gain_col[h * C:(h + 1) * C, :], gain.unsqueeze(1)).then_inc(loaded, 16)
                    sp.dma_start(offset_col[h * C:(h + 1) * C, :], offset.unsqueeze(1)).then_inc(loaded, 16)

            @block.tensor
            def _(pe):
                pe.wait_ge(rows, 1)
                for q, (a, b) in enumerate(cuts):
                    pe.matmul(folded[q][:, 0:b - a], offset_rows[:], weight[:, a:b],
                              start=True, stop=True).then_inc(summed, 1)

            @block.vector
            def _(dve):
                dve.memset(weight[:], 0.0).then_inc(zeroed, 1)
                dve.memset(bias_rows[:], 0.0).then_inc(zeroed, 1)
                dve.memset(offset_rows[:], 0.0).then_inc(zeroed, 1)
                dve.memset(bias3[:], 0.0).then_inc(step, 1)
                dve.wait_ge(loaded, 16 * n_loads)
                dve.wait_ge(zeroed, 3)
                for q in range(3):
                    ins = dve.tensor_copy(offset_rows[:, 32 * q:32 * q + 1], offset_col[:])
                ins.then_inc(rows, 1)
                dve.wait_ge(summed, len(cuts))
                for q, (a, b) in enumerate(cuts):
                    ins = dve.tensor_tensor(bias_rows[:, a:b], bias_rows[:, a:b], folded[q][:, 0:b - a], ALU.add)
                ins.then_inc(step, 1)
                dve.tensor_scalar(weight[:], weight[:], gain_col[:], None, ALU.mult).then_inc(step, 1)
                at = 3
                dve.wait_ge(step, at)
                for q in range(3):
                    dve.tensor_copy(part[q][:], bias_rows[:]).then_inc(step, 1)
                    at += 1
                    dve.wait_ge(step, at)
                    if q < 2:
                        dve.tensor_tensor(bias_rows[:], bias_rows[:], part[q][:], ALU.subtract).then_inc(step, 1)
                        at += 1
                        dve.wait_ge(step, at)
                cols = bias3.shape[1]
                for q in range(3):
                    ins = dve.tensor_copy(bias3[32 * q:32 * q + 32, :], part[q][32 * q:32 * q + 32, 0:cols])
                ins.then_inc(step, 1)
        center_weights(nc, tag + "c", [weight[:]], ident, folded)


PLAIN = (1.0, 1e-5)
DOUBLE = (1.0 + 1e-5, 1e-11)
MEASURES = 2


def layer_norm(m, tiles, kind, numbers):
    stats = m.sb("ln_stats", [P, tiles, 6])
    moments = m.sb("ln_moments", [P, tiles, 2])
    var = [m.sb(f"ln_var{q}", [P, tiles]) for q in range(2)]
    rstd = [m.sb(f"ln_rstd{q}", [P, tiles]) for q in range(2)]
    counted, var_made, known, seen = (m.sem(n) for n in ("ln_counted", "ln_var_made", "ln_known", "ln_seen"))

    def find_variances(dve, n, q, tokens):
        for k, tile in enumerate(tokens):
            ins = dve.bn_stats(stats[:, k, :], tile)
        ins.then_inc(counted, 1)
        dve.wait_ge(counted, n * MEASURES + 1)
        dve.sem_inc(seen, 1)
        for k in range(tiles):
            ins = dve.bn_aggr(moments[:, k, :], stats[:, k, :])
        ins.then_inc(counted, 1)
        dve.wait_ge(counted, n * MEASURES + 2)
        dve.tensor_scalar(var[q][:], moments[:, :, 1], *kind, ALU.mult, ALU.add).then_inc(var_made, 1)

    def find_scales(pool, n, q):
        pool.wait_ge(var_made, n + 1)
        pool.tensor_tensor(rstd[q][:], var[q][:], numbers[:, 0:1].to_broadcast([P, tiles]), ALU.pow).then_inc(known, 1)

    return find_variances, find_scales, rstd, known


def quads(eng, unit):
    with eng.Fori(0, G // 4 - 1) as t:
        for j in range(4):
            unit(t * 4 + j, t, j, 3)
    for j in range(4):
        unit(G - 4 + j, G // 4 - 1, j, 3 - j)


def quads_peeled(eng, unit):
    for j in range(4):
        unit(j, 0, j, 3, j > 0)
    with eng.Fori(1, G // 4 - 1) as t:
        for j in range(4):
            unit(t * 4 + j, t, j, 3, True)
    for j in range(4):
        unit(G - 4 + j, G // 4 - 1, j, 3 - j, True)


def conv_project(nc, tag, x, mask, w, a_res, b_dram, gate_dram, ident, ones3, numbers):
    W_COLS = 10 * C
    with Scope(nc, tag) as m:
        weight = m.sb("weight", [P, W_COLS])
        bias3 = m.sb("bias3", [P, W_COLS], BF16)
        prepare_weights(nc, tag + "p", weight, bias3,
                        [(w["w_ag"], w["b_ag"]), (w["w_bg"], w["b_bg"]), (w["w_ap"], w["b_ap"]),
                         (w["w_bp"], w["b_bp"]), (w["w_g"], w["b_g"])], w["ln_in_w"], w["ln_in_b"],
                        ident)

        mask_sb = m.sb("mask", [P, H, N])
        b_stage = m.sb("b_stage", [P, 2, H, C // CH, BLK, CH])
        xs = [m.sb(f"x{q}", [P, H, R, C]) for q in range(4)]
        xn = [m.sb(f"xn{q}", [P, R, H, C]) for q in range(2)]
        zt = [m.sb(f"zt{q}", [P, R * P]) for q in range(2)]
        sig = m.sb("sig", [P, R, 4 * C])
        prod = m.sb("prod", [P, R, 2, H, C])
        gs = [m.sb(f"gs{q}", [P, H, R, C]) for q in range(2)]
        find_variances, find_scales, rstd, known = layer_norm(m, H * R, DOUBLE, numbers)
        tp = [m.ps(f"tp{q}") for q in range(2)]
        pg = [m.ps(f"pg{q}") for q in range(2)]
        pv = [m.ps(f"pv{i}") for i in range(R)]

        mask_in = m.sem("mask_in")
        x_in = [m.sem(f"x_in{q}") for q in range(4)]
        xn_made, xt_made, zt_made = m.sem("xn_made"), m.sem("xt_made"), m.sem("zt_made")
        v_made, sig_made, prod_made, g_made, gs_made = (
            m.sem(n) for n in ("v_made", "sig_made", "prod_made", "g_made", "gs_made"))
        gs_stored = [m.sem(f"gs_stored{q}") for q in range(2)]
        a_made, b_made = m.sem("a_made"), m.sem("b_made")
        b_stored = [m.sem(f"b_stored{q}") for q in range(2)]

        with nc.Block() as block:

            @block.sync
            def _(sp):
                sp.dma_start(mask_sb[:], mask).then_inc(mask_in, 16)
                sp.sem_inc(xn_made, 4)
                for buf in range(2):
                    sp.sem_inc(b_stored[buf], 16 * H)

                def load(n, j):
                    sp.wait_ge(xn_made, n + 1)
                    sp.dma_start(xs[j][:], x[:, :, bass.ds(n * R, R), :]).then_inc(x_in[j], 16)

                def store_b(row_half, blk, buf, groups):
                    sp.wait_ge(b_made, groups + 1)
                    for k in range(H):
                        sp.dma_start(b_dram[row_half, :, :, k, bass.ds(blk, 1)].rearrange("n p b i c -> p n (b i c)"),
                                     b_stage[:, buf, k].rearrange("p n i c -> p n (i c)")).then_inc(b_stored[buf], 16)

                AHEAD = 3
                PER = BLK // R
                for n in range(AHEAD):
                    load(n, n)
                for row_half in range(H):
                    last = row_half == H - 1
                    with sp.Fori(0, RB // 2 - 1 if last else RB // 2) as b2:
                        for buf in range(2):
                            first = row_half * RB * PER + (b2 * 2 + buf) * PER
                            for g in range(PER):
                                load(first + g + AHEAD, (g + AHEAD) % 4)
                            store_b(row_half, b2 * 2 + buf, buf, first + PER)
                    if last:
                        for buf in range(2):
                            first = G - (2 - buf) * PER
                            for g in range(PER):
                                if first + g + AHEAD < G:
                                    load(first + g + AHEAD, (g + AHEAD) % 4)
                            store_b(row_half, RB - 2 + buf, buf, first + PER)
                for buf in range(2):
                    sp.wait_ge(b_stored[buf], 16 * H * (NB // 2 + 1))

            @block.vector
            def _(dve):
                dve.sem_inc(prod_made, R)
                dve.sem_inc(a_made, 1)
                dve.sem_inc(b_made, 1)

                def measure(n, t, j):
                    dve.wait_ge(x_in[j], 16 * (t + 1))
                    find_variances(dve, n, j % 2, [xs[j][:, h, i, :] for h in range(H) for i in range(R)])

                def rescale(n, j):
                    dve.wait_ge(known, n + 1)
                    dve.tensor_tensor(xn[j % 2][:].rearrange("p i h c -> p h i c"), xs[j][:],
                                      over(rstd[j % 2][:].rearrange("p (h i) -> p h i", h=H), C),
                                      ALU.mult).then_inc(xn_made, 1)

                def product(u, i):
                    dve.wait_ge(sig_made, u * R + i + 1)
                    dve.tensor_tensor(prod[:, i].rearrange("p a h c -> p (a h c)"), pv[i][:, 4 * C:8 * C],
                                      sig[:, i, :], ALU.mult).then_inc(prod_made, 1)

                measure(0, 0, 0)
                measure(1, 0, 1)
                rescale(0, 0)
                measure(2, 0, 2)

                def unit(u, t, j, ahead):
                    if ahead:
                        rescale(u + 1, (j + 1) % 4)
                    for i in range(R):
                        if i == 0:
                            dve.wait_ge(a_made, u + 1)
                        if i == R // 2:
                            dve.wait_ge(b_made, u + 1)
                        product(u, i)
                        if i == 1 and ahead > 2:
                            measure(u + 3, t + (j + 3) // 4, (j + 3) % 4)

                quads(dve, unit)

            @block.gpsimd
            def _(pool):
                find_scales(pool, 0, 0)
                find_scales(pool, 1, 1)
                find_scales(pool, 2, 0)
                pool.wait_ge(mask_in, 16)

                def mask_rows(u, part, buf, row):
                    i0, n = part * (R // 2), R // 2
                    pool.wait_ge(prod_made, u * R + R + i0 + n)
                    by = mask_sb[:, :, bass.ds(u * R + i0, n)]
                    pool.tensor_tensor(a_res[:, :, :, bass.ds(u * R + i0, n)].rearrange("p h c i -> p i h c"),
                                       prod[:, i0:i0 + n, 0], over(by.rearrange("p h i -> p i h"), C), ALU.mult)
                    for h in range(H):
                        ins = pool.tensor_tensor(
                            b_stage[:, buf, h, :, bass.ds(row + i0, n), :].rearrange("p n i c -> p i n c"),
                            prod[:, i0:i0 + n, 1, h, :].rearrange("p i (n c) -> p i n c", c=CH),
                            over(over(mask_sb[:, h, bass.ds(u * R + i0, n)], C // CH), CH), ALU.mult)
                    ins.then_inc(b_made if part else a_made, 1)

                def unit(u, j, ahead, buf, row):
                    mask_rows(u, 0, buf, row)
                    if ahead > 2:
                        find_scales(pool, u + 3, (j + 3) % 2)
                    mask_rows(u, 1, buf, row)

                per = BLK // R // 4

                for blk in range(NB):
                    if blk >= 2:
                        pool.wait_ge(b_stored[blk % 2], (blk // 2 + 1) * 16 * H)
                    last = blk == NB - 1
                    with pool.Fori(0, per - 1 if last else per) as t:
                        for j in range(4):
                            unit(blk * (BLK // R) + t * 4 + j, j, 3, blk % 2, (t * 4 + j) * R)
                    if last:
                        for j in range(4):
                            unit(G - 4 + j, j, 3 - j, blk % 2, BLK - 4 * R + j * R)

            @block.tensor
            def _(pe):
                def flip(n, q):
                    pe.wait_ge(xn_made, n + 5)
                    for i in range(R):
                        ins = pe.transpose(tp[q][:, i * P:(i + 1) * P],
                                           xn[q][:, i].rearrange("p h c -> p (h c)"), ident[:])
                    ins.then_inc(xt_made, 1)

                def project(u, q, i):
                    tokens = zt[q][:, i * P:(i + 1) * P]
                    if i == 0:
                        pe.wait_ge(zt_made, u + 1)
                        pe.wait_ge(gs_made, u + 1)
                        pe.matmul(pg[q][:], ones3[:], bias3[:, 8 * C:].unsqueeze(1).to_broadcast([P, R, 2 * C]),
                                  start=True, stop=True)
                    pe.wait_ge(prod_made, u * R + i + 1)
                    pe.matmul(pv[i][:], ones3[:], bias3[:, 0:8 * C], start=True, stop=False)
                    pe.matmul(pv[i][:], tokens, weight[:, 0:8 * C], start=False, stop=True).then_inc(v_made, 1)
                    ins = pe.matmul(pg[q][:, i * 2 * C:(i + 1) * 2 * C], tokens, weight[:, 8 * C:],
                                    start=False, stop=True, skip_group_check=True)
                    if i == R - 1:
                        ins.then_inc(g_made, 1)

                flip(0, 0)

                def unit(u, t, j, ahead):
                    for i in range(R):
                        if i == 2 and ahead:
                            flip(u + 1, (j + 1) % 2)
                        project(u, j % 2, i)

                quads(pe, unit)

            @block.scalar
            def _(act):
                act.sem_inc(gs_made, 2)
                act.sem_inc(gs_stored[0], 16)
                act.sem_inc(gs_stored[1], 16)

                def take(n, q):
                    act.wait_ge(xt_made, n + 1)
                    act.activation(zt[q][:], tp[q][:], ACT.Copy).then_inc(zt_made, 1)

                take(0, 0)

                def unit(u, t, j, ahead):
                    q = j % 2
                    for i in range(R):
                        if i == 3 and ahead:
                            take(u + 1, 1 - q)
                        act.wait_ge(v_made, u * R + i + 1)
                        act.activation(sig[:, i, :], pv[i][:, 0:4 * C], ACT.Sigmoid).then_inc(sig_made, 1)
                    act.wait_ge(g_made, u + 1)
                    act.wait_ge(gs_stored[q], (t * 2 + j // 2 + 1) * 16)
                    act.activation(gs[q][:].rearrange("p h i c -> p i h c"),
                                   pg[q][:].rearrange("p (i h c) -> p i h c", i=R, h=H),
                                   ACT.Sigmoid).then_inc(gs_made, 1)
                    act.wait_ge(gs_made, u + 3)
                    act.dma_start(gate_dram[:, :, bass.ds(u * R, R), :], gs[q][:]).then_inc(gs_stored[q], 16)

                quads(act, unit)
                for q in range(2):
                    act.wait_ge(gs_stored[q], 16 * (G // 2 + 1))


def conv_combine(nc, tag, x, w, a_res, b_dram, gate_dram, out, ident, ones3, numbers):
    TI = P
    TILES = [(h, ih) for h in range(H) for ih in range(N // TI)]
    STEPS = 16
    SR = TI // STEPS
    SC = C // STEPS
    SUBS = SC // CH
    PAIRS = SR // 2
    ROUNDS = len(TILES) + 1
    last_step = len(TILES) * STEPS - 1
    rows = [t.rearrange("p h i c -> p (h i) c") for t in (x, gate_dram, out)]
    with Scope(nc, tag) as m:
        weight = m.sb("weight", [P, H * C])
        bias3 = m.sb("bias3", [P, C], BF16)
        prepare_weights(nc, tag + "p", weight, bias3, [(w["w_z"], w["b_z"])], w["ln_out_w"], w["ln_out_b"], ident)
        ptile = [m.sb(f"p{q}", [P, TI, C]) for q in range(2)]
        bch = [m.sb(f"bch{q}", [P, H, P, CH]) for q in range(SUBS)]
        gs = [m.sb(f"g{q}", [P, SR, C]) for q in range(2)]
        pn = m.sb("pn", [P, SR, C])
        pt = m.sb("pt", [P, PAIRS * P])
        find_variances, find_scales, rstd, known = layer_norm(m, SR, PLAIN, numbers)
        psum = [m.ps(f"sum{q}") for q in range(2)]
        tp = [m.ps(f"tp{q}") for q in range(2)]
        po = [m.ps(f"po{q}") for q in range(2)]

        b_in = [m.sem(f"b_in{j}") for j in range(SUBS)]
        chunk_used, p_made = m.sem("chunk_used"), m.sem("p_made")
        x_in = [m.sem(f"x_in{q}") for q in range(2)]
        g_in = [m.sem(f"g_in{q}") for q in range(2)]
        pn_made, pt_made, pt_copied, o_made, gated, added, stored = (
            m.sem(n) for n in ("pn_made", "pt_made", "pt_copied", "o_made", "gated", "added", "stored"))

        def rounds(eng, body):
            for r in range(ROUNDS):
                for q in range(2):
                    body(r, 0, q, q == 0, False)
                with eng.Fori(1, STEPS // 2 - 1) as t:
                    for q in range(2):
                        body(r, t, q, False, False)
                for q in range(2):
                    body(r, STEPS // 2 - 1, q, False, q == 1)

        def now(part, r, t, q):
            if r > 0:
                half = t + (r - 1) * (STEPS // 2)
                part(half * 2 + q, half, q, r - 1)

        def behind(part, r, t, q, first):
            if r > 0 and not (r == 1 and first):
                half = t + (r - 1) * (STEPS // 2) - (1 - q)
                part(half * 2 + 1 - q, half, 1 - q, r - 2 if first else r - 1)

        def before(part, r, t, q, last):
            if r == 1 and isinstance(t, int) and t == 0 and q == 0:
                part(0, 0, 0, 0)
            if r > 0 and not (r == ROUNDS - 1 and last):
                half = t + (r - 1) * (STEPS // 2) + q
                part(half * 2 + 1 - q, half, 1 - q, r if last else r - 1)

        def at_end(part):
            part(last_step, last_step // 2, 1, len(TILES) - 1)

        def slot(n, tile, i=None):
            at = (n - tile * STEPS) * SR
            return bass.ds(at, SR) if i is None else bass.ds(at + i, 1)

        with nc.Block() as block:

            @block.sync
            def _(sp):
                sp.sem_inc(chunk_used, SUBS)

                def body(r, t, q, first, last):
                    if r < len(TILES):
                        for j in range(SUBS):
                            s = t * 2 + q
                            sp.wait_ge(chunk_used, (s + r * STEPS) * SUBS + j + 1)
                            sp.dma_start(bch[j][:].rearrange("p k j c -> p (k j c)"),
                                         b_dram[TILES[r][0], bass.ds(s * SUBS + j, 1)]
                                         .rearrange("n p k b j c -> p (n k b j c)")).then_inc(b_in[j], 16)

                rounds(sp, body)

            @block.tensor
            def _(pe):
                pe.sem_inc(pt_made, 1)

                def add_up(r, s, q):
                    _, ih = TILES[r]
                    n = s + r * STEPS
                    pe.wait_ge(p_made, n + 1)
                    for j in range(SUBS):
                        pe.wait_ge(b_in[j], (n + 1) * 16)
                        for c in range(CH):
                            at = (j * CH + c) * TI
                            for k in range(H):
                                ins = pe.matmul(psum[q][:, at:at + TI], bch[j][:, k, :, c],
                                                a_res[:, k, bass.ds(s * SC + j * CH + c, 1), ih * TI:(ih + 1) * TI],
                                                start=k == 0, stop=k == H - 1)
                        ins.then_inc(chunk_used, 1)

                def flip(n, half, q, tile):
                    pe.wait_ge(pn_made, n + 1)
                    for j in range(PAIRS):
                        ins = pe.transpose(tp[q][:, j * P:(j + 1) * P],
                                           pn[:, 2 * j:2 * j + 2, :].rearrange("p i c -> p (i c)"), ident[:])
                    ins.then_inc(pt_made, 1)

                def project(n, half, q, tile):
                    pe.wait_ge(pt_copied, n + 1)
                    pe.wait_ge(gated, n + 1)
                    pe.matmul(po[q][:], ones3[:], bias3[:].unsqueeze(1).to_broadcast([P, SR, C]),
                              start=True, stop=True)
                    for j in range(PAIRS):
                        ins = pe.matmul(po[q][:, j * 2 * C:(j + 1) * 2 * C], pt[:, j * P:(j + 1) * P], weight[:],
                                        start=False, stop=True, skip_group_check=True)
                    ins.then_inc(o_made, 1)

                def body(r, t, q, first, last):
                    if r < len(TILES):
                        add_up(r, t * 2 + q, q)
                    behind(project, r, t, q, first)
                    now(flip, r, t, q)

                rounds(pe, body)
                at_end(project)

            @block.vector
            def _(dve):
                dve.sem_inc(gated, 2)

                def measure(n, half, q, tile):
                    dve.wait_ge(p_made, (tile + 1) * STEPS + 2)
                    find_variances(dve, n, q, [ptile[tile % 2][:, slot(n, tile, i), :] for i in range(SR)])

                def scale(n, half, q, tile):
                    dve.wait_ge(known, n + 1)
                    dve.wait_ge(pt_made, n + 1)
                    dve.tensor_tensor(pn[:], ptile[tile % 2][:, slot(n, tile), :], over(rstd[q][:], C),
                                      ALU.mult).then_inc(pn_made, 1)

                def gate(n, half, q, tile):
                    dve.wait_ge(o_made, n + 1)
                    dve.wait_ge(g_in[q], (half + 1) * 16)
                    flat = gs[q][:].rearrange("p i c -> p (i c)")
                    dve.tensor_tensor(flat, po[q][:], flat, ALU.mult).then_inc(gated, 1)

                def body(r, t, q, first, last):
                    before(measure, r, t, q, last)
                    now(scale, r, t, q)
                    behind(gate, r, t, q, first)

                rounds(dve, body)
                at_end(gate)

            @block.gpsimd
            def _(pool):
                def rescaling(n, half, q, tile):
                    find_scales(pool, n, q)

                def add(n, half, q, tile):
                    pool.wait_ge(gated, n + 3)
                    pool.wait_ge(x_in[q], (half + 1) * 16)
                    at = ptile[tile % 2][:, slot(n, tile), :]
                    pool.tensor_tensor(at, at, gs[q][:], ALU.add).then_inc(added, 1)

                def body(r, t, q, first, last):
                    before(rescaling, r, t, q, last)
                    behind(add, r, t, q, first)

                rounds(pool, body)
                at_end(add)

            @block.scalar
            def _(act):
                act.sem_inc(p_made, 2)

                def fetch_gate(n, q):
                    act.dma_start(gs[q][:], rows[1][:, bass.ds(n * SR, SR), :]).then_inc(g_in[q], 16)

                fetch_gate(0, 0)
                fetch_gate(1, 1)

                def take_sums(r, s, q):
                    n = s + r * STEPS
                    act.wait_ge(chunk_used, (n + 2) * SUBS)
                    act.activation(ptile[r % 2][:, :, bass.ds(s * SC, SC)].rearrange("p i c -> p c i"),
                                   psum[q][:].rearrange("p (c i) -> p c i", c=SC), ACT.Copy).then_inc(p_made, 1)

                def take_flipped(n, half, q, tile):
                    act.wait_ge(pt_made, n + 2)
                    act.activation(pt[:], tp[q][:], ACT.Copy).then_inc(pt_copied, 1)
                    act.dma_start(ptile[tile % 2][:, slot(n, tile), :],
                                  rows[0][:, bass.ds(n * SR, SR), :]).then_inc(x_in[q], 16)

                def store(n, half, q, tile):
                    act.wait_ge(added, n + 1)
                    act.dma_start(rows[2][:, bass.ds(n * SR, SR), :],
                                  ptile[tile % 2][:, slot(n, tile), :]).then_inc(stored, 16)
                    if not isinstance(n, int) or n + 2 <= last_step:
                        fetch_gate(n + 2, q)

                def body(r, t, q, first, last):
                    if first:
                        behind(store, r, t, q, first)
                        if 2 <= r < len(TILES):
                            act.wait_ge(stored, 16 * STEPS * (r - 1))
                    if r < len(TILES):
                        take_sums(r, t * 2 + q, q)
                    now(take_flipped, r, t, q)
                    if not first:
                        behind(store, r, t, q, first)

                rounds(act, body)
                at_end(store)
                act.wait_ge(stored, 16 * (last_step + 1))


def scan_input(nc, tag, x, w_t, gamma, beta, wx, scale, shift, ident, numbers):
    with Scope(nc, tag) as m:
        weight = m.sb("weight", [P, P])
        average = m.sb("average", [P, P])
        gamma_col, beta_col = m.sb("gamma", [P, 1]), m.sb("beta", [P, 1])
        xs = [m.sb(f"x{q}", [P, H, R, C]) for q in range(4)]
        xn = [m.sb(f"xn{q}", [P, R, H, C]) for q in range(2)]
        zt = [m.sb(f"zt{q}", [P, R * P]) for q in range(2)]
        find_variances, find_scales, rstd, known = layer_norm(m, H * R, PLAIN, numbers)
        batch = m.sb("batch", [P, G, 6])
        moments = m.sb("moments", [P, 2])
        means, diff, var = m.sb("means", [P, 1]), m.sb("diff", [P, 1]), m.sb("var", [P, 1])
        inv = m.sb("inv", [P, 1])
        tp = [m.ps(f"tp{q}") for q in range(2)]
        po = [m.ps(f"po{q}") for q in range(2)]
        pm = m.ps("pm")
        pm2 = m.ps("pm2")
        x_in = [m.sem(f"x_in{q}") for q in range(4)]
        w_in, zeroed, w_made = m.sem("w_in"), m.sem("zeroed"), m.sem("w_made")
        xn_made, xt_made, zt_made, o_made, wx_made, counted = (
            m.sem(n) for n in ("xn_made", "xt_made", "zt_made", "o_made", "wx_made", "counted"))
        end = m.sem("end")
        inv_made = m.sem("inv_made")
        averaged = m.sem("averaged")

        with nc.Block() as block:

            @block.sync
            def _(sp):
                sp.wait_ge(zeroed, 1)
                for h in range(H):
                    sp.dma_start(weight[h * C:(h + 1) * C, h * C:(h + 1) * C], w_t).then_inc(w_in, 16)
                    sp.dma_start(gamma_col[h * C:(h + 1) * C, :], gamma.unsqueeze(1)).then_inc(w_in, 16)
                    sp.dma_start(beta_col[h * C:(h + 1) * C, :], beta.unsqueeze(1)).then_inc(w_in, 16)
                sp.wait_ge(w_in, 16 * 3 * H)

            @block.vector
            def _(dve):
                dve.memset(weight[:], 0.0).then_inc(zeroed, 1)

        center_weights(nc, tag + "c", [weight[:]], ident, po)

        with nc.Block() as block:

            @block.sync
            def _(sp):
                sp.sem_inc(xn_made, 4)
                with sp.Fori(0, G // 4) as t:
                    for j in range(4):
                        n = t * 4 + j
                        sp.wait_ge(xn_made, n + 1)
                        sp.dma_start(xs[j][:], x[:, :, bass.ds(n * R, R), :]).then_inc(x_in[j], 16)

            @block.vector
            def _(dve):
                at = 0
                for a in range(H):
                    for b in range(H):
                        cols = average[:, a * C:(a + 1) * C]
                        if b == 0:
                            dve.tensor_scalar(cols, ident[:, 0:C], 0.5, None, ALU.mult).then_inc(end, 1)
                        else:
                            dve.wait_ge(end, at)
                            dve.scalar_tensor_tensor(cols, ident[:, C:2 * C], 0.5, cols, ALU.mult, ALU.add
                                                     ).then_inc(end, 1)
                        at += 1

                def measure(n, t, j):
                    dve.wait_ge(x_in[j], 16 * (t + 1))
                    find_variances(dve, n, j % 2, [xs[j][:, h, i, :] for h in range(H) for i in range(R)])

                def rescale(n, j):
                    dve.wait_ge(known, n + 1)
                    dve.tensor_tensor(xn[j % 2][:].rearrange("p i h c -> p h i c"), xs[j][:],
                                      over(rstd[j % 2][:].rearrange("p (h i) -> p h i", h=H), C),
                                      ALU.mult).then_inc(xn_made, 1)

                def count(u):
                    dve.wait_ge(wx_made, u + 3)
                    dve.bn_stats(batch[:, bass.ds(u, 1), :], wx[:, :, bass.ds(u * R, R)]).then_inc(counted, 1)

                measure(0, 0, 0)
                measure(1, 0, 1)
                rescale(0, 0)
                measure(2, 0, 2)

                def unit(u, t, j, ahead):
                    if ahead:
                        rescale(u + 1, (j + 1) % 4)
                    if ahead > 2:
                        measure(u + 3, t + (j + 3) // 4, (j + 3) % 4)
                    count(u)

                quads(dve, unit)
                dve.wait_ge(counted, G)
                dve.bn_aggr(moments[:], batch[:].rearrange("p g f -> p (g f)")).then_inc(end, 1)
                dve.wait_ge(averaged, 1)
                dve.tensor_copy(means[:], pm[:, 0:1]).then_inc(end, 1)
                dve.wait_ge(end, at + 2)
                dve.tensor_tensor(diff[:], moments[:, 0:1], means[:], ALU.subtract).then_inc(end, 1)
                dve.wait_ge(end, at + 3)
                dve.tensor_tensor(diff[:], diff[:], diff[:], ALU.mult).then_inc(end, 1)
                dve.wait_ge(end, at + 4)
                dve.tensor_tensor(var[:], diff[:], moments[:, 1:2], ALU.add).then_inc(end, 1)
                dve.wait_ge(averaged, 2)
                dve.tensor_scalar(inv[:], pm2[:, 0:1], 1e-5, None, ALU.add).then_inc(end, 1)
                dve.wait_ge(inv_made, 1)
                dve.wait_ge(w_in, 16 * 3 * H)
                dve.tensor_tensor(scale[:], inv[:], gamma_col[:], ALU.mult).then_inc(end, 1)
                dve.wait_ge(end, at + 7)
                dve.tensor_tensor(diff[:], means[:], scale[:], ALU.mult).then_inc(end, 1)
                dve.wait_ge(end, at + 8)
                dve.tensor_tensor(shift[:], beta_col[:], diff[:], ALU.subtract).then_inc(end, 1)

            @block.gpsimd
            def _(pool):
                find_scales(pool, 0, 0)
                find_scales(pool, 1, 1)
                find_scales(pool, 2, 0)

                def unit(u, t, j, ahead):
                    if ahead > 2:
                        find_scales(pool, u + 3, (j + 3) % 2)

                quads(pool, unit)
                pool.wait_ge(end, 2 * H + 6)
                pool.tensor_tensor(inv[:], inv[:], numbers[:], ALU.pow).then_inc(inv_made, 1)

            @block.tensor
            def _(pe):
                def flip(n, q):
                    pe.wait_ge(xn_made, n + 5)
                    for i in range(R):
                        ins = pe.transpose(tp[q][:, i * P:(i + 1) * P], xn[q][:, i].rearrange("p h c -> p (h c)"),
                                           ident[:])
                    ins.then_inc(xt_made, 1)

                flip(0, 0)
                pe.wait_ge(w_in, 16 * 3 * H)

                def unit(u, t, j, ahead):
                    q = j % 2
                    pe.wait_ge(zt_made, u + 1)
                    pe.wait_ge(wx_made, u + 1)
                    pe.matmul(po[q][:], weight[:], zt[q][:], start=True, stop=True).then_inc(o_made, 1)
                    if ahead:
                        flip(u + 1, 1 - q)

                quads(pe, unit)
                pe.wait_ge(end, 2 * H + 1)
                pe.matmul(pm[:, 0:2], average[:], moments[:], start=True, stop=True).then_inc(averaged, 1)
                pe.wait_ge(end, 2 * H + 5)
                pe.matmul(pm2[:, 0:1], average[:], var[:], start=True, stop=True).then_inc(averaged, 1)

            @block.scalar
            def _(act):
                act.sem_inc(wx_made, 2)

                def take(n, q):
                    act.wait_ge(xt_made, n + 1)
                    act.activation(zt[q][:], tp[q][:], ACT.Copy).then_inc(zt_made, 1)

                take(0, 0)

                def unit(u, t, j, ahead):
                    q = j % 2
                    act.wait_ge(o_made, u + 1)
                    act.activation(wx[:, :, bass.ds(u * R, R)].rearrange("p s i -> p i s"),
                                   po[q][:].rearrange("p (i s) -> p i s", i=R), ACT.Copy).then_inc(wx_made, 1)
                    if ahead:
                        take(u + 1, 1 - q)

                quads(act, unit)


def scan(nc, tag, v_t, wx, scale, shift, y_dram):
    STEPS = 64
    SH = P // STEPS
    CHUNKS = N * H * SH
    WARM = 16
    NY = 8
    LANES = SH * 2
    CLOSE = 2.0 ** -18
    with Scope(nc, tag) as m:
        vt = m.sb("vt", [P, P])
        ys = m.sb("ys", [P, 2, SH, NB, NY, BLK])
        start = m.sb("start", [P, SH, N])
        found = m.sb("found", [P, SH, N])
        ends = m.sb("ends", [P, SH, N])
        pre = m.sb("pre", [P, LANES, P])
        worst = m.sb("worst", [P, 1])
        ones_col = m.sb("ones_col", [P, 1])
        again = m.sb("again", [P, 1], I32)
        pl = [m.ps(f"lane{q}") for q in range(LANES)]
        pc = m.ps("count")
        v_in, zeroed, started, product, summed, y_made, ends_made, check, counted, again_made = (
            m.sem(n) for n in ("v_in", "zeroed", "started", "product", "summed", "y_made", "ends_made", "check",
                               "counted", "again_made"))
        seen = m.sem("seen")
        CHECKS = 5
        stored = [m.sem(f"stored{q}") for q in range(2)]
        SWEEP_STORES = STEPS // NY // 2

        def lane(q):
            return q // 2, q % 2

        def steps(eng, sweep, batch):
            if sweep is None:
                for buf in range(WARM // NY):
                    batch(buf * NY, STEPS - WARM + buf * NY, buf, None, buf)
            else:
                for b2 in range(STEPS // NY // 2):
                    for buf in range(2):
                        k0 = (b2 * 2 + buf) * NY
                        batch(sweep * STEPS + (WARM + k0), k0, buf, sweep * SWEEP_STORES + b2, b2 * 2 + buf)

        def sweeps(eng, run, sets_flag=False):
            run(0)
            eng.wait_ge(again_made, 1)
            flag = eng.value_load(again[0:1, 0:1], min_val=0, max_val=1)
            with eng.If(flag > 0):
                with eng.Fori(1, CHUNKS) as k:
                    eng.wait_ge(again_made, k)
                    eng.sem_inc(seen, 1)
                    more = eng.value_load(again[0:1, 0:1], min_val=0, max_val=1)
                    with eng.If(more > 0):
                        run(k)
                    if sets_flag:
                        with eng.If(more < 1):
                            eng.sem_inc(again_made, 1)

        with nc.Block() as block:

            @block.tensor
            def _(pe):
                pe.wait_ge(v_in, 16 * H)
                pe.wait_ge(zeroed, 4)

                def batch(base, k0, buf, stores, b):
                    for k in range(NY):
                        for q in range(LANES):
                            sh, ih = lane(q)
                            if k == 0 and b == 0:
                                state = start[:, sh, ih * P:(ih + 1) * P]
                            else:
                                from_buf, from_k = (buf, k - 1) if k else (1 - buf, NY - 1)
                                pe.wait_ge(y_made, (base + k - 1) * LANES + q + 1)
                                state = ys[:, from_buf, sh, ih * (NB // 2):(ih + 1) * (NB // 2), from_k, :]
                            pe.matmul(pl[q][:, 0:P], vt[:], state, start=True, stop=True).then_inc(product, 1)

                steps(pe, None, batch)

                def run(sweep):
                    pe.wait_ge(started, sweep + 1)
                    steps(pe, sweep, batch)
                    pe.wait_ge(check, (sweep + 1) * CHECKS)
                    pe.matmul(pc[0:1, 0:1], worst[:], ones_col[:], start=True, stop=True).then_inc(counted, 1)

                sweeps(pe, run)

            @block.vector
            def _(dve):
                dve.memset(vt[:], 0.0).then_inc(zeroed, 1)
                dve.memset(start[:], 0.0).then_inc(zeroed, 1)
                dve.memset(found[:], 0.0).then_inc(zeroed, 1)
                dve.memset(ones_col[:], 1.0).then_inc(zeroed, 1)

                def batch(base, k0, buf, stores, b):
                    for k in range(NY):
                        for q in range(LANES):
                            sh, ih = lane(q)
                            dve.wait_ge(product, (base + k) * LANES + q + 1)
                            dve.scalar_tensor_tensor(pre[:, q, :], wx[:, sh * STEPS + k0 + k, ih * P:(ih + 1) * P],
                                                     scale[:], pl[q][:, 0:P], ALU.mult, ALU.add).then_inc(summed, 1)

                def guesses(to, step):
                    dve.wait_ge(y_made, step * LANES)
                    for sh in range(SH):
                        dve.tensor_copy(ends[:, sh].rearrange("p (b i) -> p b i", i=BLK),
                                        ys[:, 1, sh, :, NY - 1, :]).then_inc(ends_made, 1)

                    return [lambda: dve.tensor_copy(to[:, 1, :], ends[:, 0, :]),
                            lambda: dve.tensor_copy(to[C:P, 0, :], ends[0:C, 1, :]),
                            lambda: dve.tensor_copy(to[0:C, 0, 1:N], ends[C:P, 1, 0:N - 1])]

                steps(dve, None, batch)
                dve.wait_ge(zeroed, 4)
                copies = guesses(start, WARM)
                dve.wait_ge(ends_made, SH)
                for copy in copies:
                    ins = copy()
                ins.then_inc(started, 1)

                def run(sweep):
                    steps(dve, sweep, batch)
                    copies = guesses(found, sweep * STEPS + (WARM + STEPS))
                    dve.wait_ge(ends_made, sweep * SH + 2 * SH)
                    for copy in copies:
                        ins = copy()
                    at = sweep * CHECKS
                    ins.then_inc(check, 1)
                    dve.wait_ge(check, at + 1)
                    dve.tensor_tensor(ends[:], found[:], start[:], ALU.subtract).then_inc(check, 1)
                    dve.wait_ge(check, at + 2)
                    dve.tensor_tensor(ends[:], ends[:], ends[:], ALU.mult).then_inc(check, 1)
                    dve.wait_ge(check, at + 3)
                    dve.tensor_reduce(worst[:], ends[:], AX.XY, ALU.max).then_inc(check, 1)
                    dve.wait_ge(check, at + 4)
                    dve.tensor_scalar(worst[:], worst[:], CLOSE * CLOSE, None, ALU.is_gt).then_inc(check, 1)
                    dve.tensor_copy(start[:], found[:]).then_inc(started, 1)
                    dve.wait_ge(counted, sweep + 1)
                    dve.tensor_scalar(again[0:1, :], pc[0:1, 0:1], 0.5, None, ALU.is_gt).then_inc(again_made, 1)

                sweeps(dve, run, sets_flag=True)

            @block.scalar
            def _(act):
                act.sem_inc(stored[0], 16 * SH)
                act.sem_inc(stored[1], 16 * SH)

                def batch(base, k0, buf, stores, b):
                    if stores is not None:
                        act.wait_ge(stored[buf], (stores + 1) * (16 * SH))
                    for k in range(NY):
                        for q in range(LANES):
                            sh, ih = lane(q)
                            act.wait_ge(summed, (base + k) * LANES + q + 1)
                            act.activation(ys[:, buf, sh, ih * (NB // 2):(ih + 1) * (NB // 2), k, :],
                                           pre[:, q, :].rearrange("p (b i) -> p b i", i=BLK), ACT.Sigmoid,
                                           bias=shift[:]).then_inc(y_made, 1)

                steps(act, None, batch)

                def run(sweep):
                    act.wait_ge(started, sweep + 1)
                    steps(act, sweep, batch)

                sweeps(act, run)

            @block.sync
            def _(sp):
                sp.wait_ge(zeroed, 1)
                for h in range(H):
                    sp.dma_start(vt[h * C:(h + 1) * C, h * C:(h + 1) * C], v_t).then_inc(v_in, 16)

                def batch(base, k0, buf, stores, b):
                    if stores is None:
                        return
                    sp.wait_ge(y_made, (base + NY) * LANES)
                    for sh in range(SH):
                        to = y_dram[:, :, sh * STEPS + k0:sh * STEPS + k0 + NY, :]
                        sp.dma_start(to.rearrange("p b s i -> p b (s i)"),
                                     ys[:, buf, sh].rearrange("p b s i -> p b (s i)")).then_inc(stored[buf], 16)

                def run(sweep):
                    steps(sp, sweep, batch)
                    for buf in range(2):
                        sp.wait_ge(stored[buf], (sweep + 1) * (SWEEP_STORES * 16 * SH) + 16 * SH)
                    sp.sem_inc(seen, 1)

                sweeps(sp, run)


def add_scan(nc, tag, x, y_dram, out, ident):
    GB = BLK // R
    with Scope(nc, tag) as m:
        yb = [m.sb(f"y{q}", [P, P, BLK]) for q in range(2)]
        xs = [m.sb(f"x{q}", [P, H, R, C]) for q in range(4)]
        tp = [m.ps(f"tp{q}") for q in range(2)]
        y_in = [m.sem(f"y_in{q}") for q in range(2)]
        x_in = [m.sem(f"x_in{q}") for q in range(4)]
        stored = [m.sem(f"stored{q}") for q in range(4)]
        flipped, added, y_used = m.sem("flipped"), m.sem("added"), m.sem("y_used")

        with nc.Block() as block:

            @block.sync
            def _(sp):
                with sp.Fori(0, G // 4) as t:
                    for j in range(4):
                        sp.wait_ge(stored[j], (t + 1) * 16)
                        sp.dma_start(xs[j][:], x[:, :, bass.ds((t * 4 + j) * R, R), :]).then_inc(x_in[j], 16)

            @block.gpsimd
            def _(pool):
                pool.sem_inc(y_used, 2)
                with pool.Fori(0, NB // 2) as b2:
                    for buf in range(2):
                        pool.wait_ge(y_used, b2 * 2 + buf + 1)
                        pool.dma_start(yb[buf][:], y_dram[:, bass.ds(b2 * 2 + buf, 1)]
                                      .rearrange("p b s i -> p (b s) i")).then_inc(y_in[buf], 16)

            @block.tensor
            def _(pe):
                with pe.Fori(0, NB // 2) as b2:
                    for buf in range(2):
                        pe.wait_ge(y_in[buf], (b2 + 1) * 16)
                        for g in range(GB):
                            n = (b2 * 2 + buf) * GB + g
                            pe.wait_ge(added, n + 1)
                            for i in range(R):
                                ins = pe.transpose(tp[g % 2][:, i * P:(i + 1) * P], yb[buf][:, :, g * R + i], ident[:])
                            ins.then_inc(flipped, 1)
                            if g == GB - 1:
                                pe.wait_ge(flipped, n + 1)
                                pe.sem_inc(y_used, 1)

            @block.vector
            def _(dve):
                dve.sem_inc(added, 2)
                with dve.Fori(0, G // 4) as t:
                    for j in range(4):
                        n = t * 4 + j
                        dve.wait_ge(x_in[j], (t + 1) * 16)
                        dve.wait_ge(flipped, n + 1)
                        at = xs[j][:].rearrange("p h i c -> p i h c")
                        dve.tensor_tensor(at, tp[j % 2][:].rearrange("p (i h c) -> p i h c", i=R, h=H), at,
                                          ALU.add).then_inc(added, 1)

            @block.scalar
            def _(act):
                for j in range(4):
                    act.sem_inc(stored[j], 16)
                with act.Fori(0, G // 4) as t:
                    for j in range(4):
                        n = t * 4 + j
                        act.wait_ge(added, n + 3)
                        act.dma_start(out[:, :, bass.ds(n * R, R), :], xs[j][:]).then_inc(stored[j], 16)
                for j in range(4):
                    act.wait_ge(stored[j], 16 * (G // 4 + 1))


def experts(nc, tag, x, router_w, router_b, expert_w, expert_b, out, ident, ones3, numbers):
    T = H * R
    TH = 4
    PAIRS = E // 2
    ROUNDS = (T // TH) * PAIRS
    FAR = 1e30
    F16 = mybir.dt.float16
    with Scope(nc, tag) as m:
        router = m.sb("router", [P, E])
        router3 = m.sb("router3", [P, E], BF16)
        router_rows = m.sb("router_rows", [P, E])
        part = m.sb("part", [P, 3, E], BF16)
        expert = m.sb("expert", [P, PAIRS, C])
        expert_bias = m.sb("expert_bias", [T * E, T, C])
        spread = m.sb("spread", [P, T, PAIRS, 2, C], F16)
        twice = m.sb("twice", [P, T * E])
        rank = m.sb("rank", [P, E])
        xs = [m.sb(f"x{q}", [P, H, R, C]) for q in range(4)]
        xn = m.sb("xn", [P, R, H, C])
        xt = [m.sb(f"xt{q}", [P, T, P]) for q in range(4)]
        xe = [m.sb(f"xe{q}", [P, TH, P]) for q in range(2)]
        find_variances, find_scales, rstd, known = layer_norm(m, T, PLAIN, numbers)
        logit = m.sb("logit", [P, T, E])
        first = m.sb("first", [P, T, E])
        second = m.sb("second", [P, T, E])
        work = m.sb("work", [P, T, E])
        top = m.sb("top", [P, 2, T])
        pick = m.sb("pick", [P, T])
        gap = m.sb("gap", [P, T])
        share = m.sb("share", [P, 2, T])
        shares = m.sb("shares", [P, 2, T * E])
        wt = [m.sb(f"wt{q}", [T * E, P]) for q in range(2)]
        wt16 = [m.sb(f"wt16{q}", [P, P], F16) for q in range(2)]
        whole16 = m.sb("whole16", [P, P], F16)
        outs = [m.sb(f"out{q}", [P, H, R, C]) for q in range(4)]
        tp = [m.ps(f"tp{q}") for q in range(2)]
        pl = m.ps("logits")
        pw = m.ps("turned")
        pb = [m.ps(f"spread{q}") for q in range(2)]
        po = [m.ps(f"po{q}") for q in range(2)]

        zeroed, loaded, made = (m.sem(n) for n in ("zeroed", "loaded", "made"))
        n_loads = 2 + 3 + E + T * E
        with nc.Block() as block:

            @block.sync
            def _(sp):
                sp.wait_ge(zeroed, 5)
                sp.dma_start(router[0:C, :], router_w).then_inc(loaded, 16)
                for q in range(3):
                    sp.dma_start(router_rows[32 * q:32 * q + 1, :], router_b.unsqueeze(0)).then_inc(loaded, 16)
                for e in range(E):
                    sp.dma_start(expert[(e % 2) * C:(e % 2 + 1) * C, e // 2, :], expert_w[e]).then_inc(loaded, 16)
                for t in range(T):
                    sp.dma_start(expert_bias[t * E:(t + 1) * E, t, :], expert_b).then_inc(loaded, 16)

            @block.vector
            def _(dve):
                for t in (router, router_rows, expert_bias, router3):
                    dve.memset(t[:], 0.0).then_inc(zeroed, 1)
                for e in range(E):
                    ins = dve.memset(rank[:, e:e + 1], float(E - e))
                ins.then_inc(zeroed, 1)
                dve.tensor_tensor(twice[:], ident[:, 0:C], ident[:, C:2 * C], ALU.add).then_inc(made, 1)
                dve.wait_ge(made, 1)
                dve.tensor_copy(spread[:].rearrange("p t a b c -> p (t a b) c"), over(twice[:], C)).then_inc(made, 1)
                dve.wait_ge(loaded, 16 * (1 + 3 + E + T))
                at = 2
                for q in range(3):
                    dve.tensor_copy(part[:, q, :], router_rows[:]).then_inc(made, 1)
                    at += 1
                    dve.wait_ge(made, at)
                    if q < 2:
                        dve.tensor_tensor(router_rows[:], router_rows[:], part[:, q, :], ALU.subtract).then_inc(made, 1)
                        at += 1
                        dve.wait_ge(made, at)
                for q in range(3):
                    ins = dve.tensor_copy(router3[32 * q:32 * q + 32, :], part[32 * q:32 * q + 32, q, :])
                ins.then_inc(made, 1)

        center_weights(nc, tag + "c", [router[:], expert[:].rearrange("p a c -> p (a c)")], ident, po)

        x_in = [m.sem(f"x_in{q}") for q in range(4)]
        xn_made, xt_made, xt_copied, l_made = m.sem("xn_made"), m.sem("xt_made"), m.sem("xt_copied"), m.sem("l_made")
        gap_made, share_made, w_made, w_turned, w_copied, w_split, spread_made, xe_made, o_made, out_made, route = (
            m.sem(n) for n in ("gap_made", "share_made", "w_made", "w_turned", "w_copied", "w_split", "spread_made",
                               "xe_made", "o_made", "out_made", "route"))
        stored = [m.sem(f"stored{q}") for q in range(4)]
        xe_used = m.sem("xe_used")
        ROUTE_STEPS = 14

        with nc.Block() as block:

            @block.sync
            def _(sp):
                sp.sem_inc(out_made, 4)
                with sp.Fori(0, G // 4) as t:
                    for j in range(4):
                        n = t * 4 + j
                        sp.wait_ge(out_made, n + 1)
                        sp.dma_start(xs[j][:], x[:, :, bass.ds(n * R, R), :]).then_inc(x_in[j], 16)

            @block.vector
            def _(dve):
                def measure(n, t, j):
                    dve.wait_ge(x_in[j], 16 * (t + 1))
                    find_variances(dve, n, j % 2, [xs[j][:, h, i, :] for h in range(H) for i in range(R)])

                def choose(n, part):
                    base = n * ROUTE_STEPS

                    def after(step):
                        dve.wait_ge(route, base + step)

                    def candidates(largest):
                        return dve.tensor_tensor(work[:], logit[:], over(largest, E), ALU.is_ge)

                    def rank_them():
                        return dve.tensor_tensor(work[:], work[:], rank[:].unsqueeze(1).to_broadcast([P, T, E]),
                                                 ALU.mult)

                    if part == 0:
                        dve.wait_ge(l_made, n + 1)
                        dve.tensor_copy(logit[:].rearrange("p t e -> p (t e)"), pl[:, 0:T * E]).then_inc(route, 1)
                        after(1)
                        dve.tensor_reduce(top[:, 0, :], logit[:], AX.X, ALU.max).then_inc(route, 1)
                    if part == 1:
                        after(2)
                        candidates(top[:, 0, :]).then_inc(route, 1)
                        after(3)
                        rank_them().then_inc(route, 1)
                        after(4)
                        dve.tensor_reduce(pick[:], work[:], AX.X, ALU.max).then_inc(route, 1)
                    if part == 2:
                        after(5)
                        dve.tensor_tensor(first[:], work[:], over(pick[:], E), ALU.is_ge).then_inc(route, 1)
                        after(6)
                        dve.scalar_tensor_tensor(logit[:], first[:], -FAR, logit[:], ALU.mult, ALU.add
                                                 ).then_inc(route, 1)
                        after(7)
                        dve.tensor_reduce(top[:, 1, :], logit[:], AX.X, ALU.max).then_inc(route, 1)
                    if part == 3:
                        after(8)
                        dve.tensor_tensor(gap[:], top[:, 1, :], top[:, 0, :], ALU.subtract).then_inc(gap_made, 1)
                        candidates(top[:, 1, :]).then_inc(route, 1)
                        after(9)
                        rank_them().then_inc(route, 1)
                    if part == 4:
                        after(10)
                        dve.tensor_reduce(pick[:], work[:], AX.X, ALU.max).then_inc(route, 1)
                        after(11)
                        dve.tensor_tensor(second[:], work[:], over(pick[:], E), ALU.is_ge).then_inc(route, 1)
                    if part == 5:
                        after(12)
                        dve.wait_ge(share_made, n + 1)
                        dve.tensor_tensor(first[:], first[:], over(share[:, 0, :], E), ALU.mult).then_inc(route, 1)
                        dve.tensor_tensor(second[:], second[:], over(share[:, 1, :], E), ALU.mult).then_inc(route, 1)
                        after(14)
                        dve.tensor_tensor(shares[:], twofold(first), twofold(second), ALU.add).then_inc(w_made, 1)

                def twofold(t):
                    return t[:].rearrange("p t e -> p (t e)").unsqueeze(1).to_broadcast([P, 2, T * E])

                def split(n, q):
                    dve.wait_ge(w_turned, n + 1)
                    dve.tensor_copy(wt[q][:], pw[0:T * E, 0:P])
                    dve.tensor_copy(whole16[:], pw[:, 0:P]).then_inc(w_split, 1)
                    dve.wait_ge(w_split, n * 2 + 1)
                    dve.tensor_copy(wt16[q][0:C, :], whole16[0:C, :])
                    dve.tensor_tensor(wt16[q][C:P, :], pw[C:P, 0:P], whole16[C:P, :], ALU.subtract
                                      ).then_inc(w_split, 1)

                def scale_inputs(u, j, k):
                    dve.wait_ge(spread_made, u * ROUNDS + k + 1)
                    dve.wait_ge(xe_used, u * ROUNDS + k + 1)
                    dve.tensor_tensor(xe[k % 2][:].rearrange("p t s -> p (t s)"), pb[k % 2][:],
                                      xt[j][:, (k // PAIRS) * TH:(k // PAIRS + 1) * TH, :]
                                      .rearrange("p t s -> p (t s)"), ALU.mult).then_inc(xe_made, 1)

                def finish(n, t, j):
                    dve.wait_ge(o_made, n + 1)
                    dve.wait_ge(stored[j], (t + 1) * 16)
                    dve.tensor_tensor(outs[j][:].rearrange("p h i c -> p (h i c)"), po[j % 2][:],
                                      xs[j][:].rearrange("p h i c -> p (h i c)"), ALU.add).then_inc(out_made, 1)

                dve.sem_inc(xe_made, 2)
                measure(0, 0, 0)
                measure(1, 0, 1)
                for part in range(6):
                    choose(0, part)
                split(0, 0)
                measure(2, 0, 2)

                def unit(u, t, j, ahead, behind):
                    for k in range(ROUNDS):
                        scale_inputs(u, j, k)
                        if k == 1 and behind:
                            finish(u - 1, t - 1 if j == 0 else t, (j + 3) % 4)
                        if k < 6 and ahead:
                            choose(u + 1, k)
                        if k == 5 and ahead > 2:
                            measure(u + 3, t + (j + 3) // 4, (j + 3) % 4)
                        if k == 6 and ahead:
                            split(u + 1, (j + 1) % 2)

                quads_peeled(dve, unit)
                finish(G - 1, G // 4 - 1, 3)

            @block.gpsimd
            def _(pool):
                def rescale(n, j):
                    find_scales(pool, n, j % 2)
                    pool.wait_ge(known, n + 1)
                    pool.wait_ge(xt_made, n + 1)
                    pool.tensor_tensor(xn[:].rearrange("p i h c -> p h i c"), xs[j][:],
                                       over(rstd[j % 2][:].rearrange("p (h i) -> p h i", h=H), C),
                                       ALU.mult).then_inc(xn_made, 1)

                rescale(0, 0)
                rescale(1, 1)

                def unit(u, t, j, ahead):
                    if ahead > 1:
                        rescale(u + 2, (j + 2) % 4)

                quads(pool, unit)

            @block.scalar
            def _(act):
                for j in range(4):
                    act.sem_inc(stored[j], 16)

                def take(n, j):
                    act.wait_ge(xt_made, n + 2)
                    for b in range(2):
                        for h in range(H):
                            ins = act.activation(xt[j][b * C:(b + 1) * C, h * R:(h + 1) * R, :]
                                                 .rearrange("p t s -> p (t s)"), tp[j % 2][h * C:(h + 1) * C, :],
                                                 ACT.Copy)
                    ins.then_inc(xt_copied, 1)

                def weigh(n):
                    act.wait_ge(gap_made, n + 1)
                    act.activation(share[:, 0, :], gap[:], ACT.Sigmoid, scale=-1.0)
                    act.activation(share[:, 1, :], gap[:], ACT.Sigmoid).then_inc(share_made, 1)

                def store(n, j):
                    act.wait_ge(out_made, n + 5)
                    act.dma_start(out[:, :, bass.ds(n * R, R), :], outs[j][:]).then_inc(stored[j], 16)

                take(0, 0)
                weigh(0)
                take(1, 1)

                def unit(u, t, j, ahead, behind):
                    if behind:
                        store(u - 1, (j + 3) % 4)
                    if ahead > 1:
                        take(u + 2, (j + 2) % 4)
                    if ahead:
                        weigh(u + 1)

                quads_peeled(act, unit)
                store(G - 1, 3)
                for j in range(4):
                    act.wait_ge(stored[j], 16 * (G // 4 + 1))

            @block.tensor
            def _(pe):
                pe.sem_inc(xt_made, 1)
                pe.sem_inc(xe_used, 2)

                def flip(n, j):
                    pe.wait_ge(xn_made, n + 1)
                    for i in range(R):
                        ins = pe.transpose(tp[j % 2][:, i * P:(i + 1) * P], xn[:, i].rearrange("p h c -> p (h c)"),
                                           ident[:])
                    ins.then_inc(xt_made, 1)

                def rate(n, j):
                    pe.matmul(pl[:, 0:T * E], ones3[:], router3[:].unsqueeze(1).to_broadcast([P, T, E]),
                              start=True, stop=True)
                    pe.wait_ge(xt_copied, n + 1)
                    for t in range(T):
                        ins = pe.matmul(pl[:, t * E:(t + 1) * E], xt[j][:, t, :], router[:], start=False, stop=True,
                                        skip_group_check=True)
                    ins.then_inc(l_made, 1)

                def turn_shares(n):
                    pe.wait_ge(w_made, n + 1)
                    pe.transpose(pw[:, 0:P], shares[:].rearrange("p b t -> p (b t)"), ident[:]).then_inc(w_turned, 1)

                def spread_out(u, q, k):
                    if k == 0:
                        pe.wait_ge(w_split, u * 2 + 2)
                    pe.wait_ge(xe_made, u * ROUNDS + k + 1)
                    for j in range(TH):
                        ins = pe.matmul(pb[k % 2][:, j * P:(j + 1) * P],
                                        spread[:, (k // PAIRS) * TH + j, k % PAIRS].rearrange("p b c -> p (b c)"),
                                        wt16[q][:], start=True, stop=True)
                    ins.then_inc(spread_made, 1)

                def add_experts(u, q, k):
                    pe.wait_ge(xe_made, u * ROUNDS + k + 3)
                    for j in range(TH):
                        t = (k // PAIRS) * TH + j
                        ins = pe.matmul(po[q][:, t * C:(t + 1) * C], xe[k % 2][:, j, :], expert[:, k % PAIRS, :],
                                        start=False, stop=True, skip_group_check=True)
                    ins.then_inc(xe_used, 1)
                    if k == ROUNDS - 1:
                        pe.wait_ge(xe_used, (u + 1) * ROUNDS + 2)
                        pe.sem_inc(o_made, 1)

                flip(0, 0)
                rate(0, 0)
                turn_shares(0)
                flip(1, 1)
                rate(1, 1)
                spread_out(0, 0, 0)

                def unit(u, t, j, ahead):
                    q = j % 2
                    pe.wait_ge(out_made, u + 3)
                    pe.matmul(po[q][:], wt[q][:], expert_bias[:].rearrange("k t c -> k (t c)"), start=True, stop=True)
                    for k in range(ROUNDS):
                        if k + 1 < ROUNDS:
                            spread_out(u, q, k + 1)
                        elif ahead:
                            spread_out(u + 1, 1 - q, 0)
                        if k == 2 and ahead > 1:
                            flip(u + 2, (j + 2) % 4)
                        if k == 4 and ahead > 1:
                            rate(u + 2, (j + 2) % 4)
                        if k == 6 and ahead:
                            turn_shares(u + 1)
                        add_experts(u, q, k)

                quads(pe, unit)


CONV = ["ln_in_w", "ln_in_b", "w_ap", "b_ap", "w_ag", "b_ag", "w_bp", "b_bp", "w_bg", "b_bg", "ln_out_w",
        "ln_out_b", "w_z", "b_z", "w_g", "b_g"]


def build(nc, a, out):
    def scratch(name, shape):
        return nc.dram_tensor(name, shape, F32, kind="Internal").ap()

    b_dram = scratch("b_scratch", [H, C // CH, P, H, RB, BLK, CH])
    gate_dram = scratch("gate_scratch", [P, H, N, C])
    t0 = scratch("after_conv0", [P, H, N, C])
    y_dram = scratch("scan_scratch", [P, NB, P, BLK])
    t1 = scratch("after_scan", [P, H, N, C])
    t2 = scratch("after_conv1", [P, H, N, C])

    with ExitStack() as s:
        ident = s.enter_context(nc.sbuf_tensor("ident", [P, P], F32))
        ones3 = s.enter_context(nc.sbuf_tensor("ones3", [P, P], BF16))
        numbers = s.enter_context(nc.sbuf_tensor("numbers", [P, 1], F32))
        constants(nc, ident, ones3, numbers)
        for layer, (x, y) in enumerate([(a["x"], t0), (t1, t2)]):
            w = {k: a[f"L{layer}_conv_{k}"] for k in CONV}
            with nc.sbuf_tensor(f"a_res{layer}", [P, H, C, N], F32) as a_res:
                conv_project(nc, f"cp{layer}", x, a[f"L{layer}_conv_mask"], w, a_res, b_dram, gate_dram, ident,
                             ones3, numbers)
                conv_combine(nc, f"cc{layer}", x, w, a_res, b_dram, gate_dram, y, ident, ones3, numbers)
            if layer == 0:
                with nc.sbuf_tensor("wx", [P, P, N], F32) as wx, nc.sbuf_tensor("bn_scale", [P, 1], F32) as scale, \
                        nc.sbuf_tensor("bn_shift", [P, 1], F32) as shift:
                    scan_input(nc, "si", t0, a["L0_ffn_W_t"], a["L0_ffn_gamma"], a["L0_ffn_beta"], wx, scale, shift,
                               ident, numbers)
                    scan(nc, "sc", a["L0_ffn_V_t"], wx, scale, shift, y_dram)
                add_scan(nc, "as", t0, y_dram, t1, ident)
        experts(nc, "ex", t2, a["L1_ffn_router_w"], a["L1_ffn_router_b"], a["L1_ffn_expert_w"],
                a["L1_ffn_expert_b"], out, ident, ones3, numbers)


def kernel(**inputs):
    import concourse.bacc as bacc
    from concourse.bass_utils import run_bass_kernel_spmd

    arrays = {}
    for name, value in inputs.items():
        v = np.asarray(value)
        if name == "x":
            v = v.reshape(N, H, P, C).transpose(2, 1, 0, 3)
        elif name.endswith("_mask"):
            v = v.reshape(N, H, P).transpose(2, 1, 0)
        elif name in ("L0_ffn_W", "L0_ffn_V"):
            name, v = name + "_t", v.T
        arrays[name] = np.ascontiguousarray(v)
    nc = bacc.Bacc("TRN2", target_bir_lowering=False, num_devices=1)
    aps = {k: nc.dram_tensor("in_" + k, v.shape, mybir.dt.from_np(v.dtype), kind="ExternalInput").ap()
           for k, v in arrays.items()}
    out = nc.dram_tensor("out_0", (P, H, N, C), F32, kind="ExternalOutput").ap()
    build(nc, aps, out)
    r = run_bass_kernel_spmd(nc, [{"in_" + k: v for k, v in arrays.items()}], core_ids=[0])
    return r.results[0]["out_0"].transpose(2, 1, 0, 3).reshape(1, N, N, C)
```

```python
from contextlib import ExitStack

import numpy as np
import concourse.bass as bass
from concourse import mybir

F32 = mybir.dt.float32
BF16 = mybir.dt.bfloat16
I32 = mybir.dt.int32
ALU = mybir.AluOpType
ACT = mybir.ActivationFunctionType
AX = mybir.AxisListType

P = 128
N = 256
C = 64
H = 2
R = 4
G = N // R
BLK = 32
NB = N // BLK
RB = NB // H
CH = 2
YROWS = 2 * R
YB = N // YROWS
E = 8


class Scope(ExitStack):

    def __init__(self, nc, tag):
        super().__init__()
        self.nc, self.tag, self.sems = nc, tag, []

    def sb(self, name, shape, dt=F32):
        return self.enter_context(self.nc.sbuf_tensor(f"{self.tag}_{name}", shape, dt))

    def ps(self, name, shape=(P, 512), dt=F32):
        return self.enter_context(self.nc.psum_tensor(f"{self.tag}_{name}", list(shape), dt))

    def sem(self, name):
        self.sems.append(self.nc.alloc_semaphore(f"{self.tag}_{name}"))
        return self.sems[-1]

    def __exit__(self, *raised):
        if self.sems and raised[0] is None:
            self.nc.clear_and_free_semaphores(self.sems)
            self.nc.all_engine_barrier()
        return super().__exit__(*raised)


def over(ap, n):
    return ap.unsqueeze(len(ap.shape)).to_broadcast(list(ap.shape) + [n])


def constants(nc, ident, ones3, numbers):
    with Scope(nc, "cst") as m:
        made, rows_made = m.sem("made"), m.sem("rows_made")
        with nc.Block() as block:

            @block.vector
            def _(dve):
                dve.memset(ones3[:], 0.0).then_inc(rows_made, 1)
                dve.wait_ge(rows_made, 1)
                for q in range(3):
                    dve.memset(ones3[32 * q:32 * q + 1, :], 1.0).then_inc(rows_made, 1)

            @block.gpsimd
            def _(pool):
                pool.memset(ident[:], 0.0).then_inc(made, 1)
                pool.memset(numbers[:, 0:1], -0.5).then_inc(made, 1)
                pool.memset(numbers[:, 1:2], 1.0).then_inc(made, 1)
                pool.wait_ge(made, 3)
                pool.affine_select(out=ident[:], in_=ident[:], compare_op=ALU.not_equal, fill=1.0, base=0,
                                   pattern=[[-1, P]], channel_multiplier=1).then_inc(made, 1)



def center_weights(nc, tag, weights, ident, banks, biases=None):
    with Scope(nc, tag) as m:
        center = m.sb("center", [P, P])
        deal = m.sb("deal", [P, P]) if biases else None
        pc = banks
        step, centered = m.sem("step"), m.sem("centered")
        cuts = [(w, bias, at, min(at + 512, w.shape[1])) for w, bias in zip(weights, biases or weights)
                for at in range(0, w.shape[1], 512)]
        with nc.Block() as block:

            @block.vector
            def _(dve):
                if biases:
                    dve.memset(deal[:], 0.0)
                dve.memset(center[:], 0.0).then_inc(step, 1)
                dve.wait_ge(step, 1)
                for h in range(H):
                    if biases:
                        dve.memset(deal[32 * h:32 * h + 1, h * C:(h + 1) * C], 1.0 / C)
                    ins = dve.memset(center[h * C:(h + 1) * C, h * C:(h + 1) * C], -1.0 / C)
                ins.then_inc(step, 1)
                dve.wait_ge(step, 2)
                dve.tensor_tensor(center[:], center[:], ident[:], ALU.add).then_inc(step, 1)
                for n, (w, bias, a, b) in enumerate(cuts):
                    dve.wait_ge(centered, n + 1)
                    dve.tensor_copy(w[:, a:b], pc[n % 2][:, 0:b - a]).then_inc(step, 1)

            @block.tensor
            def _(pe):
                for n, (w, bias, a, b) in enumerate(cuts):
                    pe.wait_ge(step, 3 + max(n - 1, 0))
                    ins = pe.matmul(pc[n % 2][:, 0:b - a], center[:], w[:, a:b], start=True, stop=not biases)
                    if biases:
                        ins = pe.matmul(pc[n % 2][:, 0:b - a], deal[:], bias[:, a:b], start=False, stop=True)
                    ins.then_inc(centered, 1)


def prepare_weights(nc, tag, weight, bias3, blocks, gain, offset, ident):
    width = len(blocks) * H * C
    with Scope(nc, tag) as m:
        gain_col = m.sb("gain_col", [P, 1])
        offset_col = m.sb("offset_col", [P, 1])
        offset_rows = m.sb("offset_rows", [P, P])
        bias_rows = m.sb("bias_rows", [P, width])
        part = [m.sb(f"part{q}", [P, width], BF16) for q in range(3 if bias3 is not None else 0)]
        folded = [m.ps(f"folded{q}") for q in range(2)]
        zeroed, loaded, rows, summed, step = (m.sem(n) for n in ("zeroed", "loaded", "rows", "summed", "step"))
        n_loads = len(blocks) * (H + 1) + 2 * H
        cuts = [(at, min(at + 512, width)) for at in range(0, width, 512)]
        with nc.Block() as block:

            @block.sync
            def _(sp):
                sp.wait_ge(zeroed, 3)
                for k, (matrix, bias) in enumerate(blocks):
                    for h in range(H):
                        at = (k * H + h) * C
                        sp.dma_start(weight[h * C:(h + 1) * C, at:at + C], matrix).then_inc(loaded, 16)
                    at = k * H * C
                    sp.dma_start(bias_rows[0:65:32, at:at + H * C].rearrange("q (h c) -> q h c", h=H),
                                 bias.unsqueeze(0).unsqueeze(0).to_broadcast([3, H, C])).then_inc(loaded, 16)
                for h in range(H):
                    sp.dma_start(gain_col[h * C:(h + 1) * C, :], gain.unsqueeze(1)).then_inc(loaded, 16)
                    sp.dma_start(offset_col[h * C:(h + 1) * C, :], offset.unsqueeze(1)).then_inc(loaded, 16)

            @block.tensor
            def _(pe):
                pe.wait_ge(rows, 1)
                for q, (a, b) in enumerate(cuts):
                    pe.matmul(folded[q][:, 0:b - a], offset_rows[:], weight[:, a:b],
                              start=True, stop=True).then_inc(summed, 1)

            @block.vector
            def _(dve):
                dve.memset(weight[:], 0.0).then_inc(zeroed, 1)
                dve.memset(bias_rows[:], 0.0).then_inc(zeroed, 1)
                dve.memset(offset_rows[:], 0.0).then_inc(zeroed, 1)
                if bias3 is not None:
                    dve.memset(bias3[:], 0.0).then_inc(step, 1)
                dve.wait_ge(loaded, 16 * n_loads)
                dve.wait_ge(zeroed, 3)
                for q in range(3):
                    ins = dve.tensor_copy(offset_rows[:, 32 * q:32 * q + 1], offset_col[:])
                ins.then_inc(rows, 1)
                dve.wait_ge(summed, len(cuts))
                for q, (a, b) in enumerate(cuts):
                    ins = dve.tensor_tensor(bias_rows[:, a:b], bias_rows[:, a:b], folded[q][:, 0:b - a], ALU.add)
                ins.then_inc(step, 1)
                dve.tensor_scalar(weight[:], weight[:], gain_col[:], None, ALU.mult).then_inc(step, 1)
                if bias3 is None:
                    dve.wait_ge(step, 2)
                    columns = bias_rows[:].rearrange("p (k h c) -> p k h c", h=H, c=C)
                    for h in range(H):
                        dve.memset(columns[32 * h:32 * h + 1, :, 1 - h, :], 0.0)
                    return
                at = 3
                dve.wait_ge(step, at)
                for q in range(3):
                    dve.tensor_copy(part[q][:], bias_rows[:]).then_inc(step, 1)
                    at += 1
                    dve.wait_ge(step, at)
                    if q < 2:
                        dve.tensor_tensor(bias_rows[:], bias_rows[:], part[q][:], ALU.subtract).then_inc(step, 1)
                        at += 1
                        dve.wait_ge(step, at)
                cols = bias3.shape[1]
                for q in range(3):
                    ins = dve.tensor_copy(bias3[32 * q:32 * q + 32, :], part[q][32 * q:32 * q + 32, 0:cols])
                ins.then_inc(step, 1)
        center_weights(nc, tag + "c", [weight[:]], ident, folded,
                       [bias_rows[:]] if bias3 is None else None)


PLAIN = (1.0, 1e-5)
DOUBLE = (1.0 + 1e-5, 1e-11)
MEASURES = 2


def layer_norm(m, tiles, kind, numbers, shifts=None):
    stats = m.sb("ln_stats", [P, tiles, 6])
    moments = m.sb("ln_moments", [P, tiles, 2])
    var = [m.sb(f"ln_var{q}", [P, tiles]) for q in range(2)]
    rstd = [m.sb(f"ln_rstd{q}", [P, tiles]) for q in range(2)]
    mean = [m.sb(f"ln_mean{q}", [P, tiles]) for q in range(2)] if shifts else None
    counted, var_made, known, seen, scaled = (
        m.sem(n) for n in ("ln_counted", "ln_var_made", "ln_known", "ln_seen", "ln_scaled"))

    def take_stats(dve, tokens, first):
        for k, tile in enumerate(tokens):
            ins = dve.bn_stats(stats[:, first + k, :], tile)
        if first + len(tokens) == tiles:
            ins.then_inc(counted, 1)

    def finish_variances(dve, n, q):
        dve.wait_ge(counted, n * MEASURES + 1)
        dve.sem_inc(seen, 1)
        for k in range(tiles):
            ins = dve.bn_aggr(moments[:, k, :], stats[:, k, :])
        ins.then_inc(counted, 1)
        dve.wait_ge(counted, n * MEASURES + 2)
        if shifts:
            dve.tensor_copy(mean[q][:], moments[:, :, 0])
        dve.tensor_scalar(var[q][:], moments[:, :, 1], *kind, ALU.mult, ALU.add).then_inc(var_made, 1)

    def find_scales(pool, n, q):
        pool.wait_ge(var_made, n + 1)
        pool.tensor_tensor(rstd[q][:], var[q][:], numbers[:, 0:1].to_broadcast([P, tiles]), ALU.pow
                           ).then_inc(scaled if shifts else known, 1)
        if shifts:
            pool.wait_ge(scaled, n + 1)
            pool.tensor_tensor(shifts[q][:], mean[q][:], rstd[q][:], ALU.mult).then_inc(known, 1)

    return take_stats, finish_variances, find_scales, rstd, known


def quads(eng, unit):
    with eng.Fori(0, G // 4 - 1) as t:
        for j in range(4):
            unit(t * 4 + j, t, j, 3)
    for j in range(4):
        unit(G - 4 + j, G // 4 - 1, j, 3 - j)


def quads_peeled(eng, unit):
    for j in range(4):
        unit(j, 0, j, 3, j > 0)
    with eng.Fori(1, G // 4 - 1) as t:
        for j in range(4):
            unit(t * 4 + j, t, j, 3, True)
    for j in range(4):
        unit(G - 4 + j, G // 4 - 1, j, 3 - j, True)


def conv_project(nc, tag, x, mask, w, a_res, b_dram, gate_dram, ident, numbers, parts=None):
    W_COLS = 10 * C
    PER = BLK // R
    PIECE = C // CH // PER
    B_STORED = 16 * H * PER
    with Scope(nc, tag) as m:
        weight = m.sb("weight", [P, W_COLS])
        prepare_weights(nc, tag + "p", weight, None,
                        [(w["w_ag"], w["b_ag"]), (w["w_bg"], w["b_bg"]), (w["w_ap"], w["b_ap"]),
                         (w["w_bp"], w["b_bp"]), (w["w_g"], w["b_g"])], w["ln_in_w"], w["ln_in_b"],
                        ident)

        mask_sb = m.sb("mask", [P, H, N])
        b_stage = m.sb("b_stage", [P, 2, H, C // CH, BLK, CH])
        xs = [m.sb(f"x{q}", [P, H, R, C]) for q in range(4)]
        xn = [m.sb(f"xn{q}", [P, R, H, C]) for q in range(2)]
        zt = [m.sb(f"zt{q}", [P, R * P]) for q in range(2)]
        sig = m.sb("sig", [P, R, 4 * C])
        prod = m.sb("prod", [P, R, 2, H, C])
        gs = [m.sb(f"gs{q}", [P, H, R, C]) for q in range(2)]
        shifts = [m.sb(f"shift{q}", [P, H * R]) for q in range(2)]
        take_stats, finish_variances, find_scales, rstd, known = layer_norm(
            m, H * R, DOUBLE, numbers, shifts)
        tp = [m.ps(f"tp{q}") for q in range(2)]
        ty = tp[1]
        yb = [m.sb(f"y{q}", [P, P, YROWS]) for q in range(2)] if parts else None
        pg = [m.ps(f"pg{q}") for q in range(2)]
        pv = [m.ps(f"pv{i}") for i in range(R)]

        mask_in, xn_scaled = m.sem("mask_in"), m.sem("xn_scaled")
        y_in = [m.sem(f"y_in{q}") for q in range(2)]
        y_turned, summed, seen = m.sem("y_turned"), m.sem("summed"), m.sem("seen")
        sum_stored = [m.sem(f"sum_stored{q}") for q in range(4)]
        x_in = [m.sem(f"x_in{q}") for q in range(4)]
        xn_made, xt_made, zt_made = m.sem("xn_made"), m.sem("xt_made"), m.sem("zt_made")
        v_made, sig_made, prod_made, g_made, gs_made = (
            m.sem(n) for n in ("v_made", "sig_made", "prod_made", "g_made", "gs_made"))
        gs_stored = [m.sem(f"gs_stored{q}") for q in range(2)]
        a_made, b_made = m.sem("a_made"), m.sem("b_made")
        b_stored = [m.sem(f"b_stored{q}") for q in range(2)]

        with nc.Block() as block:

            @block.sync
            def _(sp):
                sp.dma_start(mask_sb[:], mask).then_inc(mask_in, 16)
                sp.sem_inc(xn_made, 4)
                for buf in range(2):
                    sp.sem_inc(b_stored[buf], B_STORED)

                source = parts[0] if parts else x
                if parts:
                    sp.sem_inc(y_turned, 4)
                    for j in range(4):
                        sp.sem_inc(sum_stored[j], 16)

                def load(n, j, t):
                    sp.wait_ge(xn_made, n + 1)
                    if parts:
                        sp.sem_inc(seen, 1)
                        sp.wait_ge(sum_stored[j], (t + 1) * 16)
                        sp.sem_inc(seen, 1)
                        if j % 2 == 0:
                            sp.wait_ge(y_turned, n + 2)
                            sp.sem_inc(seen, 1)
                            sp.dma_start(yb[j // 2][:], parts[1][:, bass.ds(t * 2 + j // 2, 1)]
                                         .rearrange("p b s i -> p (b s) i")).then_inc(y_in[j // 2], 16)
                    sp.dma_start(xs[j][:], source[:, :, bass.ds(n * R, R), :]).then_inc(x_in[j], 16)

                def store_b(blk, piece):
                    chunks = bass.ds(piece * PIECE, PIECE)
                    for k in range(H):
                        sp.dma_start(b_dram[blk // RB, chunks, :, k, blk % RB].rearrange("n p i c -> p n (i c)"),
                                     b_stage[:, blk % 2, k, chunks].rearrange("p n i c -> p n (i c)")
                                     ).then_inc(b_stored[blk % 2], 16)

                AHEAD = 3
                for n in range(AHEAD):
                    load(n, n, 0)
                for blk in range(NB):
                    last = blk == NB - 1
                    with sp.Fori(0, PER // 4 - 1 if last else PER // 4) as t:
                        for j in range(4):
                            load(blk * PER + t * 4 + j + AHEAD, (j + AHEAD) % 4,
                                 blk * (PER // 4) + t + (j + AHEAD) // 4)
                            if blk > 0:
                                sp.wait_ge(b_made, blk * PER + 1)
                                store_b(blk - 1, t * 4 + j)
                    if last:
                        load(G - 1, 3, G // 4 - 1)
                        for piece in range(PER - 4, PER):
                            store_b(blk - 1, piece)
                        sp.wait_ge(b_made, G + 1)
                        with sp.Fori(0, PER) as piece:
                            store_b(blk, piece)
                for buf in range(2):
                    sp.wait_ge(b_stored[buf], B_STORED * (NB // 2 + 1))

            @block.vector
            def _(dve):
                dve.sem_inc(prod_made, R)
                dve.sem_inc(a_made, 1)
                dve.sem_inc(b_made, 1)

                def measure(n, t, j):
                    dve.wait_ge(x_in[j], 16 * (t + 1))
                    if parts:
                        dve.wait_ge(summed, n + 1)
                    take_stats(dve, [xs[j][:, h, i, :] for i in range(R) for h in range(H)], 0)

                def rescale(n, j):
                    dve.wait_ge(known, n + 1)
                    dve.tensor_tensor(xn[j % 2][:], xs[j][:].rearrange("p h i c -> p i h c"),
                                      over(rstd[j % 2][:].rearrange("p (i h) -> p i h", h=H), C),
                                      ALU.mult).then_inc(xn_scaled, 1)

                def shift(n, j):
                    tiles = xn[j % 2][:].rearrange("p i h c -> p (i h) c")
                    dve.wait_ge(xn_scaled, n + 1)
                    dve.scalar_tensor_tensor(tiles, tiles, 1.0, over(shifts[j % 2][:], C), ALU.add, ALU.subtract
                                             ).then_inc(xn_made, 1)

                def product(u, i):
                    dve.wait_ge(sig_made, u * R + i + 1)
                    dve.tensor_tensor(prod[:, i].rearrange("p a h c -> p (a h c)"), pv[i][:, 4 * C:8 * C],
                                      sig[:, i, :], ALU.mult).then_inc(prod_made, 1)

                def add_y(n, t, j):
                    if parts:
                        dve.wait_ge(x_in[j], 16 * (t + 1))
                        dve.wait_ge(y_turned, n + 5)
                        to = xs[j][:].rearrange("p h i c -> p i h c")
                        dve.tensor_tensor(to, ty[:].rearrange("p (i h c) -> p i h c", i=R, h=H), to, ALU.add
                                          ).then_inc(summed, 1)

                for n in range(3):
                    if n == 2:
                        rescale(0, 0)
                        shift(0, 0)
                    add_y(n, 0, n)
                    measure(n, 0, n)
                    finish_variances(dve, n, n % 2)

                def unit(u, t, j, ahead):
                    if ahead:
                        rescale(u + 1, (j + 1) % 4)
                    if ahead > 2:
                        add_y(u + 3, t + (j + 3) // 4, (j + 3) % 4)
                    if ahead:
                        shift(u + 1, (j + 1) % 4)
                    for i in range(R):
                        if i == 0:
                            dve.wait_ge(a_made, u + 1)
                        if i == R // 2:
                            dve.wait_ge(b_made, u + 1)
                        product(u, i)
                        if i == 1 and ahead > 2:
                            measure(u + 3, t + (j + 3) // 4, (j + 3) % 4)
                        if i == 2 and ahead > 2:
                            finish_variances(dve, u + 3, (j + 3) % 2)

                quads(dve, unit)

            @block.gpsimd
            def _(pool):
                find_scales(pool, 0, 0)
                find_scales(pool, 1, 1)
                find_scales(pool, 2, 0)
                pool.wait_ge(mask_in, 16)

                def mask_rows(u, part, buf, row):
                    i0, n = part * (R // 2), R // 2
                    pool.wait_ge(prod_made, u * R + R + i0 + n)
                    by = mask_sb[:, :, bass.ds(u * R + i0, n)]
                    pool.tensor_tensor(a_res[:, :, :, bass.ds(u * R + i0, n)].rearrange("p h c i -> p i h c"),
                                       prod[:, i0:i0 + n, 0], over(by.rearrange("p h i -> p i h"), C), ALU.mult)
                    for h in range(H):
                        ins = pool.tensor_tensor(
                            b_stage[:, buf, h, :, bass.ds(row + i0, n), :].rearrange("p n i c -> p i n c"),
                            prod[:, i0:i0 + n, 1, h, :].rearrange("p i (n c) -> p i n c", c=CH),
                            over(over(mask_sb[:, h, bass.ds(u * R + i0, n)], C // CH), CH), ALU.mult)
                    ins.then_inc(b_made if part else a_made, 1)

                def unit(u, j, ahead, buf, row):
                    mask_rows(u, 0, buf, row)
                    if ahead > 2:
                        find_scales(pool, u + 3, (j + 3) % 2)
                    mask_rows(u, 1, buf, row)

                per = BLK // R // 4

                for blk in range(NB):
                    if blk >= 2:
                        pool.wait_ge(b_stored[blk % 2], (blk // 2 + 1) * B_STORED)
                    last = blk == NB - 1
                    with pool.Fori(0, per - 1 if last else per) as t:
                        for j in range(4):
                            unit(blk * (BLK // R) + t * 4 + j, j, 3, blk % 2, (t * 4 + j) * R)
                    if last:
                        for j in range(4):
                            unit(G - 4 + j, j, 3 - j, blk % 2, BLK - 4 * R + j * R)

            @block.tensor
            def _(pe):
                def turn_y(n, t, j):
                    if parts:
                        if j % 2 == 0:
                            pe.wait_ge(y_in[j // 2], (t + 1) * 16)
                        if not isinstance(n, int) or n > 0:
                            pe.wait_ge(summed, n)
                        for i in range(R):
                            ins = pe.transpose(ty[:, i * P:(i + 1) * P], yb[j // 2][:, :, (j % 2) * R + i], ident[:])
                        ins.then_inc(y_turned, 1)

                def flip(n, q):
                    pe.wait_ge(xn_made, n + 5)
                    if parts:
                        pe.wait_ge(zt_made, n + 1)
                    for i in range(R):
                        ins = pe.transpose(tp[0 if parts else q][:, i * P:(i + 1) * P],
                                           xn[q][:, i].rearrange("p h c -> p (h c)"), ident[:])
                    ins.then_inc(xt_made, 1)

                def project(u, q, i):
                    tokens = zt[q][:, i * P:(i + 1) * P]
                    if i == 0:
                        pe.wait_ge(zt_made, u + 1 + (1 if parts else 0))
                        pe.wait_ge(gs_made, u + 1)
                    pe.wait_ge(prod_made, u * R + i + 1)
                    pe.matmul(pv[i][:], tokens, weight[:, 0:8 * C], start=True, stop=True).then_inc(v_made, 1)
                    ins = pe.matmul(pg[q][:, i * 2 * C:(i + 1) * 2 * C], tokens, weight[:, 8 * C:],
                                    start=True, stop=True)
                    if i == R - 1:
                        ins.then_inc(g_made, 1)

                if parts:
                    pe.sem_inc(zt_made, 1)
                turn_y(0, 0, 0)
                turn_y(1, 0, 1)
                flip(0, 0)
                turn_y(2, 0, 2)

                def unit(u, t, j, ahead):
                    if ahead > 2:
                        turn_y(u + 3, t + (j + 3) // 4, (j + 3) % 4)
                    for i in range(R):
                        if i == 2 and ahead:
                            flip(u + 1, (j + 1) % 2)
                        project(u, j % 2, i)

                quads(pe, unit)

            @block.scalar
            def _(act):
                act.sem_inc(gs_made, 2)
                act.sem_inc(gs_stored[0], 16)
                act.sem_inc(gs_stored[1], 16)

                def take(n, q):
                    act.wait_ge(xt_made, n + 1)
                    act.activation(zt[q][:], tp[0 if parts else q][:], ACT.Copy).then_inc(zt_made, 1)

                def store_sum(n, j):
                    if parts:
                        act.wait_ge(summed, n + 1)
                        act.dma_start(x[:, :, bass.ds(n * R, R), :], xs[j][:]).then_inc(sum_stored[j], 16)

                store_sum(0, 0)
                store_sum(1, 1)
                take(0, 0)
                store_sum(2, 2)

                def unit(u, t, j, ahead):
                    q = j % 2
                    for i in range(R):
                        if i == 3 and ahead:
                            take(u + 1, 1 - q)
                        act.wait_ge(v_made, u * R + i + 1)
                        act.activation(sig[:, i, :], pv[i][:, 0:4 * C], ACT.Sigmoid).then_inc(sig_made, 1)
                    act.wait_ge(g_made, u + 1)
                    act.wait_ge(gs_stored[q], (t * 2 + j // 2 + 1) * 16)
                    act.activation(gs[q][:].rearrange("p h i c -> p i h c"),
                                   pg[q][:].rearrange("p (i h c) -> p i h c", i=R, h=H),
                                   ACT.Sigmoid).then_inc(gs_made, 1)
                    if ahead > 2:
                        store_sum(u + 3, (j + 3) % 4)
                    act.wait_ge(gs_made, u + 3)
                    act.dma_start(gate_dram[:, :, bass.ds(u * R, R), :], gs[q][:]).then_inc(gs_stored[q], 16)

                quads(act, unit)
                for q in range(2):
                    act.wait_ge(gs_stored[q], 16 * (G // 2 + 1))
                if parts:
                    for j in range(4):
                        act.wait_ge(sum_stored[j], 16 * (G // 4 + 1))


def conv_combine(nc, tag, x, w, a_res, b_dram, gate_dram, out, ident, ones3, numbers):
    TI = P
    TILES = [(h, ih) for h in range(H) for ih in range(N // TI)]
    STEPS = 16
    SR = TI // STEPS
    SC = C // STEPS
    SUBS = SC // CH
    BUFS = 3
    TURN = 2 * BUFS
    PAIRS = SR // 2
    ROUNDS = len(TILES) + 1
    last_step = len(TILES) * STEPS - 1
    rows = [t.rearrange("p h i c -> p (h i) c") for t in (x, gate_dram, out)]
    with Scope(nc, tag) as m:
        weight = m.sb("weight", [P, H * C])
        bias3 = m.sb("bias3", [P, C], BF16)
        prepare_weights(nc, tag + "p", weight, bias3, [(w["w_z"], w["b_z"])], w["ln_out_w"], w["ln_out_b"], ident)
        ptile = [m.sb(f"p{q}", [P, TI, C]) for q in range(2)]
        bch = [m.sb(f"bch{q}", [P, H, P, CH]) for q in range(BUFS)]
        gs = [m.sb(f"g{q}", [P, SR, C]) for q in range(2)]
        pn = m.sb("pn", [P, SR, C])
        pt = m.sb("pt", [P, PAIRS * P])
        take_stats, finish_variances, find_scales, rstd, known = layer_norm(m, SR, PLAIN, numbers)
        psum = [m.ps(f"sum{q}") for q in range(2)]
        tp = [m.ps(f"tp{q}") for q in range(2)]
        po = [m.ps(f"po{q}") for q in range(2)]

        b_in = [m.sem(f"b_in{j}") for j in range(BUFS)]
        chunk_used, p_made = m.sem("chunk_used"), m.sem("p_made")
        x_in = [m.sem(f"x_in{q}") for q in range(2)]
        g_in = [m.sem(f"g_in{q}") for q in range(2)]
        pn_made, pt_made, pt_copied, o_made, gated, added, stored = (
            m.sem(n) for n in ("pn_made", "pt_made", "pt_copied", "o_made", "gated", "added", "stored"))

        def rounds(eng, body):
            for r in range(ROUNDS):
                for q in range(2):
                    body(r, 0, q, q == 0, False, (0, (r * STEPS + q) * SUBS))
                with eng.Fori(0, (STEPS - 4) // TURN) as turn:
                    for k in range(TURN):
                        body(r, turn * BUFS + (1 + k // 2), k % 2, False, False, (turn, (r * STEPS + 2 + k) * SUBS))
                for q in range(2):
                    body(r, STEPS // 2 - 1, q, False, q == 1, (0, ((r + 1) * STEPS - 2 + q) * SUBS))

        def chunk(at, j):
            turn, number = at
            return (number + j) % BUFS, turn * (TURN * SUBS // BUFS) + (number + j) // BUFS

        def now(part, r, t, q):
            if r > 0:
                half = t + (r - 1) * (STEPS // 2)
                part(half * 2 + q, half, q, r - 1)

        def behind(part, r, t, q, first):
            if r > 0 and not (r == 1 and first):
                half = t + (r - 1) * (STEPS // 2) - (1 - q)
                part(half * 2 + 1 - q, half, 1 - q, r - 2 if first else r - 1)

        def before(part, r, t, q, last):
            if r == 1 and isinstance(t, int) and t == 0 and q == 0:
                part(0, 0, 0, 0)
            if r > 0 and not (r == ROUNDS - 1 and last):
                half = t + (r - 1) * (STEPS // 2) + q
                part(half * 2 + 1 - q, half, 1 - q, r if last else r - 1)

        def at_end(part):
            part(last_step, last_step // 2, 1, len(TILES) - 1)

        def slot(n, tile, i=None):
            at = (n - tile * STEPS) * SR
            return bass.ds(at, SR) if i is None else bass.ds(at + i, 1)

        with nc.Block() as block:

            @block.sync
            def _(sp):
                sp.sem_inc(chunk_used, BUFS)

                def body(r, t, q, first, last, at):
                    if r < len(TILES):
                        for j in range(SUBS):
                            s = t * 2 + q
                            buf, _ = chunk(at, j)
                            sp.wait_ge(chunk_used, (s + r * STEPS) * SUBS + j + 1)
                            sp.dma_start(bch[buf][:].rearrange("p k j c -> p (k j c)"),
                                         b_dram[TILES[r][0], bass.ds(s * SUBS + j, 1)]
                                         .rearrange("n p k b j c -> p (n k b j c)")).then_inc(b_in[buf], 16)

                rounds(sp, body)

            @block.tensor
            def _(pe):
                pe.sem_inc(pt_made, 1)

                def add_up(r, s, q, chunks):
                    _, ih = TILES[r]
                    n = s + r * STEPS
                    pe.wait_ge(p_made, n + 1)
                    for j in range(SUBS):
                        buf, before_it = chunk(chunks, j)
                        pe.wait_ge(b_in[buf], (before_it + 1) * 16)
                        for c in range(CH):
                            at = (j * CH + c) * TI
                            for k in range(H):
                                ins = pe.matmul(psum[q][:, at:at + TI], bch[buf][:, k, :, c],
                                                a_res[:, k, bass.ds(s * SC + j * CH + c, 1), ih * TI:(ih + 1) * TI],
                                                start=k == 0, stop=k == H - 1)
                        ins.then_inc(chunk_used, 1)

                def flip(n, half, q, tile):
                    pe.wait_ge(pn_made, n + 1)
                    for j in range(PAIRS):
                        ins = pe.transpose(tp[q][:, j * P:(j + 1) * P],
                                           pn[:, 2 * j:2 * j + 2, :].rearrange("p i c -> p (i c)"), ident[:])
                    ins.then_inc(pt_made, 1)

                def project(n, half, q, tile):
                    pe.wait_ge(pt_copied, n + 1)
                    pe.wait_ge(gated, n + 1)
                    pe.matmul(po[q][:], ones3[:], bias3[:].unsqueeze(1).to_broadcast([P, SR, C]),
                              start=True, stop=True)
                    for j in range(PAIRS):
                        ins = pe.matmul(po[q][:, j * 2 * C:(j + 1) * 2 * C], pt[:, j * P:(j + 1) * P], weight[:],
                                        start=False, stop=True, skip_group_check=True)
                    ins.then_inc(o_made, 1)

                def body(r, t, q, first, last, at):
                    if r < len(TILES):
                        add_up(r, t * 2 + q, q, at)
                    behind(project, r, t, q, first)
                    now(flip, r, t, q)

                rounds(pe, body)
                at_end(project)

            @block.vector
            def _(dve):
                dve.sem_inc(gated, 2)

                def measure(n, half, q, tile):
                    dve.wait_ge(p_made, (tile + 1) * STEPS + 2)
                    take_stats(dve, [ptile[tile % 2][:, slot(n, tile, i), :] for i in range(SR)], 0)
                    finish_variances(dve, n, q)

                def scale(n, half, q, tile):
                    dve.wait_ge(known, n + 1)
                    dve.wait_ge(pt_made, n + 1)
                    dve.tensor_tensor(pn[:], ptile[tile % 2][:, slot(n, tile), :], over(rstd[q][:], C),
                                      ALU.mult).then_inc(pn_made, 1)

                def gate(n, half, q, tile):
                    dve.wait_ge(o_made, n + 1)
                    dve.wait_ge(g_in[q], (half + 1) * 16)
                    flat = gs[q][:].rearrange("p i c -> p (i c)")
                    dve.tensor_tensor(flat, po[q][:], flat, ALU.mult).then_inc(gated, 1)

                def body(r, t, q, first, last, at):
                    before(measure, r, t, q, last)
                    now(scale, r, t, q)
                    behind(gate, r, t, q, first)

                rounds(dve, body)
                at_end(gate)

            @block.gpsimd
            def _(pool):
                def rescaling(n, half, q, tile):
                    find_scales(pool, n, q)

                def add(n, half, q, tile):
                    pool.wait_ge(gated, n + 3)
                    pool.wait_ge(x_in[q], (half + 1) * 16)
                    at = ptile[tile % 2][:, slot(n, tile), :]
                    pool.tensor_tensor(at, at, gs[q][:], ALU.add).then_inc(added, 1)

                def body(r, t, q, first, last, at):
                    before(rescaling, r, t, q, last)
                    behind(add, r, t, q, first)

                rounds(pool, body)
                at_end(add)

            @block.scalar
            def _(act):
                act.sem_inc(p_made, 2)

                def fetch_gate(n, q):
                    act.dma_start(gs[q][:], rows[1][:, bass.ds(n * SR, SR), :]).then_inc(g_in[q], 16)

                fetch_gate(0, 0)
                fetch_gate(1, 1)

                def take_sums(r, s, q):
                    n = s + r * STEPS
                    act.wait_ge(chunk_used, (n + 1) * SUBS + BUFS)
                    act.activation(ptile[r % 2][:, :, bass.ds(s * SC, SC)].rearrange("p i c -> p c i"),
                                   psum[q][:].rearrange("p (c i) -> p c i", c=SC), ACT.Copy).then_inc(p_made, 1)

                def take_flipped(n, half, q, tile):
                    act.wait_ge(pt_made, n + 2)
                    act.activation(pt[:], tp[q][:], ACT.Copy).then_inc(pt_copied, 1)
                    act.dma_start(ptile[tile % 2][:, slot(n, tile), :],
                                  rows[0][:, bass.ds(n * SR, SR), :]).then_inc(x_in[q], 16)

                def store(n, half, q, tile):
                    act.wait_ge(added, n + 1)
                    act.dma_start(rows[2][:, bass.ds(n * SR, SR), :],
                                  ptile[tile % 2][:, slot(n, tile), :]).then_inc(stored, 16)
                    if not isinstance(n, int) or n + 2 <= last_step:
                        fetch_gate(n + 2, q)

                def body(r, t, q, first, last, at):
                    if first:
                        behind(store, r, t, q, first)
                        if 2 <= r < len(TILES):
                            act.wait_ge(stored, 16 * STEPS * (r - 1))
                    if r < len(TILES):
                        take_sums(r, t * 2 + q, q)
                    now(take_flipped, r, t, q)
                    if not first:
                        behind(store, r, t, q, first)

                rounds(act, body)
                at_end(store)
                act.wait_ge(stored, 16 * (last_step + 1))


def scan_input(nc, tag, x, w_t, gamma, beta, wx, scale, shift, ident, numbers):
    with Scope(nc, tag) as m:
        weight = m.sb("weight", [P, P])
        average = m.sb("average", [P, P])
        gamma_col, beta_col = m.sb("gamma", [P, 1]), m.sb("beta", [P, 1])
        xs = [m.sb(f"x{q}", [P, H, R, C]) for q in range(4)]
        xn = [m.sb(f"xn{q}", [P, R, H, C]) for q in range(2)]
        zt = [m.sb(f"zt{q}", [P, R * P]) for q in range(2)]
        take_stats, finish_variances, find_scales, rstd, known = layer_norm(m, H * R, PLAIN, numbers)
        batch = m.sb("batch", [P, G, 6])
        moments = m.sb("moments", [P, 2])
        means, diff, var = m.sb("means", [P, 1]), m.sb("diff", [P, 1]), m.sb("var", [P, 1])
        inv = m.sb("inv", [P, 1])
        tp = [m.ps(f"tp{q}") for q in range(2)]
        po = [m.ps(f"po{q}") for q in range(2)]
        pm = m.ps("pm")
        pm2 = m.ps("pm2")
        x_in = [m.sem(f"x_in{q}") for q in range(4)]
        w_in, zeroed = m.sem("w_in"), m.sem("zeroed")
        xn_made, xt_made, zt_made, o_made, wx_made, counted = (
            m.sem(n) for n in ("xn_made", "xt_made", "zt_made", "o_made", "wx_made", "counted"))
        end = m.sem("end")
        inv_made = m.sem("inv_made")
        averaged = m.sem("averaged")

        with nc.Block() as block:

            @block.sync
            def _(sp):
                sp.wait_ge(zeroed, 1)
                for h in range(H):
                    sp.dma_start(weight[h * C:(h + 1) * C, h * C:(h + 1) * C], w_t).then_inc(w_in, 16)
                    sp.dma_start(gamma_col[h * C:(h + 1) * C, :], gamma.unsqueeze(1)).then_inc(w_in, 16)
                    sp.dma_start(beta_col[h * C:(h + 1) * C, :], beta.unsqueeze(1)).then_inc(w_in, 16)
                sp.wait_ge(w_in, 16 * 3 * H)

            @block.vector
            def _(dve):
                dve.memset(weight[:], 0.0).then_inc(zeroed, 1)

        center_weights(nc, tag + "c", [weight[:]], ident, po)

        with nc.Block() as block:

            @block.sync
            def _(sp):
                sp.sem_inc(xn_made, 4)
                with sp.Fori(0, G // 4) as t:
                    for j in range(4):
                        n = t * 4 + j
                        sp.wait_ge(xn_made, n + 1)
                        sp.dma_start(xs[j][:], x[:, :, bass.ds(n * R, R), :]).then_inc(x_in[j], 16)

            @block.vector
            def _(dve):
                at = 0
                for a in range(H):
                    for b in range(H):
                        cols = average[:, a * C:(a + 1) * C]
                        if b == 0:
                            dve.tensor_scalar(cols, ident[:, 0:C], 0.5, None, ALU.mult).then_inc(end, 1)
                        else:
                            dve.wait_ge(end, at)
                            dve.scalar_tensor_tensor(cols, ident[:, C:2 * C], 0.5, cols, ALU.mult, ALU.add
                                                     ).then_inc(end, 1)
                        at += 1

                def measure(n, t, j):
                    dve.wait_ge(x_in[j], 16 * (t + 1))
                    take_stats(dve, [xs[j][:, h, i, :] for h in range(H) for i in range(R)], 0)

                def rescale(n, j):
                    dve.wait_ge(known, n + 1)
                    dve.tensor_tensor(xn[j % 2][:].rearrange("p i h c -> p h i c"), xs[j][:],
                                      over(rstd[j % 2][:].rearrange("p (h i) -> p h i", h=H), C),
                                      ALU.mult).then_inc(xn_made, 1)

                def count(u):
                    dve.wait_ge(wx_made, u + 3)
                    dve.bn_stats(batch[:, bass.ds(u, 1), :], wx[:, :, bass.ds(u * R, R)]).then_inc(counted, 1)

                for n in range(3):
                    if n == 2:
                        rescale(0, 0)
                    measure(n, 0, n)
                    finish_variances(dve, n, n % 2)

                def unit(u, t, j, ahead):
                    if ahead:
                        rescale(u + 1, (j + 1) % 4)
                    if ahead > 2:
                        measure(u + 3, t + (j + 3) // 4, (j + 3) % 4)
                    count(u)
                    if ahead > 2:
                        finish_variances(dve, u + 3, (j + 3) % 2)

                quads(dve, unit)
                dve.wait_ge(counted, G)
                dve.bn_aggr(moments[:], batch[:].rearrange("p g f -> p (g f)")).then_inc(end, 1)
                dve.wait_ge(averaged, 1)
                dve.tensor_copy(means[:], pm[:, 0:1]).then_inc(end, 1)
                dve.wait_ge(end, at + 2)
                dve.tensor_tensor(diff[:], moments[:, 0:1], means[:], ALU.subtract).then_inc(end, 1)
                dve.wait_ge(end, at + 3)
                dve.tensor_tensor(diff[:], diff[:], diff[:], ALU.mult).then_inc(end, 1)
                dve.wait_ge(end, at + 4)
                dve.tensor_tensor(var[:], diff[:], moments[:, 1:2], ALU.add).then_inc(end, 1)
                dve.wait_ge(averaged, 2)
                dve.tensor_scalar(inv[:], pm2[:, 0:1], 1e-5, None, ALU.add).then_inc(end, 1)
                dve.wait_ge(inv_made, 1)
                dve.wait_ge(w_in, 16 * 3 * H)
                dve.tensor_tensor(scale[:], inv[:], gamma_col[:], ALU.mult).then_inc(end, 1)
                dve.wait_ge(end, at + 7)
                dve.tensor_tensor(diff[:], means[:], scale[:], ALU.mult).then_inc(end, 1)
                dve.wait_ge(end, at + 8)
                dve.tensor_tensor(shift[:], beta_col[:], diff[:], ALU.subtract).then_inc(end, 1)

            @block.gpsimd
            def _(pool):
                find_scales(pool, 0, 0)
                find_scales(pool, 1, 1)
                find_scales(pool, 2, 0)

                def unit(u, t, j, ahead):
                    if ahead > 2:
                        find_scales(pool, u + 3, (j + 3) % 2)

                quads(pool, unit)
                pool.wait_ge(end, 2 * H + 6)
                pool.tensor_tensor(inv[:], inv[:], numbers[:, 0:1], ALU.pow).then_inc(inv_made, 1)

            @block.tensor
            def _(pe):
                def flip(n, q):
                    pe.wait_ge(xn_made, n + 5)
                    for i in range(R):
                        ins = pe.transpose(tp[q][:, i * P:(i + 1) * P], xn[q][:, i].rearrange("p h c -> p (h c)"),
                                           ident[:])
                    ins.then_inc(xt_made, 1)

                flip(0, 0)
                pe.wait_ge(w_in, 16 * 3 * H)

                def unit(u, t, j, ahead):
                    q = j % 2
                    pe.wait_ge(zt_made, u + 1)
                    pe.wait_ge(wx_made, u + 1)
                    pe.matmul(po[q][:], weight[:], zt[q][:], start=True, stop=True).then_inc(o_made, 1)
                    if ahead:
                        flip(u + 1, 1 - q)

                quads(pe, unit)
                pe.wait_ge(end, 2 * H + 1)
                pe.matmul(pm[:, 0:2], average[:], moments[:], start=True, stop=True).then_inc(averaged, 1)
                pe.wait_ge(end, 2 * H + 5)
                pe.matmul(pm2[:, 0:1], average[:], var[:], start=True, stop=True).then_inc(averaged, 1)

            @block.scalar
            def _(act):
                act.sem_inc(wx_made, 2)

                def take(n, q):
                    act.wait_ge(xt_made, n + 1)
                    act.activation(zt[q][:], tp[q][:], ACT.Copy).then_inc(zt_made, 1)

                take(0, 0)

                def unit(u, t, j, ahead):
                    q = j % 2
                    act.wait_ge(o_made, u + 1)
                    act.activation(wx[:, :, bass.ds(u * R, R)].rearrange("p s i -> p i s"),
                                   po[q][:].rearrange("p (i s) -> p i s", i=R), ACT.Copy).then_inc(wx_made, 1)
                    if ahead:
                        take(u + 1, 1 - q)

                quads(act, unit)


def scan(nc, tag, v_t, wx, scale, shift, y_dram):
    STEPS = 64
    SH = P // STEPS
    CHUNKS = N * H * SH
    WARM = 16
    NY = 8
    LANES = SH * 2
    CLOSE = 2.0 ** -18
    with Scope(nc, tag) as m:
        vt = m.sb("vt", [P, P])
        ys = m.sb("ys", [P, 2, SH, YB, NY, YROWS])
        start = m.sb("start", [P, SH, N])
        found = m.sb("found", [P, SH, N])
        ends = m.sb("ends", [P, SH, N])
        pre = m.sb("pre", [P, LANES, P])
        worst = m.sb("worst", [P, 1])
        ones_col = m.sb("ones_col", [P, 1])
        again = m.sb("again", [P, 1], I32)
        pl = [m.ps(f"lane{q}") for q in range(LANES)]
        pc = m.ps("count")
        v_in, zeroed, started, product, summed, y_made, ends_made, check, counted, again_made = (
            m.sem(n) for n in ("v_in", "zeroed", "started", "product", "summed", "y_made", "ends_made", "check",
                               "counted", "again_made"))
        seen = m.sem("seen")
        CHECKS = 5
        stored = [m.sem(f"stored{q}") for q in range(2)]
        SWEEP_STORES = STEPS // NY // 2

        def lane(q):
            return q // 2, q % 2

        def steps(eng, sweep, batch):
            if sweep is None:
                for buf in range(WARM // NY):
                    batch(buf * NY, STEPS - WARM + buf * NY, buf, None, buf)
            else:
                for b2 in range(STEPS // NY // 2):
                    for buf in range(2):
                        k0 = (b2 * 2 + buf) * NY
                        batch(sweep * STEPS + (WARM + k0), k0, buf, sweep * SWEEP_STORES + b2, b2 * 2 + buf)

        def sweeps(eng, run, sets_flag=False):
            run(0)
            eng.wait_ge(again_made, 1)
            flag = eng.value_load(again[0:1, 0:1], min_val=0, max_val=1)
            with eng.If(flag > 0):
                with eng.Fori(1, CHUNKS) as k:
                    eng.wait_ge(again_made, k)
                    eng.sem_inc(seen, 1)
                    more = eng.value_load(again[0:1, 0:1], min_val=0, max_val=1)
                    with eng.If(more > 0):
                        run(k)
                    if sets_flag:
                        with eng.If(more < 1):
                            eng.sem_inc(again_made, 1)

        with nc.Block() as block:

            @block.tensor
            def _(pe):
                pe.wait_ge(v_in, 16 * H)
                pe.wait_ge(zeroed, 4)

                def batch(base, k0, buf, stores, b):
                    for k in range(NY):
                        for q in range(LANES):
                            sh, ih = lane(q)
                            if k == 0 and b == 0:
                                state = start[:, sh, ih * P:(ih + 1) * P]
                            else:
                                from_buf, from_k = (buf, k - 1) if k else (1 - buf, NY - 1)
                                pe.wait_ge(y_made, (base + k - 1) * LANES + q + 1)
                                state = ys[:, from_buf, sh, ih * (YB // 2):(ih + 1) * (YB // 2), from_k, :]
                            pe.matmul(pl[q][:, 0:P], vt[:], state, start=True, stop=True).then_inc(product, 1)

                steps(pe, None, batch)

                def run(sweep):
                    pe.wait_ge(started, sweep + 1)
                    steps(pe, sweep, batch)
                    pe.wait_ge(check, (sweep + 1) * CHECKS)
                    pe.matmul(pc[0:1, 0:1], worst[:], ones_col[:], start=True, stop=True).then_inc(counted, 1)

                sweeps(pe, run)

            @block.vector
            def _(dve):
                dve.memset(vt[:], 0.0).then_inc(zeroed, 1)
                dve.memset(start[:], 0.0).then_inc(zeroed, 1)
                dve.memset(found[:], 0.0).then_inc(zeroed, 1)
                dve.memset(ones_col[:], 1.0).then_inc(zeroed, 1)

                def batch(base, k0, buf, stores, b):
                    for k in range(NY):
                        for q in range(LANES):
                            sh, ih = lane(q)
                            dve.wait_ge(product, (base + k) * LANES + q + 1)
                            dve.scalar_tensor_tensor(pre[:, q, :], wx[:, sh * STEPS + k0 + k, ih * P:(ih + 1) * P],
                                                     scale[:], pl[q][:, 0:P], ALU.mult, ALU.add).then_inc(summed, 1)

                def guesses(to, step):
                    dve.wait_ge(y_made, step * LANES)
                    for sh in range(SH):
                        dve.tensor_copy(ends[:, sh].rearrange("p (b i) -> p b i", i=YROWS),
                                        ys[:, 1, sh, :, NY - 1, :]).then_inc(ends_made, 1)

                    return [lambda: dve.tensor_copy(to[:, 1, :], ends[:, 0, :]),
                            lambda: dve.tensor_copy(to[C:P, 0, :], ends[0:C, 1, :]),
                            lambda: dve.tensor_copy(to[0:C, 0, 1:N], ends[C:P, 1, 0:N - 1])]

                steps(dve, None, batch)
                dve.wait_ge(zeroed, 4)
                copies = guesses(start, WARM)
                dve.wait_ge(ends_made, SH)
                for copy in copies:
                    ins = copy()
                ins.then_inc(started, 1)

                def run(sweep):
                    steps(dve, sweep, batch)
                    copies = guesses(found, sweep * STEPS + (WARM + STEPS))
                    dve.wait_ge(ends_made, sweep * SH + 2 * SH)
                    for copy in copies:
                        ins = copy()
                    at = sweep * CHECKS
                    ins.then_inc(check, 1)
                    dve.wait_ge(check, at + 1)
                    dve.tensor_tensor(ends[:], found[:], start[:], ALU.subtract).then_inc(check, 1)
                    dve.wait_ge(check, at + 2)
                    dve.tensor_tensor(ends[:], ends[:], ends[:], ALU.mult).then_inc(check, 1)
                    dve.wait_ge(check, at + 3)
                    dve.tensor_reduce(worst[:], ends[:], AX.XY, ALU.max).then_inc(check, 1)
                    dve.wait_ge(check, at + 4)
                    dve.tensor_scalar(worst[:], worst[:], CLOSE * CLOSE, None, ALU.is_gt).then_inc(check, 1)
                    dve.tensor_copy(start[:], found[:]).then_inc(started, 1)
                    dve.wait_ge(counted, sweep + 1)
                    dve.tensor_scalar(again[0:1, :], pc[0:1, 0:1], 0.5, None, ALU.is_gt).then_inc(again_made, 1)

                sweeps(dve, run, sets_flag=True)

            @block.scalar
            def _(act):
                act.sem_inc(stored[0], 16 * SH)
                act.sem_inc(stored[1], 16 * SH)

                def batch(base, k0, buf, stores, b):
                    if stores is not None:
                        act.wait_ge(stored[buf], (stores + 1) * (16 * SH))
                    for k in range(NY):
                        for q in range(LANES):
                            sh, ih = lane(q)
                            act.wait_ge(summed, (base + k) * LANES + q + 1)
                            act.activation(ys[:, buf, sh, ih * (YB // 2):(ih + 1) * (YB // 2), k, :],
                                           pre[:, q, :].rearrange("p (b i) -> p b i", i=YROWS), ACT.Sigmoid,
                                           bias=shift[:]).then_inc(y_made, 1)

                steps(act, None, batch)

                def run(sweep):
                    act.wait_ge(started, sweep + 1)
                    steps(act, sweep, batch)

                sweeps(act, run)

            @block.sync
            def _(sp):
                sp.wait_ge(zeroed, 1)
                for h in range(H):
                    sp.dma_start(vt[h * C:(h + 1) * C, h * C:(h + 1) * C], v_t).then_inc(v_in, 16)

                def batch(base, k0, buf, stores, b):
                    if stores is None:
                        return
                    sp.wait_ge(y_made, (base + NY) * LANES)
                    for sh in range(SH):
                        to = y_dram[:, :, sh * STEPS + k0:sh * STEPS + k0 + NY, :]
                        sp.dma_start(to.rearrange("p b s i -> p b (s i)"),
                                     ys[:, buf, sh].rearrange("p b s i -> p b (s i)")).then_inc(stored[buf], 16)

                def run(sweep):
                    steps(sp, sweep, batch)
                    for buf in range(2):
                        sp.wait_ge(stored[buf], (sweep + 1) * (SWEEP_STORES * 16 * SH) + 16 * SH)
                    sp.sem_inc(seen, 1)

                sweeps(sp, run)


def experts(nc, tag, x, router_w, router_b, expert_w, expert_b, out, ident, numbers):
    T = H * R
    FAR = 1e30
    F16 = mybir.dt.float16
    with Scope(nc, tag) as m:
        router = m.sb("router", [P, H * E])
        router_bias = m.sb("router_bias", [P, H * E])
        expert = m.sb("expert", [P, E, P])
        expert_bias = m.sb("expert_bias", [P, E, H, C])
        spread = m.sb("spread", [P, R, E, P], F16)
        twice = m.sb("twice", [P, T * E])
        rank = m.sb("rank", [P, E])
        xs = [m.sb(f"x{q}", [P, H, R, C]) for q in range(4)]
        xn = m.sb("xn", [P, R, H, C])
        xt = [m.sb(f"xt{q}", [P, R * P]) for q in range(4)]
        xe = [m.sb(f"xe{q}", [P, R * P]) for q in range(2)]
        yt = m.sb("yt", [P, R * P])
        shifts = [m.sb(f"shift{q}", [P, T]) for q in range(2)]
        shift = m.sb("shift", [P, T])
        take_stats, finish_variances, find_scales, rstd, known = layer_norm(
            m, T, PLAIN, numbers, shifts)
        logit = m.sb("logit", [P, T, E])
        first = m.sb("first", [P, T, E])
        second = m.sb("second", [P, T, E])
        work = m.sb("work", [P, T, E])
        top = m.sb("top", [P, 2, T])
        pick = m.sb("pick", [P, T])
        gap = m.sb("gap", [P, T])
        share = m.sb("share", [P, 2, T])
        shares = m.sb("shares", [P, 2, T * E])
        wt = [m.sb(f"wt{q}", [P, P]) for q in range(2)]
        wt16 = [m.sb(f"wt16{q}", [P, P], F16) for q in range(2)]
        whole16 = m.sb("whole16", [P, P], F16)
        outs = [m.sb(f"out{q}", [P, H, R, C]) for q in range(4)]
        tp = m.ps("tp")
        tb = m.ps("tb")
        pr = m.ps("routing")
        pl, pw = pr[:, 0:T * E], pr[:, P:2 * P]
        pb = [m.ps(f"spread{q}") for q in range(2)]
        po = [m.ps(f"po{q}") for q in range(2)]

        zeroed, loaded, made = (m.sem(n) for n in ("zeroed", "loaded", "made"))
        n_loads = 4 * H
        with nc.Block() as block:

            @block.sync
            def _(sp):
                sp.wait_ge(zeroed, 6)
                for h in range(H):
                    sp.dma_start(router[h * C:(h + 1) * C, h * E:(h + 1) * E], router_w).then_inc(loaded, 16)
                for h in range(H):
                    sp.dma_start(expert[h * C:(h + 1) * C, :, h * C:(h + 1) * C],
                                 expert_w.rearrange("e k c -> k e c")).then_inc(loaded, 16)
                    sp.dma_start(router_bias[32 * h:32 * h + 1, h * E:(h + 1) * E],
                                 router_b.unsqueeze(0)).then_inc(loaded, 16)
                    sp.dma_start(expert_bias[32 * h:32 * h + 1, :, h, :], expert_b.unsqueeze(0)).then_inc(loaded, 16)

            @block.vector
            def _(dve):
                for t in (whole16, router, router_bias, expert, expert_bias):
                    dve.memset(t[:], 0.0).then_inc(zeroed, 1)
                for e in range(E):
                    ins = dve.memset(rank[:, e:e + 1], float(E - e))
                ins.then_inc(zeroed, 1)
                dve.tensor_tensor(twice[:], ident[:, 0:C], ident[:, C:2 * C], ALU.add).then_inc(made, 1)
                dve.wait_ge(made, 1)
                by_tile = twice[:].rearrange("p (i h e) -> p i e h", h=H, e=E)
                for i in range(R):
                    ins = dve.tensor_copy(spread[:, i].rearrange("p e (h c) -> p e h c", h=H), over(by_tile[:, i], C))
                ins.then_inc(made, 1)
                dve.wait_ge(loaded, 16 * n_loads)

        center_weights(nc, tag + "c", [router[:], expert[:].rearrange("p a c -> p (a c)")], ident, po,
                       [router_bias[:], expert_bias[:].rearrange("p e h c -> p (e h c)")])

        x_in = [m.sem(f"x_in{q}") for q in range(4)]
        xn_made, xt_made, xt_copied, l_made, y_copied, y_turned = (
            m.sem(n) for n in ("xn_made", "xt_made", "xt_copied", "l_made", "y_copied", "y_turned"))
        gap_made, share_made, w_made, w_turned, w_copied, w_split, spread_made, xe_made, o_made, out_made, route = (
            m.sem(n) for n in ("gap_made", "share_made", "w_made", "w_turned", "w_copied", "w_split", "spread_made",
                               "xe_made", "o_made", "out_made", "route"))
        stored = [m.sem(f"stored{q}") for q in range(4)]
        xe_used, xn_scaled, shift_made = m.sem("xe_used"), m.sem("xn_scaled"), m.sem("shift_made")
        ROUTE_STEPS = 14

        with nc.Block() as block:

            @block.sync
            def _(sp):
                sp.sem_inc(out_made, 4)
                with sp.Fori(0, G // 4) as t:
                    for j in range(4):
                        n = t * 4 + j
                        sp.wait_ge(out_made, n + 1)
                        sp.dma_start(xs[j][:], x[:, :, bass.ds(n * R, R), :]).then_inc(x_in[j], 16)

            @block.vector
            def _(dve):
                def measure(n, t, j):
                    dve.wait_ge(x_in[j], 16 * (t + 1))
                    take_stats(dve, [xs[j][:, h, i, :] for h in range(H) for i in range(R)], 0)
                    finish_variances(dve, n, j % 2)

                def choose(n, part):
                    base = n * ROUTE_STEPS

                    def after(step):
                        dve.wait_ge(route, base + step)

                    def candidates(largest):
                        return dve.tensor_tensor(work[:], logit[:], over(largest, E), ALU.is_ge)

                    def rank_them():
                        return dve.tensor_tensor(work[:], work[:], rank[:].unsqueeze(1).to_broadcast([P, T, E]),
                                                 ALU.mult)

                    if part == 0:
                        dve.wait_ge(l_made, n + 1)
                        dve.tensor_copy(logit[:].rearrange("p t e -> p (t e)"), pl).then_inc(route, 1)
                        after(1)
                        dve.tensor_reduce(top[:, 0, :], logit[:], AX.X, ALU.max).then_inc(route, 1)
                    if part == 1:
                        after(2)
                        candidates(top[:, 0, :]).then_inc(route, 1)
                        after(3)
                        rank_them().then_inc(route, 1)
                        after(4)
                        dve.tensor_reduce(pick[:], work[:], AX.X, ALU.max).then_inc(route, 1)
                    if part == 2:
                        after(5)
                        dve.tensor_tensor(first[:], work[:], over(pick[:], E), ALU.is_ge).then_inc(route, 1)
                        after(6)
                        dve.scalar_tensor_tensor(logit[:], first[:], -FAR, logit[:], ALU.mult, ALU.add
                                                 ).then_inc(route, 1)
                        after(7)
                        dve.tensor_reduce(top[:, 1, :], logit[:], AX.X, ALU.max).then_inc(route, 1)
                    if part == 3:
                        after(8)
                        dve.tensor_tensor(gap[:], top[:, 1, :], top[:, 0, :], ALU.subtract).then_inc(gap_made, 1)
                        candidates(top[:, 1, :]).then_inc(route, 1)
                        after(9)
                        rank_them().then_inc(route, 1)
                    if part == 4:
                        after(10)
                        dve.tensor_reduce(pick[:], work[:], AX.X, ALU.max).then_inc(route, 1)
                        after(11)
                        dve.tensor_tensor(second[:], work[:], over(pick[:], E), ALU.is_ge).then_inc(route, 1)
                    if part == 5:
                        after(12)
                        dve.wait_ge(share_made, n + 1)
                        dve.tensor_tensor(first[:], first[:], over(share[:, 0, :], E), ALU.mult).then_inc(route, 1)
                        dve.tensor_tensor(second[:], second[:], over(share[:, 1, :], E), ALU.mult).then_inc(route, 1)
                        after(14)
                        dve.tensor_tensor(shares[:], twofold(first), twofold(second), ALU.add).then_inc(w_made, 1)

                def twofold(t):
                    return t[:].rearrange("p t e -> p (t e)").unsqueeze(1).to_broadcast([P, 2, T * E])

                def scale_inputs(u, j, e):
                    dve.wait_ge(spread_made, u * E + e + 1)
                    dve.wait_ge(xe_used, u * E + e + 1)
                    dve.tensor_tensor(xe[e % 2][:], pb[e % 2][:], xt[j][:], ALU.mult).then_inc(xe_made, 1)

                def finish(n, t, j):
                    dve.wait_ge(y_turned, n + 2)
                    dve.wait_ge(stored[j], (t + 1) * 16)
                    dve.tensor_tensor(outs[j][:].rearrange("p h i c -> p i h c"),
                                      tb[:].rearrange("p (i h c) -> p i h c", i=R, h=H),
                                      xs[j][:].rearrange("p h i c -> p i h c"), ALU.add).then_inc(out_made, 1)

                dve.sem_inc(xe_made, 2)
                measure(0, 0, 0)
                measure(1, 0, 1)
                for part in range(6):
                    choose(0, part)
                measure(2, 0, 2)

                def unit(u, t, j, ahead, behind):
                    for e in range(E):
                        scale_inputs(u, j, e)
                        if e == 2 and behind:
                            finish(u - 1, t - 1 if j == 0 else t, (j + 3) % 4)
                        if e < 5 and ahead:
                            choose(u + 1, e)
                        if e == 4 and ahead:
                            choose(u + 1, 5)
                        if ahead > 2:
                            j3 = (j + 3) % 4
                            if e == 5:
                                dve.wait_ge(x_in[j3], 16 * (t + (j + 3) // 4 + 1))
                            if e in (5, 6):
                                take_stats(dve, [xs[j3][:, e - 5, i, :] for i in range(R)], (e - 5) * R)
                            if e == 7:
                                finish_variances(dve, u + 3, j3 % 2)

                quads_peeled(dve, unit)
                finish(G - 1, G // 4 - 1, 3)

            @block.gpsimd
            def _(pool):
                def rescale(n, j):
                    q = j % 2
                    to = xn[:].rearrange("p i h c -> p h i c")
                    find_scales(pool, n, q)
                    pool.wait_ge(known, n + 1)
                    if not isinstance(n, int) or n > 0:
                        pool.wait_ge(xn_made, n)
                    pool.tensor_tensor(shift[:], shifts[q][:], numbers[:, 1:2].to_broadcast([P, T]), ALU.subtract
                                       ).then_inc(shift_made, 1)
                    pool.wait_ge(xt_made, n + 1)
                    pool.tensor_tensor(to, xs[j][:], over(rstd[q][:].rearrange("p (h i) -> p h i", h=H), C),
                                       ALU.mult).then_inc(xn_scaled, 1)
                    pool.wait_ge(shift_made, n + 1)
                    pool.wait_ge(xn_scaled, n + 1)
                    pool.tensor_tensor(to, to, over(shift[:].rearrange("p (h i) -> p h i", h=H), C),
                                       ALU.subtract).then_inc(xn_made, 1)

                def split_shares(n, q):
                    pool.wait_ge(w_copied, n + 1)
                    pool.tensor_tensor(wt16[q][:], wt[q][:], whole16[:], ALU.subtract).then_inc(w_split, 1)

                rescale(0, 0)
                rescale(1, 1)
                split_shares(0, 0)

                def unit(u, t, j, ahead):
                    if ahead > 1:
                        rescale(u + 2, (j + 2) % 4)
                    if ahead:
                        split_shares(u + 1, (j + 1) % 2)

                quads(pool, unit)

            @block.scalar
            def _(act):
                for j in range(4):
                    act.sem_inc(stored[j], 16)

                def take(n, j):
                    act.wait_ge(xt_made, n + 2)
                    act.activation(xt[j][:], tp[:], ACT.Copy).then_inc(xt_copied, 1)

                def take_outputs(n, j):
                    act.wait_ge(o_made, n + 1)
                    act.wait_ge(y_turned, n + 1)
                    act.activation(yt[:], po[j % 2][:], ACT.Copy).then_inc(y_copied, 1)

                def weigh(n):
                    act.wait_ge(gap_made, n + 1)
                    act.activation(share[:, 0, :], gap[:], ACT.Sigmoid, scale=-1.0)
                    act.activation(share[:, 1, :], gap[:], ACT.Sigmoid).then_inc(share_made, 1)

                def take_shares(n, q):
                    act.wait_ge(w_turned, n + 1)
                    act.wait_ge(w_split, n + 1)
                    act.activation(wt[q][:], pw, ACT.Copy)
                    act.activation(whole16[C:P, :], pw[C:P, :], ACT.Copy).then_inc(w_copied, 1)

                def store(n, j):
                    act.wait_ge(out_made, n + 5)
                    act.dma_start(out[:, :, bass.ds(n * R, R), :], outs[j][:]).then_inc(stored[j], 16)

                act.sem_inc(y_copied, 2)
                take(0, 0)
                take(1, 1)
                weigh(0)
                take_shares(0, 0)

                def unit(u, t, j, ahead, behind):
                    if behind:
                        take_outputs(u - 1, (j + 3) % 4)
                    if ahead > 1:
                        take(u + 2, (j + 2) % 4)
                    if ahead:
                        weigh(u + 1)
                    if behind:
                        store(u - 1, (j + 3) % 4)
                    if ahead:
                        take_shares(u + 1, (j + 1) % 2)

                quads_peeled(act, unit)
                take_outputs(G - 1, 3)
                store(G - 1, 3)
                for j in range(4):
                    act.wait_ge(stored[j], 16 * (G // 4 + 1))

            @block.tensor
            def _(pe):
                pe.sem_inc(xt_made, 1)
                pe.sem_inc(xe_used, 2)

                def flip(n):
                    pe.wait_ge(xn_made, n + 1)
                    pe.wait_ge(xt_copied, n + 1)
                    for i in range(R):
                        ins = pe.transpose(tp[:, i * P:(i + 1) * P], xn[:, i].rearrange("p h c -> p (h c)"), ident[:])
                    ins.then_inc(xt_made, 1)

                def rate(n, j):
                    pe.wait_ge(xt_copied, n + 2)
                    for i in range(R):
                        ins = pe.matmul(pl[:, i * H * E:(i + 1) * H * E], xt[j][:, i * P:(i + 1) * P], router[:],
                                        start=True, stop=True)
                    ins.then_inc(l_made, 1)

                def turn_shares(n):
                    pe.wait_ge(w_made, n + 1)
                    pe.transpose(pw, shares[:].rearrange("p b t -> p (b t)"), ident[:]).then_inc(w_turned, 1)

                def spread_out(u, q, e):
                    if e == 0:
                        pe.wait_ge(w_split, u + 2)
                    pe.wait_ge(xe_made, u * E + e + 1)
                    for i in range(R):
                        ins = pe.matmul(pb[e % 2][:, i * P:(i + 1) * P], spread[:, i, e, :], wt16[q][:],
                                        start=True, stop=True)
                    ins.then_inc(spread_made, 1)

                def add_expert(u, q, e):
                    pe.wait_ge(xe_made, u * E + e + 3)
                    if e == 0:
                        pe.wait_ge(y_copied, u + 1)
                    pe.matmul(po[q][:], expert[:, e, :], xe[e % 2][:], start=e == 0, stop=e == E - 1).then_inc(xe_used, 1)
                    if e == E - 1:
                        pe.wait_ge(xe_used, (u + 1) * E + 2)
                        pe.sem_inc(o_made, 1)

                def turn_outputs(n):
                    pe.wait_ge(y_copied, n + 3)
                    pe.wait_ge(out_made, n + 4)
                    for i in range(R):
                        ins = pe.transpose(tb[:, i * P:(i + 1) * P], yt[:, i * P:(i + 1) * P], ident[:])
                    ins.then_inc(y_turned, 1)

                pe.sem_inc(xt_copied, 1)
                pe.sem_inc(w_split, 1)
                pe.sem_inc(y_turned, 1)
                flip(0)
                rate(0, 0)
                flip(1)
                turn_shares(0)
                spread_out(0, 0, 0)
                rate(1, 1)

                def unit(u, t, j, ahead, behind):
                    q = j % 2
                    for e in range(E):
                        if e + 1 < E:
                            spread_out(u, q, e + 1)
                        elif ahead:
                            spread_out(u + 1, 1 - q, 0)
                        if e == 1 and behind:
                            turn_outputs(u - 1)
                        if e == 3 and ahead > 1:
                            flip(u + 2)
                        if e == 5 and ahead > 1:
                            rate(u + 2, (j + 2) % 4)
                        if e == 5 and ahead:
                            turn_shares(u + 1)
                        add_expert(u, q, e)

                quads_peeled(pe, unit)
                turn_outputs(G - 1)


CONV = ["ln_in_w", "ln_in_b", "w_ap", "b_ap", "w_ag", "b_ag", "w_bp", "b_bp", "w_bg", "b_bg", "ln_out_w",
        "ln_out_b", "w_z", "b_z", "w_g", "b_g"]


def build(nc, a, out):
    def scratch(name, shape):
        return nc.dram_tensor(name, shape, F32, kind="Internal").ap()

    b_dram = scratch("b_scratch", [H, C // CH, P, H, RB, BLK, CH])
    gate_dram = scratch("gate_scratch", [P, H, N, C])
    t0 = scratch("after_conv0", [P, H, N, C])
    y_dram = scratch("scan_scratch", [P, YB, P, YROWS])
    t1 = scratch("after_scan", [P, H, N, C])
    t2 = scratch("after_conv1", [P, H, N, C])

    with ExitStack() as s:
        ident = s.enter_context(nc.sbuf_tensor("ident", [P, P], F32))
        ones3 = s.enter_context(nc.sbuf_tensor("ones3", [P, P], BF16))
        numbers = s.enter_context(nc.sbuf_tensor("numbers", [P, 2], F32))
        constants(nc, ident, ones3, numbers)
        for layer, (x, y, parts) in enumerate([(a["x"], t0, None), (t1, t2, (t0, y_dram))]):
            w = {k: a[f"L{layer}_conv_{k}"] for k in CONV}
            with nc.sbuf_tensor(f"a_res{layer}", [P, H, C, N], F32) as a_res:
                conv_project(nc, f"cp{layer}", x, a[f"L{layer}_conv_mask"], w, a_res, b_dram, gate_dram, ident,
                             numbers, parts)
                conv_combine(nc, f"cc{layer}", x, w, a_res, b_dram, gate_dram, y, ident, ones3, numbers)
            if layer == 0:
                with nc.sbuf_tensor("wx", [P, P, N], F32) as wx, nc.sbuf_tensor("bn_scale", [P, 1], F32) as scale, \
                        nc.sbuf_tensor("bn_shift", [P, 1], F32) as shift:
                    scan_input(nc, "si", t0, a["L0_ffn_W_t"], a["L0_ffn_gamma"], a["L0_ffn_beta"], wx, scale, shift,
                               ident, numbers)
                    scan(nc, "sc", a["L0_ffn_V_t"], wx, scale, shift, y_dram)
        experts(nc, "ex", t2, a["L1_ffn_router_w"], a["L1_ffn_router_b"], a["L1_ffn_expert_w"],
                a["L1_ffn_expert_b"], out, ident, numbers)


def kernel(**inputs):
    import concourse.bacc as bacc
    from concourse.bass_utils import run_bass_kernel_spmd

    arrays = {}
    for name, value in inputs.items():
        v = np.asarray(value)
        if name == "x":
            v = v.reshape(N, H, P, C).transpose(2, 1, 0, 3)
        elif name.endswith("_mask"):
            v = v.reshape(N, H, P).transpose(2, 1, 0)
        elif name in ("L0_ffn_W", "L0_ffn_V"):
            name, v = name + "_t", v.T
        arrays[name] = np.ascontiguousarray(v)
    nc = bacc.Bacc("TRN2", target_bir_lowering=False, num_devices=1)
    aps = {k: nc.dram_tensor("in_" + k, v.shape, mybir.dt.from_np(v.dtype), kind="ExternalInput").ap()
           for k, v in arrays.items()}
    out = nc.dram_tensor("out_0", (P, H, N, C), F32, kind="ExternalOutput").ap()
    build(nc, aps, out)
    r = run_bass_kernel_spmd(nc, [{"in_" + k: v for k, v in arrays.items()}], core_ids=[0])
    return r.results[0]["out_0"].transpose(2, 1, 0, 3).reshape(1, N, N, C)
```
